# Optimizing a Trainium2 kernel written in Bass

```python
import numpy as np
import jax
import jax.numpy as jnp

def _softmax(x, axis=-1):
    return jax.nn.softmax(x, axis=axis)

def _gelu(x):
    return jax.nn.gelu(x, approximate=True)

def _silu(x):
    return jax.nn.silu(x)

def _sigmoid(x):
    return jax.nn.sigmoid(x)

def _layernorm(x, axis=-1, eps=1e-05):
    m = jnp.mean(x, axis=axis, keepdims=True)
    v = jnp.var(x, axis=axis, keepdims=True)
    return (x - m) / jnp.sqrt(v + eps)

def _scatter_add(tgt, idx, src, axis=0):
    return tgt.at[idx].add(src)

def _segment_sum(src, seg, n):
    return jax.ops.segment_sum(src, seg, n)
kernel_name = 'mk_flamingo_gated_d4_seqx_r8_535ef9'

def setup_inputs(seed: int=0):
    np.random.seed(seed)
    _w = jnp.asarray

    def _rec_inputs():
        import jax
        import jax.numpy as jnp
        _rk = jax.random.key(seed)
        x = -0.0002928 + 1 * jax.random.normal(jax.random.fold_in(_rk, 1), (32, 64, 128), jnp.float32)
        _lenS = 64 - jax.random.randint(jax.random.fold_in(_rk, 7), (32,), 0, max(1, 64 // 4) + 1, jnp.int32)
        _lenS2 = 64 - jax.random.randint(jax.random.fold_in(_rk, 8), (32,), 0, max(1, 64 // 4) + 1, jnp.int32)
        _ctx_1024P = jax.random.normal(jax.random.fold_in(_rk, 11), (32, 16, 128), jnp.float32)
        _ctx_1024c = jax.random.dirichlet(jax.random.fold_in(_rk, 511), 0.3 * jnp.ones((16,), jnp.float32), (32, 64))
        _ctx_1024t = jnp.einsum('bsk,bkd->bsd', _ctx_1024c, _ctx_1024P)
        _ctx_1024t = _ctx_1024t * jax.lax.rsqrt(jnp.mean(jnp.square(_ctx_1024t)) + 1e-12) * 0.953939
        ctx_1024 = -1.39393e-06 + 0.999914 * (_ctx_1024t + 0.3 * jax.random.normal(jax.random.fold_in(_rk, 611), (32, 64, 128), jnp.float32))
        _validS = jnp.arange(64)[None, :] < _lenS[:, None]
        _validS2 = jnp.arange(64)[None, :] < _lenS2[:, None]
        _causal = jnp.tril(jnp.ones((64, 64), dtype=bool))
        mask_Bx1xSxS2_ik1 = jnp.where(jnp.broadcast_to(_validS2[:, None, None, :], (32, 1, 64, 64)), 1, 0).astype(jnp.int32)
        mask_BxS2_ik0 = jnp.where(jnp.broadcast_to(_validS2[:, :], (32, 64)), 0, 1).astype(jnp.int32)
        mask_BxSxS2_ff0 = jnp.where(jnp.ones((32, 64, 64), dtype=bool), 0.0, -1000000000.0).astype(jnp.float32)
        _g = jax.random.normal(jax.random.fold_in(_rk, 9001), (2, 4), jnp.float32)
        _g = jnp.sign(_g) * jnp.maximum(jnp.abs(_g), 1.0) + (_g == 0) * 1.0
        g_xattn = _g[0]
        g_ffn = _g[1]
        return (x, ctx_1024, mask_Bx1xSxS2_ik1, mask_BxS2_ik0, mask_BxSxS2_ff0, g_xattn, g_ffn)
    x, ctx_1024, mask_Bx1xSxS2_ik1, mask_BxS2_ik0, mask_BxSxS2_ff0, g_xattn, g_ffn = _rec_inputs()

    def _L0_xattn_setup():
        import jax, jax.numpy as jnp
        import numpy as np
        D_MODEL = 128
        N_HEADS = 16
        D_K = D_MODEL // N_HEADS
        NEG_INF = -1000000000.0

        def _split_heads(x):
            B, S, _ = x.shape
            return x.reshape(B, S, N_HEADS, D_K).transpose(0, 2, 1, 3)
        key = jax.random.key(seed)
        ks = jax.random.split(key, 12)
        B, S = (2, 256)
        inp = {'q': jax.random.normal(ks[0], (B, S, D_MODEL), dtype=jnp.float32), 'k': jax.random.normal(ks[1], (B, S, D_MODEL), dtype=jnp.float32), 'v': jax.random.normal(ks[2], (B, S, D_MODEL), dtype=jnp.float32), 'mask': jax.random.randint(ks[3], (B, 1, S, S), 0, 2, dtype=jnp.int32), 'Wq': jax.random.normal(ks[4], (D_MODEL, D_MODEL), dtype=jnp.float32) / np.sqrt(D_MODEL), 'bq': jnp.zeros((D_MODEL,), dtype=jnp.float32), 'Wk': jax.random.normal(ks[5], (D_MODEL, D_MODEL), dtype=jnp.float32) / np.sqrt(D_MODEL), 'bk': jnp.zeros((D_MODEL,), dtype=jnp.float32), 'Wv': jax.random.normal(ks[6], (D_MODEL, D_MODEL), dtype=jnp.float32) / np.sqrt(D_MODEL), 'bv': jnp.zeros((D_MODEL,), dtype=jnp.float32), 'Wo': jax.random.normal(ks[7], (D_MODEL, D_MODEL), dtype=jnp.float32) / np.sqrt(D_MODEL), 'bo': jnp.zeros((D_MODEL,), dtype=jnp.float32)}
        return inp
    _L0_xattn_all = _L0_xattn_setup()
    _L0_xattn_in = {k: v for k, v in _L0_xattn_all.items() if k in ('Wq', 'bq', 'Wk', 'bk', 'Wv', 'bv', 'Wo', 'bo')}
    del _L0_xattn_all

    def _L0_ffn_setup():
        import jax, jax.numpy as jnp
        import numpy as np
        D_MODEL = 128
        key = jax.random.key(seed)
        k_x, k_w, k_a1, k_a2 = jax.random.split(key, 4)
        x = jax.random.normal(k_x, (4, 256, D_MODEL), dtype=jnp.float32)
        weight = jax.random.normal(k_w, (D_MODEL, D_MODEL), dtype=jnp.float32) * 0.02
        aux_weight1 = jax.random.normal(k_a1, (D_MODEL, D_MODEL), dtype=jnp.float32) * 0.02
        aux_weight2 = jax.random.normal(k_a2, (D_MODEL, D_MODEL), dtype=jnp.float32) * 0.02
        bias = jnp.zeros((D_MODEL,), dtype=jnp.float32)
        return {'x': x, 'weight': weight, 'aux_weight1': aux_weight1, 'aux_weight2': aux_weight2, 'bias': bias}
    _L0_ffn_all = _L0_ffn_setup()
    _L0_ffn_in = {k: v for k, v in _L0_ffn_all.items() if k in ('weight', 'aux_weight1', 'aux_weight2', 'bias')}
    del _L0_ffn_all

    def _L1_xattn_setup():
        import jax, jax.numpy as jnp
        import numpy as np
        B, LQ, LK = (8, 256, 256)
        QD = KD = VD = HD = 128
        key = jax.random.key(seed)
        ks = jax.random.split(key, 12)
        s = lambda d: 1.0 / np.sqrt(d)
        return {'q': jax.random.normal(ks[0], (B, LQ, QD), jnp.float32), 'k': jax.random.normal(ks[1], (B, LK, KD), jnp.float32), 'mask': jax.random.randint(ks[2], (B, LK), 0, 2, jnp.int32), 'Wq': jax.random.normal(ks[3], (QD, HD), jnp.float32) * s(QD), 'bq': jax.random.normal(ks[4], (HD,), jnp.float32) * 0.02, 'Wk': jax.random.normal(ks[5], (KD, HD), jnp.float32) * s(KD), 'bk': jax.random.normal(ks[6], (HD,), jnp.float32) * 0.02, 'Wv': jax.random.normal(ks[7], (VD, HD), jnp.float32) * s(VD), 'bv': jax.random.normal(ks[8], (HD,), jnp.float32) * 0.02, 'Wo': jax.random.normal(ks[9], (HD, VD), jnp.float32) * s(HD), 'bo': jax.random.normal(ks[10], (VD,), jnp.float32) * 0.02}
    _L1_xattn_all = _L1_xattn_setup()
    _L1_xattn_in = {k: v for k, v in _L1_xattn_all.items() if k in ('Wq', 'bq', 'Wk', 'bk', 'Wv', 'bv', 'Wo', 'bo')}
    del _L1_xattn_all

    def _L1_ffn_setup():
        import jax, jax.numpy as jnp
        import numpy as np
        from jax import lax
        N_HEADS = 16
        TOP_K = 2
        N_EXPERTS = 8

        def layer_norm(x, w, b, eps=1e-05):
            mu = jnp.mean(x, axis=-1, keepdims=True)
            var = jnp.mean(jnp.square(x - mu), axis=-1, keepdims=True)
            return (x - mu) * lax.rsqrt(var + eps) * w + b

        def attention(x, w_qkv, b_qkv, w_o, b_o):
            B, T, D = x.shape
            dh = D // N_HEADS
            qkv = x @ w_qkv + b_qkv
            q, k, v = jnp.split(qkv, 3, axis=-1)
            q = q.reshape(B, T, N_HEADS, dh)
            k = k.reshape(B, T, N_HEADS, dh)
            v = v.reshape(B, T, N_HEADS, dh)
            scores = jnp.einsum('bqhd,bkhd->bhqk', q, k) / jnp.sqrt(jnp.float32(dh)).astype(x.dtype)
            probs = jax.nn.softmax(scores, axis=-1)
            ctx = jnp.einsum('bhqk,bkhd->bqhd', probs, v).reshape(B, T, D)
            return ctx @ w_o + b_o

        def moe_ff(x, w_gate, w1, b1, w2, b2):
            B, T, D = x.shape
            t = x.reshape(B * T, D)
            probs = jax.nn.softmax(t @ w_gate, axis=-1)
            tw, ti = lax.top_k(probs, TOP_K)
            tw = tw / jnp.sum(tw, axis=-1, keepdims=True)
            out = jnp.zeros_like(t)
            for e in range(N_EXPERTS):
                we = jnp.sum(jnp.where(ti == e, tw, 0.0), axis=-1)
                h = jax.nn.gelu(t @ w1[e] + b1[e]) @ w2[e] + b2[e]
                out = out + we[:, None] * h
            return out.reshape(B, T, D)
        key = jax.random.key(seed)
        ks = jax.random.split(key, 8)
        B, T, D, H, E = (4, 64, 128, 512, 8)
        s = lambda d: 1.0 / np.sqrt(d)
        return {'x': jax.random.normal(ks[0], (B, T, D), jnp.float32), 'ln1_w': jnp.ones((D,), jnp.float32), 'ln1_b': jnp.zeros((D,), jnp.float32), 'ln2_w': jnp.ones((D,), jnp.float32), 'ln2_b': jnp.zeros((D,), jnp.float32), 'w_qkv': jax.random.normal(ks[1], (D, 3 * D), jnp.float32) * s(D), 'b_qkv': jnp.zeros((3 * D,), jnp.float32), 'w_o': jax.random.normal(ks[2], (D, D), jnp.float32) * s(D), 'b_o': jnp.zeros((D,), jnp.float32), 'w_gate': jax.random.normal(ks[3], (D, E), jnp.float32) * s(D), 'w1': jax.random.normal(ks[4], (E, D, H), jnp.float32) * s(D), 'b1': jnp.zeros((E, H), jnp.float32), 'w2': jax.random.normal(ks[5], (E, H, D), jnp.float32) * s(H), 'b2': jnp.zeros((E, D), jnp.float32)}
    _L1_ffn_all = _L1_ffn_setup()
    _L1_ffn_in = {k: v for k, v in _L1_ffn_all.items() if k in ('ln1_w', 'ln1_b', 'ln2_w', 'ln2_b', 'w_qkv', 'b_qkv', 'w_o', 'b_o', 'w_gate', 'w1', 'b1', 'w2', 'b2')}
    del _L1_ffn_all

    def _L2_xattn_setup():
        import jax, jax.numpy as jnp
        import numpy as np
        DIM = 128
        CTX_DIM = 128
        HEADS = 16
        DIM_HEAD = 64
        INNER = HEADS * DIM_HEAD
        FF_INNER = 4 * DIM
        EPS = 1e-05

        def layer_norm(x, g, b):
            mu = jnp.mean(x, axis=-1, keepdims=True)
            var = jnp.var(x, axis=-1, keepdims=True)
            return (x - mu) * jax.lax.rsqrt(var + EPS) * g + b
        key = jax.random.key(seed)
        ks = jax.random.split(key, 10)
        b, n, j = (2, 256, 256)
        x = jax.random.normal(ks[0], (b, n, DIM), dtype=jnp.float32)
        context = jax.random.normal(ks[1], (b, j, CTX_DIM), dtype=jnp.float32)
        mask = jnp.zeros((b, n, j), dtype=jnp.float32)
        s = 0.02
        Wq = jax.random.normal(ks[2], (DIM, INNER), dtype=jnp.float32) * s
        Wkv = jax.random.normal(ks[3], (CTX_DIM, 2 * DIM_HEAD), dtype=jnp.float32) * s
        Wout = jax.random.normal(ks[4], (INNER, DIM), dtype=jnp.float32) * s
        W1 = jax.random.normal(ks[5], (DIM, 2 * FF_INNER), dtype=jnp.float32) * s
        W2 = jax.random.normal(ks[6], (FF_INNER, DIM), dtype=jnp.float32) * s
        ln_g = jnp.ones((DIM,), jnp.float32)
        ln_b = jnp.zeros((DIM,), jnp.float32)
        cln_g = jnp.ones((CTX_DIM,), jnp.float32)
        cln_b = jnp.zeros((CTX_DIM,), jnp.float32)
        return {'x': x, 'context': context, 'mask': mask, 'ln_g': ln_g, 'ln_b': ln_b, 'cln_g': cln_g, 'cln_b': cln_b, 'Wq': Wq, 'Wkv': Wkv, 'Wout': Wout, 'W1': W1, 'W2': W2}
    _L2_xattn_all = _L2_xattn_setup()
    _L2_xattn_in = {k: v for k, v in _L2_xattn_all.items() if k in ('ln_g', 'ln_b', 'cln_g', 'cln_b', 'Wq', 'Wkv', 'Wout', 'W1', 'W2')}
    del _L2_xattn_all

    def _L2_ffn_setup():
        import jax, jax.numpy as jnp
        import numpy as np
        EMBED = 128
        HEADS = 16
        HEAD_DIM = EMBED // HEADS
        NUM_EXPERTS = 8
        TOP_K = 2
        HIDDEN = (int(2 * (4 * EMBED) / 3) + 63) // 64 * 64
        SEQ = 256
        BATCH = 2
        ROPE_BASE = 10000.0
        EPS = 1e-06

        def _rope_tables(seq_len, dim):
            inv_freq = 1.0 / ROPE_BASE ** (np.arange(0, dim, 2, dtype=np.float32) / dim)
            t = np.arange(seq_len, dtype=np.float32)
            freqs = np.einsum('i,j->ij', t, inv_freq)
            emb = np.concatenate([freqs, freqs], axis=-1)
            return (jnp.asarray(np.cos(emb)), jnp.asarray(np.sin(emb)))

        def _rotate_half(x):
            x1, x2 = jnp.split(x, 2, axis=-1)
            return jnp.concatenate([-x2, x1], axis=-1)

        def _rmsnorm(x, w):
            return x * jax.lax.rsqrt(jnp.mean(x * x, axis=-1, keepdims=True) + EPS) * w

        def _attention(x, wq, wk, wv, wo):
            B, S, _ = x.shape
            q = (x @ wq).reshape(B, S, HEADS, HEAD_DIM).transpose(0, 2, 1, 3)
            k = (x @ wk).reshape(B, S, HEADS, HEAD_DIM).transpose(0, 2, 1, 3)
            v = (x @ wv).reshape(B, S, HEADS, HEAD_DIM).transpose(0, 2, 1, 3)
            cos, sin = _rope_tables(S, HEAD_DIM)
            cos = cos[None, None]
            sin = sin[None, None]
            q = q * cos + _rotate_half(q) * sin
            k = k * cos + _rotate_half(k) * sin
            scale = HEAD_DIM ** (-0.5)
            scores = jnp.einsum('bhqd,bhkd->bhqk', q, k) * scale
            causal = jnp.triu(jnp.ones((S, S), bool), k=1)
            scores = jnp.where(causal, -jnp.inf, scores)
            attn = jax.nn.softmax(scores, axis=-1)
            out = jnp.einsum('bhqk,bhkd->bhqd', attn, v)
            out = out.transpose(0, 2, 1, 3).reshape(B, S, EMBED)
            return out @ wo

        def _moe(x, w_router, wg, wu, wd):
            B, S, E = x.shape
            xf = x.reshape(-1, E)
            logits = xf @ w_router
            probs = jax.nn.softmax(logits, axis=-1)
            topw, topi = jax.lax.top_k(probs, TOP_K)
            topw = topw / jnp.sum(topw, axis=-1, keepdims=True)
            combine = jnp.sum(jax.nn.one_hot(topi, NUM_EXPERTS, dtype=xf.dtype) * topw[..., None], axis=1)
            g = jax.nn.silu(jnp.einsum('td,xdh->txh', xf, wg))
            u = jnp.einsum('td,xdh->txh', xf, wu)
            eo = jnp.einsum('txh,xhd->txd', g * u, wd)
            out = jnp.einsum('txd,tx->td', eo, combine)
            return out.reshape(B, S, E)
        key = jax.random.key(seed)
        ks = jax.random.split(key, 12)
        s = 0.02
        return {'x': jax.random.normal(ks[0], (BATCH, SEQ, EMBED), jnp.float32), 'wq': jax.random.normal(ks[1], (EMBED, EMBED), jnp.float32) * s, 'wk': jax.random.normal(ks[2], (EMBED, EMBED), jnp.float32) * s, 'wv': jax.random.normal(ks[3], (EMBED, EMBED), jnp.float32) * s, 'wo': jax.random.normal(ks[4], (EMBED, EMBED), jnp.float32) * s, 'w_router': jax.random.normal(ks[5], (EMBED, NUM_EXPERTS), jnp.float32) * s, 'wg': jax.random.normal(ks[6], (NUM_EXPERTS, EMBED, HIDDEN), jnp.float32) * s, 'wu': jax.random.normal(ks[7], (NUM_EXPERTS, EMBED, HIDDEN), jnp.float32) * s, 'wd': jax.random.normal(ks[8], (NUM_EXPERTS, HIDDEN, EMBED), jnp.float32) * s, 'g1': jnp.ones((EMBED,), jnp.float32), 'g2': jnp.ones((EMBED,), jnp.float32)}
    _L2_ffn_all = _L2_ffn_setup()
    _L2_ffn_in = {k: v for k, v in _L2_ffn_all.items() if k in ('wq', 'wk', 'wv', 'wo', 'w_router', 'wg', 'wu', 'wd', 'g1', 'g2')}
    del _L2_ffn_all

    def _L3_xattn_setup():
        import jax, jax.numpy as jnp
        import numpy as np
        import math
        B, S, HID, H = (4, 256, 128, 16)
        D = HID // H
        key = jax.random.key(seed)
        ks = jax.random.split(key, 13)
        xavier = lambda k: jax.random.normal(k, (HID, HID), jnp.float32) * math.sqrt(2.0 / (HID + HID))
        return {'q': jax.random.normal(ks[0], (B, S, HID), jnp.float32), 'k': jax.random.normal(ks[1], (B, S, HID), jnp.float32), 'v': jax.random.normal(ks[2], (B, S, HID), jnp.float32), 'padding_mask': jax.random.randint(ks[3], (B, S), 0, 2, jnp.int32), 'Wq': xavier(ks[4]), 'bq': jnp.zeros((HID,), jnp.float32), 'Wk': xavier(ks[5]), 'bk': jnp.zeros((HID,), jnp.float32), 'Wv': xavier(ks[6]), 'bv': jnp.zeros((HID,), jnp.float32), 'Wo': xavier(ks[7]), 'bo': jnp.zeros((HID,), jnp.float32), 'is_causal': 1}
    _L3_xattn_all = _L3_xattn_setup()
    _L3_xattn_in = {k: v for k, v in _L3_xattn_all.items() if k in ('Wq', 'bq', 'Wk', 'bk', 'Wv', 'bv', 'Wo', 'bo')}
    del _L3_xattn_all

    def _L3_ffn_setup():
        import jax, jax.numpy as jnp
        import numpy as np
        EPS = 1e-06
        N_EXPERTS = 8

        def _rms_norm(x, scale, eps=EPS):
            mean_sq = jnp.mean(x.astype(jnp.float32) ** 2, axis=-1, keepdims=True)
            s = scale.astype(jnp.float32) * jax.lax.rsqrt(mean_sq + eps)
            return x * s.astype(x.dtype)

        def _dist2(x, y):
            nx = jnp.sum(x ** 2, axis=-1)[..., :, None]
            ny = jnp.sum(y ** 2, axis=-1)[..., None, :]
            return nx + ny - 2.0 * (x @ y.T)
        key = jax.random.key(seed)
        ks = jax.random.split(key, 5)
        dim, hidden, E = (128, 256, N_EXPERTS)
        x = jax.random.normal(ks[0], (4, 256, dim), dtype=jnp.float32)
        scale = jnp.ones((dim,), dtype=jnp.float32)
        centroids = jax.random.normal(ks[1], (E, dim), dtype=jnp.float32)
        up_w = jax.random.normal(ks[2], (E, dim, hidden * 2), dtype=jnp.float32) * dim ** (-0.5)
        down_w = jax.random.normal(ks[3], (E, hidden, dim), dtype=jnp.float32) * hidden ** (-0.5)
        return {'x': x, 'scale': scale, 'centroids': centroids, 'up_w': up_w, 'down_w': down_w}
    _L3_ffn_all = _L3_ffn_setup()
    _L3_ffn_in = {k: v for k, v in _L3_ffn_all.items() if k in ('scale', 'centroids', 'up_w', 'down_w')}
    del _L3_ffn_all
    return {'x': x, 'ctx_1024': ctx_1024, 'mask_Bx1xSxS2_ik1': mask_Bx1xSxS2_ik1, 'mask_BxS2_ik0': mask_BxS2_ik0, 'mask_BxSxS2_ff0': mask_BxSxS2_ff0, 'g_xattn': g_xattn, 'g_ffn': g_ffn, 'L0_xattn_Wq': _L0_xattn_in['Wq'], 'L0_xattn_bq': _L0_xattn_in['bq'], 'L0_xattn_Wk': _L0_xattn_in['Wk'], 'L0_xattn_bk': _L0_xattn_in['bk'], 'L0_xattn_Wv': _L0_xattn_in['Wv'], 'L0_xattn_bv': _L0_xattn_in['bv'], 'L0_xattn_Wo': _L0_xattn_in['Wo'], 'L0_xattn_bo': _L0_xattn_in['bo'], 'L0_ffn_weight': _L0_ffn_in['weight'], 'L0_ffn_aux_weight1': _L0_ffn_in['aux_weight1'], 'L0_ffn_aux_weight2': _L0_ffn_in['aux_weight2'], 'L0_ffn_bias': _L0_ffn_in['bias'], 'L1_xattn_Wq': _L1_xattn_in['Wq'], 'L1_xattn_bq': _L1_xattn_in['bq'], 'L1_xattn_Wk': _L1_xattn_in['Wk'], 'L1_xattn_bk': _L1_xattn_in['bk'], 'L1_xattn_Wv': _L1_xattn_in['Wv'], 'L1_xattn_bv': _L1_xattn_in['bv'], 'L1_xattn_Wo': _L1_xattn_in['Wo'], 'L1_xattn_bo': _L1_xattn_in['bo'], 'L1_ffn_ln1_w': _L1_ffn_in['ln1_w'], 'L1_ffn_ln1_b': _L1_ffn_in['ln1_b'], 'L1_ffn_ln2_w': _L1_ffn_in['ln2_w'], 'L1_ffn_ln2_b': _L1_ffn_in['ln2_b'], 'L1_ffn_w_qkv': _L1_ffn_in['w_qkv'], 'L1_ffn_b_qkv': _L1_ffn_in['b_qkv'], 'L1_ffn_w_o': _L1_ffn_in['w_o'], 'L1_ffn_b_o': _L1_ffn_in['b_o'], 'L1_ffn_w_gate': _L1_ffn_in['w_gate'], 'L1_ffn_w1': _L1_ffn_in['w1'], 'L1_ffn_b1': _L1_ffn_in['b1'], 'L1_ffn_w2': _L1_ffn_in['w2'], 'L1_ffn_b2': _L1_ffn_in['b2'], 'L2_xattn_ln_g': _L2_xattn_in['ln_g'], 'L2_xattn_ln_b': _L2_xattn_in['ln_b'], 'L2_xattn_cln_g': _L2_xattn_in['cln_g'], 'L2_xattn_cln_b': _L2_xattn_in['cln_b'], 'L2_xattn_Wq': _L2_xattn_in['Wq'], 'L2_xattn_Wkv': _L2_xattn_in['Wkv'], 'L2_xattn_Wout': _L2_xattn_in['Wout'], 'L2_xattn_W1': _L2_xattn_in['W1'], 'L2_xattn_W2': _L2_xattn_in['W2'], 'L2_ffn_wq': _L2_ffn_in['wq'], 'L2_ffn_wk': _L2_ffn_in['wk'], 'L2_ffn_wv': _L2_ffn_in['wv'], 'L2_ffn_wo': _L2_ffn_in['wo'], 'L2_ffn_w_router': _L2_ffn_in['w_router'], 'L2_ffn_wg': _L2_ffn_in['wg'], 'L2_ffn_wu': _L2_ffn_in['wu'], 'L2_ffn_wd': _L2_ffn_in['wd'], 'L2_ffn_g1': _L2_ffn_in['g1'], 'L2_ffn_g2': _L2_ffn_in['g2'], 'L3_xattn_Wq': _L3_xattn_in['Wq'], 'L3_xattn_bq': _L3_xattn_in['bq'], 'L3_xattn_Wk': _L3_xattn_in['Wk'], 'L3_xattn_bk': _L3_xattn_in['bk'], 'L3_xattn_Wv': _L3_xattn_in['Wv'], 'L3_xattn_bv': _L3_xattn_in['bv'], 'L3_xattn_Wo': _L3_xattn_in['Wo'], 'L3_xattn_bo': _L3_xattn_in['bo'], 'L3_ffn_scale': _L3_ffn_in['scale'], 'L3_ffn_centroids': _L3_ffn_in['centroids'], 'L3_ffn_up_w': _L3_ffn_in['up_w'], 'L3_ffn_down_w': _L3_ffn_in['down_w']}

def reference(x, ctx_1024, mask_Bx1xSxS2_ik1, mask_BxS2_ik0, mask_BxSxS2_ff0, g_xattn, g_ffn, L0_xattn_Wq, L0_xattn_bq, L0_xattn_Wk, L0_xattn_bk, L0_xattn_Wv, L0_xattn_bv, L0_xattn_Wo, L0_xattn_bo, L0_ffn_weight, L0_ffn_aux_weight1, L0_ffn_aux_weight2, L0_ffn_bias, L1_xattn_Wq, L1_xattn_bq, L1_xattn_Wk, L1_xattn_bk, L1_xattn_Wv, L1_xattn_bv, L1_xattn_Wo, L1_xattn_bo, L1_ffn_ln1_w, L1_ffn_ln1_b, L1_ffn_ln2_w, L1_ffn_ln2_b, L1_ffn_w_qkv, L1_ffn_b_qkv, L1_ffn_w_o, L1_ffn_b_o, L1_ffn_w_gate, L1_ffn_w1, L1_ffn_b1, L1_ffn_w2, L1_ffn_b2, L2_xattn_ln_g, L2_xattn_ln_b, L2_xattn_cln_g, L2_xattn_cln_b, L2_xattn_Wq, L2_xattn_Wkv, L2_xattn_Wout, L2_xattn_W1, L2_xattn_W2, L2_ffn_wq, L2_ffn_wk, L2_ffn_wv, L2_ffn_wo, L2_ffn_w_router, L2_ffn_wg, L2_ffn_wu, L2_ffn_wd, L2_ffn_g1, L2_ffn_g2, L3_xattn_Wq, L3_xattn_bq, L3_xattn_Wk, L3_xattn_bk, L3_xattn_Wv, L3_xattn_bv, L3_xattn_Wo, L3_xattn_bo, L3_ffn_scale, L3_ffn_centroids, L3_ffn_up_w, L3_ffn_down_w):
    import jax
    import jax.numpy as jnp

    def _L0_xattn_ref(q, k, v, mask, Wq, bq, Wk, bk, Wv, bv, Wo, bo):
        import jax, jax.numpy as jnp
        import numpy as np
        D_MODEL = 128
        N_HEADS = 16
        D_K = D_MODEL // N_HEADS
        NEG_INF = -1000000000.0

        def _split_heads(x):
            B, S, _ = x.shape
            return x.reshape(B, S, N_HEADS, D_K).transpose(0, 2, 1, 3)
        query = _split_heads(q @ Wq + bq)
        key_ = _split_heads(k @ Wk + bk)
        value = _split_heads(v @ Wv + bv)
        scale = 1.0 / np.sqrt(D_K).astype(np.float32)
        scores = jnp.einsum('bhqd,bhkd->bhqk', query, key_) * scale
        scores = jnp.where(mask == 0, NEG_INF, scores)
        attn = jax.nn.softmax(scores, axis=-1)
        ctx = jnp.einsum('bhqk,bhkd->bhqd', attn, value)
        B, H, S, Dk = ctx.shape
        ctx = ctx.transpose(0, 2, 1, 3).reshape(B, S, H * Dk)
        return ctx @ Wo + bo

    def _L0_ffn_ref(x, weight, aux_weight1, aux_weight2, bias):
        import jax, jax.numpy as jnp
        import numpy as np
        D_MODEL = 128
        h = jnp.einsum('btc,cd->btd', x, weight)
        h = jnp.einsum('btc,cd->btd', h, aux_weight1)
        h = jnp.einsum('btc,cd->btd', h, aux_weight2)
        return jnp.tanh(h + bias)

    def _L1_xattn_ref(q, k, mask, Wq, bq, Wk, bk, Wv, bv, Wo, bo):
        import jax, jax.numpy as jnp
        import numpy as np
        B, LQ, LK = (8, 256, 256)
        QD = KD = VD = HD = 128
        qh = jnp.einsum('bld,dh->blh', q, Wq) + bq
        kh = jnp.einsum('bld,dh->blh', k, Wk) + bk
        vh = jnp.einsum('blh,hv->blv', kh, Wv) + bv
        scores = jnp.einsum('bqh,bkh->bqk', qh, kh)
        scores = jnp.where(mask[:, None, :] == 0, jnp.float32(-10000.0), scores)
        probs = jax.nn.softmax(scores, axis=-1)
        out = jnp.einsum('bqk,bkh->bqh', probs, vh)
        return jnp.einsum('bqh,hv->bqv', out, Wo) + bo

    def _L1_ffn_ref(x, ln1_w, ln1_b, ln2_w, ln2_b, w_qkv, b_qkv, w_o, b_o, w_gate, w1, b1, w2, b2):
        import jax, jax.numpy as jnp
        import numpy as np
        from jax import lax
        N_HEADS = 16
        TOP_K = 2
        N_EXPERTS = 8

        def layer_norm(x, w, b, eps=1e-05):
            mu = jnp.mean(x, axis=-1, keepdims=True)
            var = jnp.mean(jnp.square(x - mu), axis=-1, keepdims=True)
            return (x - mu) * lax.rsqrt(var + eps) * w + b

        def attention(x, w_qkv, b_qkv, w_o, b_o):
            B, T, D = x.shape
            dh = D // N_HEADS
            qkv = x @ w_qkv + b_qkv
            q, k, v = jnp.split(qkv, 3, axis=-1)
            q = q.reshape(B, T, N_HEADS, dh)
            k = k.reshape(B, T, N_HEADS, dh)
            v = v.reshape(B, T, N_HEADS, dh)
            scores = jnp.einsum('bqhd,bkhd->bhqk', q, k) / jnp.sqrt(jnp.float32(dh)).astype(x.dtype)
            probs = jax.nn.softmax(scores, axis=-1)
            ctx = jnp.einsum('bhqk,bkhd->bqhd', probs, v).reshape(B, T, D)
            return ctx @ w_o + b_o

        def moe_ff(x, w_gate, w1, b1, w2, b2):
            B, T, D = x.shape
            t = x.reshape(B * T, D)
            probs = jax.nn.softmax(t @ w_gate, axis=-1)
            tw, ti = lax.top_k(probs, TOP_K)
            tw = tw / jnp.sum(tw, axis=-1, keepdims=True)
            out = jnp.zeros_like(t)
            for e in range(N_EXPERTS):
                we = jnp.sum(jnp.where(ti == e, tw, 0.0), axis=-1)
                h = jax.nn.gelu(t @ w1[e] + b1[e]) @ w2[e] + b2[e]
                out = out + we[:, None] * h
            return out.reshape(B, T, D)
        h = x + attention(layer_norm(x, ln1_w, ln1_b), w_qkv, b_qkv, w_o, b_o)
        return h + moe_ff(layer_norm(h, ln2_w, ln2_b), w_gate, w1, b1, w2, b2)

    def _L2_xattn_ref(x, context, mask, ln_g, ln_b, cln_g, cln_b, Wq, Wkv, Wout, W1, W2):
        import jax, jax.numpy as jnp
        import numpy as np
        DIM = 128
        CTX_DIM = 128
        HEADS = 16
        DIM_HEAD = 64
        INNER = HEADS * DIM_HEAD
        FF_INNER = 4 * DIM
        EPS = 1e-05

        def layer_norm(x, g, b):
            mu = jnp.mean(x, axis=-1, keepdims=True)
            var = jnp.var(x, axis=-1, keepdims=True)
            return (x - mu) * jax.lax.rsqrt(var + EPS) * g + b
        scale = DIM_HEAD ** (-0.5)
        xn = layer_norm(x, ln_g, ln_b)
        cn = layer_norm(context, cln_g, cln_b)
        b, n, _ = xn.shape
        q = (xn @ Wq).reshape(b, n, HEADS, DIM_HEAD).transpose(0, 2, 1, 3) * scale
        kv = cn @ Wkv
        k, v = jnp.split(kv, 2, axis=-1)
        sim = jnp.einsum('bhid,bjd->bhij', q, k) + mask[:, None, :, :]
        attn = jax.nn.softmax(sim, axis=-1)
        out = jnp.einsum('bhij,bjd->bhid', attn, v)
        out = out.transpose(0, 2, 1, 3).reshape(b, n, INNER) @ Wout
        h = xn @ W1
        val, gate = jnp.split(h, 2, axis=-1)
        out = out + jax.nn.silu(gate) * val @ W2
        return out

    def _L2_ffn_ref(x, wq, wk, wv, wo, w_router, wg, wu, wd, g1, g2):
        import jax, jax.numpy as jnp
        import numpy as np
        EMBED = 128
        HEADS = 16
        HEAD_DIM = EMBED // HEADS
        NUM_EXPERTS = 8
        TOP_K = 2
        HIDDEN = (int(2 * (4 * EMBED) / 3) + 63) // 64 * 64
        SEQ = 256
        BATCH = 2
        ROPE_BASE = 10000.0
        EPS = 1e-06

        def _rope_tables(seq_len, dim):
            inv_freq = 1.0 / ROPE_BASE ** (np.arange(0, dim, 2, dtype=np.float32) / dim)
            t = np.arange(seq_len, dtype=np.float32)
            freqs = np.einsum('i,j->ij', t, inv_freq)
            emb = np.concatenate([freqs, freqs], axis=-1)
            return (jnp.asarray(np.cos(emb)), jnp.asarray(np.sin(emb)))

        def _rotate_half(x):
            x1, x2 = jnp.split(x, 2, axis=-1)
            return jnp.concatenate([-x2, x1], axis=-1)

        def _rmsnorm(x, w):
            return x * jax.lax.rsqrt(jnp.mean(x * x, axis=-1, keepdims=True) + EPS) * w

        def _attention(x, wq, wk, wv, wo):
            B, S, _ = x.shape
            q = (x @ wq).reshape(B, S, HEADS, HEAD_DIM).transpose(0, 2, 1, 3)
            k = (x @ wk).reshape(B, S, HEADS, HEAD_DIM).transpose(0, 2, 1, 3)
            v = (x @ wv).reshape(B, S, HEADS, HEAD_DIM).transpose(0, 2, 1, 3)
            cos, sin = _rope_tables(S, HEAD_DIM)
            cos = cos[None, None]
            sin = sin[None, None]
            q = q * cos + _rotate_half(q) * sin
            k = k * cos + _rotate_half(k) * sin
            scale = HEAD_DIM ** (-0.5)
            scores = jnp.einsum('bhqd,bhkd->bhqk', q, k) * scale
            causal = jnp.triu(jnp.ones((S, S), bool), k=1)
            scores = jnp.where(causal, -jnp.inf, scores)
            attn = jax.nn.softmax(scores, axis=-1)
            out = jnp.einsum('bhqk,bhkd->bhqd', attn, v)
            out = out.transpose(0, 2, 1, 3).reshape(B, S, EMBED)
            return out @ wo

        def _moe(x, w_router, wg, wu, wd):
            B, S, E = x.shape
            xf = x.reshape(-1, E)
            logits = xf @ w_router
            probs = jax.nn.softmax(logits, axis=-1)
            topw, topi = jax.lax.top_k(probs, TOP_K)
            topw = topw / jnp.sum(topw, axis=-1, keepdims=True)
            combine = jnp.sum(jax.nn.one_hot(topi, NUM_EXPERTS, dtype=xf.dtype) * topw[..., None], axis=1)
            g = jax.nn.silu(jnp.einsum('td,xdh->txh', xf, wg))
            u = jnp.einsum('td,xdh->txh', xf, wu)
            eo = jnp.einsum('txh,xhd->txd', g * u, wd)
            out = jnp.einsum('txd,tx->td', eo, combine)
            return out.reshape(B, S, E)
        h = x + _attention(_rmsnorm(x, g1), wq, wk, wv, wo)
        y = h + _moe(_rmsnorm(h, g2), w_router, wg, wu, wd)
        return y

    def _L3_xattn_ref(q, k, v, padding_mask, Wq, bq, Wk, bk, Wv, bv, Wo, bo, is_causal):
        import jax, jax.numpy as jnp
        import numpy as np
        import math
        B, S, HID, H = (4, 256, 128, 16)
        D = HID // H
        b, s, _ = q.shape
        proj = lambda x, W, bias: (x @ W.T + bias).reshape(b, s, H, D).transpose(0, 2, 1, 3)
        qh, kh, vh = (proj(q, Wq, bq), proj(k, Wk, bk), proj(v, Wv, bv))
        corr = jnp.einsum('bhqd,bhkd->bhqk', qh, kh) / math.sqrt(D)
        corr = jnp.where(padding_mask[:, None, :, None] == 0, jnp.float32(-1000000000.0), corr)
        if is_causal:
            tri = jnp.triu(jnp.ones((s, s), bool), k=1)
            corr = jnp.where(tri[None, None], -jnp.inf, corr)
        prob = jax.nn.softmax(corr, axis=-1)
        hidden = jnp.einsum('bhqk,bhkd->bhqd', prob, vh)
        hidden = hidden.transpose(0, 2, 1, 3).reshape(b, s, H * D)
        return hidden @ Wo.T + bo

    def _L3_ffn_ref(x, scale, centroids, up_w, down_w):
        import jax, jax.numpy as jnp
        import numpy as np
        EPS = 1e-06
        N_EXPERTS = 8

        def _rms_norm(x, scale, eps=EPS):
            mean_sq = jnp.mean(x.astype(jnp.float32) ** 2, axis=-1, keepdims=True)
            s = scale.astype(jnp.float32) * jax.lax.rsqrt(mean_sq + eps)
            return x * s.astype(x.dtype)

        def _dist2(x, y):
            nx = jnp.sum(x ** 2, axis=-1)[..., :, None]
            ny = jnp.sum(y ** 2, axis=-1)[..., None, :]
            return nx + ny - 2.0 * (x @ y.T)
        skip = x
        xn = _rms_norm(x, scale)
        ids = jnp.argmin(_dist2(xn, centroids), axis=-1)
        out = jnp.zeros_like(x)
        for e in range(N_EXPERTS):
            h = jnp.einsum('bsd,dh->bsh', xn, up_w[e])
            a, g = jnp.split(h, 2, axis=-1)
            y = jnp.einsum('bsh,hd->bsd', a * jax.nn.silu(g), down_w[e])
            out = jnp.where((ids == e)[..., None], y, out)
        return out + skip
    x = x + jnp.tanh(g_xattn[0]) * _L0_xattn_ref(_layernorm(x, axis=-1), ctx_1024, ctx_1024, mask_Bx1xSxS2_ik1, L0_xattn_Wq, L0_xattn_bq, L0_xattn_Wk, L0_xattn_bk, L0_xattn_Wv, L0_xattn_bv, L0_xattn_Wo, L0_xattn_bo)
    x = x + jnp.tanh(g_ffn[0]) * _L0_ffn_ref(_layernorm(x, axis=-1), L0_ffn_weight, L0_ffn_aux_weight1, L0_ffn_aux_weight2, L0_ffn_bias)
    x = x + jnp.tanh(g_xattn[1]) * _L1_xattn_ref(_layernorm(x, axis=-1), ctx_1024, mask_BxS2_ik0, L1_xattn_Wq, L1_xattn_bq, L1_xattn_Wk, L1_xattn_bk, L1_xattn_Wv, L1_xattn_bv, L1_xattn_Wo, L1_xattn_bo)
    x = x + jnp.tanh(g_ffn[1]) * _L1_ffn_ref(_layernorm(x, axis=-1), L1_ffn_ln1_w, L1_ffn_ln1_b, L1_ffn_ln2_w, L1_ffn_ln2_b, L1_ffn_w_qkv, L1_ffn_b_qkv, L1_ffn_w_o, L1_ffn_b_o, L1_ffn_w_gate, L1_ffn_w1, L1_ffn_b1, L1_ffn_w2, L1_ffn_b2)
    x = x + jnp.tanh(g_xattn[2]) * _L2_xattn_ref(_layernorm(x, axis=-1), ctx_1024, mask_BxSxS2_ff0, L2_xattn_ln_g, L2_xattn_ln_b, L2_xattn_cln_g, L2_xattn_cln_b, L2_xattn_Wq, L2_xattn_Wkv, L2_xattn_Wout, L2_xattn_W1, L2_xattn_W2)
    x = x + jnp.tanh(g_ffn[2]) * _L2_ffn_ref(_layernorm(x, axis=-1), L2_ffn_wq, L2_ffn_wk, L2_ffn_wv, L2_ffn_wo, L2_ffn_w_router, L2_ffn_wg, L2_ffn_wu, L2_ffn_wd, L2_ffn_g1, L2_ffn_g2)
    x = x + jnp.tanh(g_xattn[3]) * _L3_xattn_ref(_layernorm(x, axis=-1), ctx_1024, ctx_1024, mask_BxS2_ik0, L3_xattn_Wq, L3_xattn_bq, L3_xattn_Wk, L3_xattn_bk, L3_xattn_Wv, L3_xattn_bv, L3_xattn_Wo, L3_xattn_bo, 1)
    x = x + jnp.tanh(g_ffn[3]) * _L3_ffn_ref(_layernorm(x, axis=-1), L3_ffn_scale, L3_ffn_centroids, L3_ffn_up_w, L3_ffn_down_w)
    return x

_drawn_inputs = setup_inputs


def setup_inputs(seed=0):
    import zlib

    import numpy as np

    out = dict(_drawn_inputs(seed))
    spreads = {'L0_xattn_bq': (0.0, 0.1),
     'L0_xattn_bk': (0.0, 2.0),
     'L0_xattn_bv': (0.0, 0.1),
     'L0_xattn_bo': (0.0, 0.1),
     'L0_ffn_bias': (0.0, 0.1),
     'L1_ffn_ln1_w': (1.0, 0.2),
     'L1_ffn_ln1_b': (0.0, 0.1),
     'L1_ffn_ln2_w': (1.0, 0.2),
     'L1_ffn_ln2_b': (0.0, 0.1),
     'L1_ffn_b_qkv': (0.0, 0.1),
     'L1_ffn_b_o': (0.0, 0.1),
     'L1_ffn_b1': (0.0, 0.1),
     'L1_ffn_b2': (0.0, 0.1),
     'L2_xattn_ln_g': (1.0, 0.6),
     'L2_xattn_ln_b': (0.0, 0.8),
     'L2_xattn_cln_g': (1.0, 0.6),
     'L2_xattn_cln_b': (0.0, 0.676),
     'L2_ffn_g1': (1.0, 0.6),
     'L2_ffn_g2': (1.0, 0.6),
     'L3_xattn_bq': (0.0, 2.0),
     'L3_xattn_bk': (0.0, 2.0),
     'L3_xattn_bv': (0.0, 0.337),
     'L3_xattn_bo': (0.0, 0.365),
     'L3_ffn_scale': (1.0, 0.2)}
    factors = {'g_ffn': 20.966,
     'L2_xattn_Wq': 8.0,
     'L2_xattn_W1': 4.552,
     'L2_xattn_W2': 4.793,
     'L2_ffn_wq': 8.0,
     'L2_ffn_wk': 8.0,
     'L2_ffn_w_router': 5.779,
     'L2_ffn_wg': 5.852,
     'L2_ffn_wu': 5.04,
     'L2_ffn_wd': 5.41,
     'L3_xattn_Wq': 3.12,
     'L3_xattn_Wk': 2.884}
    for name, (base, spread) in spreads.items():
        noise = np.random.default_rng([zlib.crc32(name.encode()), seed]).standard_normal(out[name].shape)
        drawn = base * np.exp(spread * noise) if base else spread * noise
        out[name] = jnp.asarray(drawn.astype(out[name].dtype))
    for name, factor in factors.items():
        out[name] = (out[name] * factor).astype(out[name].dtype)
    return out
```

```python
from contextlib import ExitStack

import concourse.bass as bass
import numpy as np
from concourse import mybir

F32 = mybir.dt.float32
I32 = mybir.dt.int32
U32 = mybir.dt.uint32
ALU = mybir.AluOpType
ACT = mybir.ActivationFunctionType
AX = mybir.AxisListType

P = 128
SEQ = 64
NSEQ = 32
BT = 4
T = BT * SEQ
NT = NSEQ // BT
W2T = 2 * T
NE = 8
DK = 8
GELU_C = float(np.sqrt(2.0 / np.pi))

FX, FC, FM, FCOLS = 0, T, 2 * T, 3 * T
IM0, IM1, IM3, ICOLS = 0, T, T + 2 * SEQ, T + 2 * SEQ + BT


def columns(parts):
    at, place = 0, {}
    for name, n in parts:
        place[name] = (at, at + n)
        at += n
    return place, at


CONST_PARTS = [("ident", P), ("center", P), ("mean", P), ("cos", SEQ), ("sin", SEQ), ("causal", SEQ),
               ("headsel", 4), ("halves", 32), ("iota8", 8)]
VEC_PARTS = [("gx", 4), ("gf", 4), ("bq0", 1), ("bk0", 1), ("bv0", 2), ("bo0", 1), ("bf0", 1),
             ("bq1", 1), ("bk1", 1), ("bv1", 1), ("bo1", 1), ("ln1w", 1), ("ln1b", 1), ("ln2w", 1), ("ln2b", 1),
             ("bqa", 1), ("bka", 1), ("bva", 2), ("boa", 1), ("b1", NE * 4), ("g1", 1), ("g2", 1),
             ("lng", 1), ("lnb", 1), ("clng", 1), ("clnb", 1), ("bq3", 1), ("bk3", 1), ("bv3", 2), ("bo3", 1),
             ("scale3", 1), ("cent", NE), ("gate1", NE), ("router2", NE), ("b2", P)]
W_PARTS = [
    ("early", [("q0", P), ("k0", P), ("v0", P), ("o0", 2 * P),
               ("q1", P), ("k1", P), ("v1", P), ("o1", P), ("qa", P), ("ka", P), ("va", P), ("oa", 2 * P)]),
    ("ff0", [("wT", P), ("a1T", P), ("a2", P)]),
    ("moe1", [("up1", NE * 4 * P), ("dn1", NE * 4 * P)]),
    ("mid", [("qx", 8 * P), ("kx", P), ("vx", 64), ("ox", 8 * P), ("ffx", 8 * P), ("ff2x", 4 * P),
             ("q2", P), ("qr2", P), ("k2", P), ("kr2", P), ("v2", P), ("o2", 2 * P)]),
    ("moe2", [("up2", NE * 6 * P), ("dn2", NE * 3 * P)]),
    ("late", [("q3", P), ("k3", P), ("v3", P), ("o3", 2 * P)]),
    ("moe3", [("up3", NE * 4 * P), ("dn3", NE * 2 * P)]),
]

NORM_SIGNALS = ["centred", "squared", "copied", "meansq", "stat", "first", "second", "rooted", "spread", "normed",
                "chain"]
ATTN_SIGNALS = NORM_SIGNALS + [
    "big_context", "big_contextT_taken", "big_exped", "big_hidden", "big_hidden_done",
    "big_hidden_tanh", "big_k_taken", "big_probsT", "big_probsT_taken", "big_probs_normed",
    "big_proj_k", "big_proj_q", "big_proj_v", "big_q_heads", "big_q_heads_dve", "big_scores",
    "big_shifted", "big_v_blocks", "context", "contextT", "contextT_taken", "context_normed",
    "exped", "ff_hidden", "ff_hidden_tanh", "gated", "k_taken", "probsT", "probsT_taken",
    "proj_k", "proj_q", "proj_v", "projected", "projected_inner", "q_heads", "roped", "scores",
    "shifted", "v_blocks", "x_new"]
MOE_SIGNALS = ["m_" + name for name in NORM_SIGNALS] + ["m_rowsq", "m_logits", "m_gap", "m_gap_exp",
               "m_comb", "m_combT", "m_combT_taken", "m_weight", "m_weight_taken", "m_up", "m_tanh", "m_up_free",
               "m_act", "m_square", "m_poly", "m_cubic", "m_down", "m_out"]


def take_turns(a, b):
    order = sorted([((i + 0.5) / max(a, 1), 0) for i in range(a)] + [((i + 0.5) / max(b, 1), 1) for i in range(b)])
    return [half for _, half in order]


def side_by_side(attn, moe, order):
    halves = [attn, moe]
    for half in order:
        next(halves[half])
    for half in halves:
        if half is not None:
            assert next(half, "end") == "end", "a half has more slots on this engine than on TensorE"


def build(nc, fin, iin, consts, vecs, weights, out):
    cplace, ccols = columns(CONST_PARTS)
    vplace, vcols = columns(VEC_PARTS)
    wplace = {}
    for group, parts in W_PARTS:
        place, _ = columns(parts)
        wplace.update({name: (group, *ab) for name, ab in place.items()})

    with ExitStack() as ctx:
        def sb(name, shape, dt=F32):
            return ctx.enter_context(nc.sbuf_tensor(name, shape, dt))

        def bank(name):
            return ctx.enter_context(nc.psum_tensor(name, [P, W2T], F32))

        def sem(name):
            return ctx.enter_context(nc.semaphore(name))

        csb = sb("csb", [P, ccols])
        vsb = sb("vsb", [P, vcols])
        wsb = {g: sb(f"w_{g}", [P, columns(parts)[1]]) for g, parts in W_PARTS if g != "ff0"}

        def C(name):
            a, b = cplace[name]
            return csb[:, a:b]

        def V(name, i=0, n=1):
            a, _ = vplace[name]
            return vsb[:, a + i:a + i + n]

        def Wt(name, i=0, n=1, rows=P):
            g, a, _ = wplace[name]
            return wsb[g][0:rows, a + i * P:a + (i + n) * P]

        ff0 = sb("ff0", [P, P])
        tg = sb("tg", [P, 8])
        bo = sb("bo", [P, 4])
        bog = sb("bog", [P, 4])
        bq4 = sb("bq4", [P, 3, 4])
        cent2 = sb("cent2", [P, NE])
        centsq = sb("centsq", [P, NE])
        b2x2 = sb("b2x2", [NE, P])
        negones = sb("negones", [P, NE])

        stage_f = sb("stage_f", [P, FCOLS])
        stage_i = sb("stage_i", [P, ICOLS], I32)
        tile_f = sb("tile_f", [P, FCOLS])
        xF, ctxF, addmask = tile_f[:, FX:FX + T], tile_f[:, FC:FC + T], tile_f[:, FM:FM + T]
        xS = sb("xS", [P, T])
        ctxS = sb("ctxS", [P, T])
        hF = sb("hF", [P, T])
        hS = sb("hS", [P, T])
        rowF = sb("rowF", [P, BT])
        rowS = sb("rowS", [P, BT])

        SA, SB, TP, OY = bank("SA"), bank("SB"), bank("TP"), bank("OY")
        fx = sb("fx", [P, 2, T])
        un = sb("un", [P, W2T])
        small = sb("small", [P, 24])
        msmall = sb("msmall", [P, 24])
        neghalf = sb("neghalf", [P, 4])
        xn = sb("xn", [P, T])
        q4 = sb("q4", [P, BT, 4, SEQ])
        qk = sb("qk", [P, W2T])
        qkr = sb("qkr", [P, W2T])
        vblk = sb("vblk", [P, BT, P])
        probs = sb("probs", [P, 2, W2T])
        probsT = sb("probsT", [P, 2, W2T])
        mx = sb("mx", [P, 2, 8])
        sums = sb("sums", [P, BT, 4, 2])
        rinv = sb("rinv", [P, BT * 8])
        maskA = sb("maskA", [P, BT, SEQ])
        mask1 = sb("mask1", [P, 2, 2 * SEQ])
        upd = sb("upd", [P, T])
        qx = sb("qx", [P, 4, BT, 2, SEQ])
        vdiag = sb("vdiag", [P, BT, P])
        otx = sb("otx", [P, 4, W2T])
        sq = qkr
        onorm = upd[:, :].rearrange("p (b n) -> p b n", b=BT)
        otT = qkr[0:64, :].rearrange("p (b h q) -> p b h q", b=BT, h=2)
        fact = q4[:, :, :, :].rearrange("p a b q -> p a (b q)")

        H0, H1, WB, YM = bank("H0"), bank("H1"), bank("WB"), bank("YM")
        H = [H0, H1]
        msq = sb("msq", [P, T])
        mu = sb("mu", [P, T])
        my = sb("my", [P, T])
        lg = sb("lg", [P, 2, NE])
        top = sb("top", [P, 2, 8])
        topi = sb("topi", [P, 2, 8], U32)
        topf = sb("topf", [P, 2, 8])
        gap = sb("gap", [P, 2])
        gapx = sb("gapx", [P, 2])
        w01 = sb("w01", [P, 2, 2])
        pick = sb("pick", [P, 2, 2, NE])
        comb = sb("comb", [P, 2, NE])
        combT = sb("combT", [NE, T])
        wexp = sb("wexp", [P, 2, T])
        hb = sb("hb", [P, 3, W2T])
        hp = sb("hp", [P, 2, W2T])
        act = sb("act", [P, 3, W2T])

        wsb["ff0"] = act[:, 0:2, :].rearrange("p a n -> p (a n)")[:, 0:3 * P]
        a12 = act[:, 2, 0:P]

        dma_const = sem("dma_const")
        dma_vec = sem("dma_vec")
        dma_w = {g: sem(f"dma_w_{g}") for g, _ in W_PARTS}
        dma_first = sem("dma_first")
        sets = [{n: sem(f"{n}_0") for n in ATTN_SIGNALS + MOE_SIGNALS + ["tile_in"] if not n.startswith(("big_", "ff_"))},
                {n: sem(f"{n}_1") for n in ATTN_SIGNALS + MOE_SIGNALS + ["out_store"]}]
        setup_tanh, setup_pe, setup_act, setup_dve = (sets[1][n] for n in ("ff_hidden_tanh", "ff_hidden", "copied", "stat"))
        late_pe, late_dve = sets[0]["projected"], sets[0]["gated"]

        class Counts:

            def __init__(self, sems):
                self.sems, self.seen, self.given = sems, {}, {}

            def next(self, name):
                self.seen[name] = self.seen.get(name, 0) + 1
                return self.sems[name], self.seen[name]

            def skip(self, name, n):
                self.seen[name] = self.seen.get(name, 0) + n

            def give(self, name):
                self.given[name] = self.given.get(name, 0) + 1
                return self.sems[name], 1

        class Norm:
            def __init__(self, prefix, centred, stat, spread, spread2, squares, u, small):
                self.sig = lambda name: prefix + name
                self.centred, self.stat, self.spread, self.spread2 = centred, stat, spread, spread2
                self.squares, self.u, self.small = squares, u, small

            def col(self, what, n):
                return self.small[:, 4 * what:4 * what + n]

        ANORM = Norm("", SA, SB, TP, OY, sq, un, small)
        MNORM = Norm("m_", H0, H1, WB, None, msq, mu, msmall)

        def norm_pe(c, k, kind, src, fresh=False, second=None):
            pe = nc.tensor
            n = 2 if second is None else 4
            if fresh:
                pe.wait_ge(*c.next("x_new"))
            if kind != "rms":
                mm = pe.matmul(k.centred[:, 0:T], C("center"), src, start=True, stop=True)
                if second is not None:
                    mm = pe.matmul(k.centred[:, T:], C("center"), second, start=True, stop=True)
                mm.then_inc(*c.give(k.sig("centred")))
            yield
            pe.wait_ge(*c.next(k.sig("squared")))
            for s in range(n):
                mm = pe.matmul(k.stat[:, s:s + 1], k.squares[:, s * P:(s + 1) * P], C("mean")[:, 0:1],
                               start=True, stop=True, skip_group_check=True)
            mm.then_inc(*c.give(k.sig("meansq")))
            yield
            if kind == "both":
                yield
            pe.wait_ge(*c.next(k.sig("rooted")))
            for s in range(2):
                if kind == "both":
                    pe.matmul(k.spread[:, T + s * P:T + (s + 1) * P], k.col(5, 4)[:, s:s + 1].to_broadcast([P, P]),
                              C("ident"), start=True, stop=True)
                if n == 4:
                    pe.matmul(k.spread2[:, s * P:(s + 1) * P], k.col(2, 4)[:, 2 + s:3 + s].to_broadcast([P, P]),
                              C("ident"), start=True, stop=True)
                mm = pe.matmul(k.spread[:, s * P:(s + 1) * P], k.col(2, 4)[:, s:s + 1].to_broadcast([P, P]),
                               C("ident"), start=True, stop=True)
            mm.then_inc(*c.give(k.sig("spread")))
            yield

        def norm_act(c, k, kind, src=None, w=T):
            a = nc.scalar
            if kind == "rms":
                a.activation(k.squares[:, 0:w], src, ACT.Square).then_inc(*c.give(k.sig("squared")))
            else:
                a.wait_ge(*c.next(k.sig("centred")))
                a.activation(k.squares[:, 0:w], k.centred[:, 0:w], ACT.Square).then_inc(*c.give(k.sig("squared")))
                a.activation(k.u[:, 0:w], k.centred[:, 0:w], ACT.Copy).then_inc(*c.give(k.sig("copied")))
            yield
            yield
            if kind == "both":
                yield
            yield

        def norm_pool(c, k, kind, w=T):
            g, n = nc.gpsimd, w // P
            yield
            g.wait_ge(*c.next(k.sig("stat")))
            g.tensor_tensor(k.col(2, n), k.col(1, n), neghalf[:, 0:n], ALU.pow)\
             .then_inc(*c.give(k.sig("rooted" if kind != "both" else "first")))
            yield
            if kind == "both":
                g.wait_ge(*c.next(k.sig("stat")))
                g.tensor_tensor(k.col(4, 2), k.col(3, 2), neghalf[:, 0:2], ALU.pow).then_inc(*c.give(k.sig("second")))
                yield
            yield

        def link(c, ins, name="chain"):
            ins.then_inc(*c.give(name))
            nc.vector.wait_ge(*c.next(name))

        def norm_dve(c, k, kind, src=None, y=None, g=None, b=None, eps2=None, w=T, ctx_gb=None):
            dve, n = nc.vector, w // P
            lk = lambda ins: link(c, ins, k.sig("chain"))
            yield
            dve.wait_ge(*c.next(k.sig("meansq")))
            if kind == "both":
                dve.tensor_copy(k.col(0, 2), k.stat[:, 0:2])
            dve.tensor_scalar(k.col(1, n), k.stat[:, 0:n], eps2 if kind == "rms" else 1e-5, None, ALU.add)\
               .then_inc(*c.give(k.sig("stat")))
            yield
            if kind == "both":
                r = k.col(2, 2)
                dve.wait_ge(*c.next(k.sig("first")))
                lk(dve.tensor_tensor(k.col(3, 2), k.col(0, 2), r, ALU.mult))
                lk(dve.tensor_tensor(k.col(3, 2), k.col(3, 2), r, ALU.mult))
                dve.tensor_scalar(k.col(3, 2), k.col(3, 2), eps2, None, ALU.add).then_inc(*c.give(k.sig("stat")))
                dve.wait_ge(*c.next(k.sig("second")))
                dve.tensor_tensor(k.col(5, 2), k.col(4, 2), r, ALU.mult).then_inc(*c.give(k.sig("rooted")))
                yield
            dve.wait_ge(*c.next(k.sig("spread")))
            if kind == "rms":
                dve.scalar_tensor_tensor(out=y, in0=src, scalar=g, in1=k.spread[:, 0:T], op0=ALU.mult, op1=ALU.mult)\
                   .then_inc(*c.give(k.sig("normed")))
                yield
                return
            dve.wait_ge(*c.next(k.sig("copied")))
            if kind == "both":
                ins = dve.scalar_tensor_tensor(out=y, in0=k.u[:, 0:T], scalar=g, in1=k.spread[:, T:], op0=ALU.mult,
                                               op1=ALU.mult)
                if b is not None:
                    lk(ins)
                    ins = dve.tensor_scalar(y, y, b, None, ALU.add)
                lk(ins)
            if ctx_gb is not None:
                lk(dve.scalar_tensor_tensor(out=k.u[:, T:], in0=k.u[:, T:], scalar=ctx_gb[0], in1=k.spread2[:, 0:T],
                                            op0=ALU.mult, op1=ALU.mult))
                dve.tensor_scalar(k.u[:, T:], k.u[:, T:], ctx_gb[1], None, ALU.add)
            ins = dve.tensor_tensor(k.u[:, 0:T], k.u[:, 0:T], k.spread[:, 0:T], ALU.mult)
            if kind == "layer" and y is not None:
                lk(ins)
                ins = dve.tensor_scalar(y, k.u[:, 0:T], g, b, ALU.mult, ALU.add)
            ins.then_inc(*c.give(k.sig("normed")))
            yield

        def heads_pe(c, wq, wk, wv, wo, xq, xkv, rope=None, inner=False):
            pe = nc.tensor
            pe.wait_ge(*c.next("normed"))
            if rope is None:
                pe.matmul(SA[:, 0:T], wq, xq, start=True, stop=True).then_inc(*c.give("proj_q"))
                pe.matmul(SB[:, 0:T], wk, xkv, start=True, stop=True).then_inc(*c.give("proj_k"))
            else:
                pe.matmul(SA[:, 0:T], wq, xq, start=True, stop=True)
                pe.matmul(SA[:, T:], wk, xkv, start=True, stop=True)
                pe.matmul(SB[:, 0:T], rope[0], xq, start=True, stop=True)
                pe.matmul(SB[:, T:], rope[1], xkv, start=True, stop=True).then_inc(*c.give("proj_q"))
            for b in range(BT):
                for half in (0, SEQ):
                    mm = pe.matmul(TP[half:half + SEQ, b * P:(b + 1) * P], xkv[:, b * SEQ:(b + 1) * SEQ], wv,
                                   start=True, stop=True, skip_group_check=True)
            mm.then_inc(*c.give("proj_v"))
            yield
            kT = qk[:, T:]

            def scores(g):
                if g == 0:
                    pe.wait_ge(*c.next("q_heads"))
                    if rope is None:
                        pe.wait_ge(*c.next("k_taken"))
                S = (SA, SB)[g % 2]
                r = slice(32 * g, 32 * g + 32)
                for b in range(BT):
                    for j in range(2):
                        at = (2 * b + j) * SEQ
                        mm = pe.matmul(S[:, at:at + SEQ], q4[r, b, 2 * j:2 * j + 2, :].rearrange("p h q -> p (h q)"),
                                       kT[r, b * SEQ:(b + 1) * SEQ], start=True, stop=True,
                                       skip_group_check=True)
                mm.then_inc(*c.give("scores"))

            def transposes(g):
                pe.wait_ge(*c.next("exped"))
                if g == 0:
                    pe.wait_ge(*c.next("v_blocks"))
                else:
                    pe.wait_ge(*c.next("probsT_taken"))
                for b in range(BT):
                    mm = pe.transpose(TP[:, b * P:(b + 1) * P], probs[:, g % 2, b * P:(b + 1) * P], C("ident"))
                mm.then_inc(*c.give("probsT"))

            def weigh(g):
                if g == 3:
                    pe.wait_ge(*c.next("probsT_taken"))
                for b in range(BT):
                    at = b * P + 32 * g
                    mm = pe.matmul(OY[:, at:at + 32], probsT[:, g % 2, b * P:(b + 1) * P],
                                   vblk[:, b, 32 * g:32 * g + 32], start=True, stop=True, skip_group_check=True)
                if g == 3:
                    mm.then_inc(*c.give("context"))

            for k in range(6):
                if k < 4:
                    scores(k)
                if 1 <= k < 5:
                    transposes(k - 1)
                if k >= 2:
                    weigh(k - 2)
                yield
            pe.wait_ge(*c.next("context_normed"))
            for b in range(BT):
                mm = pe.transpose(TP[0:64, b * P:(b + 1) * P], onorm[:, b, :], C("ident"))
            mm.then_inc(*c.give("contextT"))
            yield
            pe.wait_ge(*c.next("contextT_taken"))
            for h2 in range(2):
                mm = pe.matmul(SA[:, 0:T], wo(h2), otT[:, :, h2, :], start=(h2 == 0), stop=(h2 == 1))
            mm.then_inc(*c.give("projected_inner" if inner else "projected"))
            yield

        def heads_act(c, bias4, gate=None, rope=False):
            a = nc.scalar
            if rope:
                a.wait_ge(*c.next("roped"))
                src = qk[:, 0:T]
            else:
                a.wait_ge(*c.next("proj_q"))
                src = SA[:, 0:T]
            for i in range(4):
                q = a.activation(q4[:, :, i, :], src.rearrange("p (b q) -> p b q", b=BT), ACT.Identity, scale=csb[:, cplace["headsel"][0] + i:][:, 0:1],
                                 bias=bias4(i) if bias4 else 0.0)
            q.then_inc(*c.give("q_heads"))
            yield
            for k in range(6):
                if 1 <= k < 5:
                    a.wait_ge(*c.next("probsT"))
                    a.activation(probsT[:, (k - 1) % 2, :], TP[:, :], ACT.Copy).then_inc(*c.give("probsT_taken"))
                if k < 4:
                    a.wait_ge(*c.next("shifted"))
                    a.activation(probs[:, k % 2, :], probs[:, k % 2, :], ACT.Exp).then_inc(*c.give("exped"))
                yield
            a.wait_ge(*c.next("contextT"))
            a.activation(qkr[0:64, :], TP[0:64, :], ACT.Copy)\
             .then_inc(*c.give("contextT_taken"))
            yield
            if gate is not None:
                a.wait_ge(*c.next("projected"))
                a.activation(upd[:, :], SA[:, 0:T], ACT.Identity, scale=gate[0], bias=gate[1])\
                 .then_inc(*c.give("gated"))
            yield

        def heads_dve(c, kbias, mask, x, inner=None, rope=False):
            dve = nc.vector
            kT = qk[:, T:]
            if rope:
                dve.wait_ge(*c.next("proj_q"))
                cs = C("cos").unsqueeze(1).to_broadcast([P, 8, SEQ])
                sn = C("sin").unsqueeze(1).to_broadcast([P, 8, SEQ])
                by_seq = lambda t: t.rearrange("p (a t) -> p a t", t=SEQ)
                dve.tensor_tensor(by_seq(qk[:, :]), by_seq(SA[:, :]), cs, ALU.mult)
                link(c, dve.tensor_tensor(by_seq(qkr[:, :]), by_seq(SB[:, :]), sn, ALU.mult))
                dve.tensor_tensor(qk[:, :], qk[:, :], qkr[:, :], ALU.add).then_inc(*c.give("roped"))
            else:
                dve.wait_ge(*c.next("proj_k"))
                if kbias is None:
                    dve.tensor_copy(kT, SB[:, 0:T]).then_inc(*c.give("k_taken"))
                else:
                    dve.tensor_scalar(kT, SB[:, 0:T], kbias, None, ALU.add).then_inc(*c.give("k_taken"))
            dve.wait_ge(*c.next("proj_v"))
            halves = C("halves").unsqueeze(1).to_broadcast([P, 16, 32])
            dve.tensor_tensor(vblk[:, :, :].rearrange("p b (g n) -> p (b g) n", g=4),
                              TP[:, :].rearrange("p (a n) -> p a n", n=32), halves, ALU.mult)\
               .then_inc(*c.give("v_blocks"))
            yield

            def add_up(k):
                dve.wait_ge(*c.next("exped"))
                return dve.tensor_reduce(sums[:, :, k, :], probs[:, k % 2, :].rearrange("p (b j k) -> p b j k", b=BT, j=2),
                                         AX.X, ALU.add)

            for k in range(6):
                if k < 4:
                    dve.wait_ge(*c.next("scores"))
                    if k >= 2:
                        dve.wait_ge(*c.next("probsT"))
                    S = (SA, SB)[k % 2][:, :]
                    p = probs[:, k % 2, :]
                    p3 = p.rearrange("p (a k) -> p a k", k=SEQ)
                    if mask is None:
                        src = S
                    else:
                        m = mask
                        if len(m.shape) == 2:
                            m = m.unsqueeze(1).to_broadcast([P, 8, SEQ])
                            link(c, dve.tensor_tensor(p3, S.rearrange("p (a k) -> p a k", k=SEQ), m, ALU.min))
                        else:
                            m = m.unsqueeze(2).to_broadcast([P, BT, 2, SEQ])
                            link(c, dve.tensor_tensor(p.rearrange("p (b j k) -> p b j k", b=BT, j=2),
                                                      S.rearrange("p (b j k) -> p b j k", b=BT, j=2), m, ALU.min))
                        src = p
                    s3 = src.rearrange("p (a k) -> p a k", k=SEQ)
                    link(c, dve.tensor_reduce(mx[:, k % 2, :], s3, AX.X, ALU.max))
                    sh = dve.tensor_tensor(p3, s3, mx[:, k % 2, :].unsqueeze(2).to_broadcast([P, 8, SEQ]), ALU.subtract)
                    sh.then_inc(*c.give("shifted"))
                if 1 <= k < 5:
                    link(c, add_up(k - 1))
                if k == 4:
                    link(c, dve.reciprocal(rinv[:, :], sums[:, :, :, :].rearrange("p b g j -> p (b g j)")))
                if k == 5:
                    dve.wait_ge(*c.next("context"))
                    for h2 in range(2):
                        r = slice(64 * h2, 64 * h2 + 64)
                        o = dve.tensor_tensor(
                            onorm[r, :, :].rearrange("p b (a d) -> p (b a) d", d=DK),
                            OY[r, :].rearrange("p (a h d) -> p a h d", h=2, d=DK)[:, :, h2, :],
                            rinv[r, :].unsqueeze(2).to_broadcast([64, 32, DK]), ALU.mult)
                    o.then_inc(*c.give("context_normed"))
                yield
            c.skip("probsT", 2)
            yield
            if inner is None:
                dve.wait_ge(*c.next("gated"))
                dve.tensor_tensor(x, x, upd[:, :], ALU.add).then_inc(*c.give("x_new"))
            else:
                h, base, bias = inner
                dve.wait_ge(*c.next("projected_inner"))
                dve.scalar_tensor_tensor(out=h, in0=SA[:, 0:T], scalar=bias, in1=base, op0=ALU.add,
                                         op1=ALU.add).then_inc(*c.give("x_new"))
            yield

        def single_pe(c):
            pe = nc.tensor
            kT = qk[:, T:]
            pe.wait_ge(*c.next("normed"))
            pe.matmul(SA[:, 0:T], Wt("q1"), un[:, 0:T], start=True, stop=True).then_inc(*c.give("big_proj_q"))
            pe.matmul(SB[:, 0:T], Wt("k1"), ctxF, start=True, stop=True).then_inc(*c.give("big_proj_k"))
            yield
            pe.wait_ge(*c.next("big_q_heads"))
            pe.wait_ge(*c.next("big_k_taken"))
            for b in range(BT):
                t = slice(b * SEQ, (b + 1) * SEQ)
                r = slice(SEQ * (b % 2), SEQ * (b % 2) + SEQ)
                mm = pe.matmul(SA[r, SEQ * (b // 2):SEQ * (b // 2) + SEQ], q4[:, b, 0, :], kT[:, t],
                               start=True, stop=True, skip_group_check=True)
            mm.then_inc(*c.give("big_scores"))
            for b in range(BT):
                mm = pe.matmul(TP[0:SEQ, b * P:(b + 1) * P], kT[:, b * SEQ:(b + 1) * SEQ], Wt("v1"),
                               start=True, stop=True)
            mm.then_inc(*c.give("big_proj_v"))
            yield
            yield
            pe.wait_ge(*c.next("big_probs_normed"))
            for m in range(2):
                mm = pe.transpose(OY[0:SEQ, m * P:(m + 1) * P], probs[:, 0, m * SEQ:(m + 1) * SEQ], C("ident"))
            mm.then_inc(*c.give("big_probsT"))
            yield
            pe.wait_ge(*c.next("big_v_blocks"))
            pe.wait_ge(*c.next("big_probsT_taken"))
            for b in range(BT):
                mm = pe.matmul(SB[:, b * SEQ:(b + 1) * SEQ], vblk[0:SEQ, b, :],
                               probsT[0:SEQ, 0, b * SEQ:(b + 1) * SEQ], start=True, stop=True, skip_group_check=True)
            mm.then_inc(*c.give("big_context"))
            yield
            pe.wait_ge(*c.next("big_contextT_taken"))
            pe.matmul(SA[:, 0:T], Wt("o1"), qkr[:, 0:T], start=True, stop=True).then_inc(*c.give("projected"))
            yield

        def single_act(c):
            a = nc.scalar
            a.wait_ge(*c.next("big_proj_q"))
            a.activation(q4[:, :, 0, :], SA[:, 0:T].rearrange("p (b q) -> p b q", b=BT), ACT.Identity, bias=V("bq1")).then_inc(*c.give("big_q_heads"))
            yield
            a.wait_ge(*c.next("big_proj_v"))
            a.activation(vblk[0:SEQ, :, :].rearrange("p b n -> p (b n)"), TP[0:SEQ, :], ACT.Copy)\
             .then_inc(*c.give("big_v_blocks"))
            a.wait_ge(*c.next("big_shifted"))
            a.activation(probs[:, 0, 0:P], probs[:, 0, 0:P], ACT.Exp).then_inc(*c.give("big_exped"))
            yield
            yield
            a.wait_ge(*c.next("big_probsT"))
            a.activation(probsT[0:SEQ, 0, 0:T], OY[0:SEQ, 0:T], ACT.Copy).then_inc(*c.give("big_probsT_taken"))
            yield
            a.wait_ge(*c.next("big_context"))
            a.activation(qkr[:, 0:T], SB[:, 0:T], ACT.Copy).then_inc(*c.give("big_contextT_taken"))
            yield
            a.wait_ge(*c.next("projected"))
            a.activation(upd[:, :], SA[:, 0:T], ACT.Identity, scale=tg[:, 1:2], bias=bog[:, 1:2])\
             .then_inc(*c.give("gated"))
            yield

        def single_dve(c):
            dve = nc.vector
            s = probs[:, 0, 0:P]
            s2 = s.rearrange("p (m k) -> p m k", m=2)
            dve.wait_ge(*c.next("big_proj_k"))
            dve.tensor_scalar(qk[:, T:], SB[:, 0:T], V("bk1"), None, ALU.add).then_inc(*c.give("big_k_taken"))
            yield
            dve.wait_ge(*c.next("big_scores"))
            link(c, dve.tensor_tensor(s, SA[:, 0:P], mask1[:, 0, :], ALU.mult))
            link(c, dve.tensor_tensor(s, s, mask1[:, 1, :], ALU.add))
            link(c, dve.tensor_reduce(mx[:, 0, 0:2], s2, AX.X, ALU.max))
            dve.tensor_tensor(s2, s2, mx[:, 0, 0:2].unsqueeze(2).to_broadcast([P, 2, SEQ]), ALU.subtract)\
               .then_inc(*c.give("big_shifted"))
            yield
            dve.wait_ge(*c.next("big_exped"))
            link(c, dve.tensor_reduce(mx[:, 1, 0:2], s2, AX.X, ALU.add))
            link(c, dve.reciprocal(mx[:, 1, 0:2], mx[:, 1, 0:2]))
            dve.tensor_tensor(s2, s2, mx[:, 1, 0:2].unsqueeze(2).to_broadcast([P, 2, SEQ]), ALU.mult)\
               .then_inc(*c.give("big_probs_normed"))
            yield
            yield
            yield
            dve.wait_ge(*c.next("gated"))
            dve.tensor_tensor(xF, xF, upd[:, :], ALU.add).then_inc(*c.give("x_new"))
            yield

        def ff0_pe(c):
            nc.tensor.wait_ge(*c.next("normed"))
            nc.tensor.matmul(SA[:, 0:T], ff0[:, :], un[:, 0:T], start=True, stop=True).then_inc(*c.give("ff_hidden"))
            yield

        def ff0_act(c):
            nc.scalar.wait_ge(*c.next("ff_hidden"))
            nc.scalar.activation(upd[:, :], SA[:, 0:T], ACT.Tanh, bias=V("bf0")).then_inc(*c.give("ff_hidden_tanh"))
            yield

        def ff0_dve(c):
            nc.vector.wait_ge(*c.next("ff_hidden_tanh"))
            nc.vector.scalar_tensor_tensor(out=xF, in0=upd[:, :], scalar=tg[:, 4:5], in1=xF, op0=ALU.mult,
                                           op1=ALU.add).then_inc(*c.give("x_new"))
            yield

        def by_chunk(S):
            return S[:, :].rearrange("p (c b q) -> p b c q", c=2, b=BT)

        def wide_pe(c):
            pe = nc.tensor
            kT, cn = qk[:, T:], un[:, T:]
            pe.wait_ge(*c.next("normed"))
            pe.matmul(OY[:, 0:T], Wt("kx"), cn, start=True, stop=True).then_inc(*c.give("big_proj_k"))
            g, a, z = wplace["vx"]
            for b in range(BT):
                for half in (0, SEQ):
                    mm = pe.matmul(TP[half:half + SEQ, b * 64:(b + 1) * 64], cn[:, b * SEQ:(b + 1) * SEQ],
                                   wsb[g][:, a:z], start=True, stop=True, skip_group_check=True)
            mm.then_inc(*c.give("big_proj_v"))

            def queries(p):
                for i in range(2):
                    mm = pe.matmul((SA, SB)[p % 2][:, i * T:(i + 1) * T], Wt("qx", 2 * p + i), xn[:, :],
                                   start=True, stop=True)
                mm.then_inc(*c.give("big_proj_q"))

            queries(0)
            queries(1)
            yield
            pe.wait_ge(*c.next("big_q_heads"))
            queries(2)
            pe.wait_ge(*c.next("big_q_heads_dve"))
            queries(3)
            yield

            def scores(u):
                j, mp = u // 2, u % 2
                r = slice(64 * j, 64 * j + 64)
                if u == 0:
                    pe.wait_ge(*c.next("big_k_taken"))
                    pe.wait_ge(*c.next("big_q_heads"))
                    pe.wait_ge(*c.next("big_q_heads_dve"))
                if u >= 2:
                    pe.wait_ge(*c.next("big_shifted"))
                for b in range(BT):
                    for m2 in range(2):
                        at = (2 * b + m2) * SEQ
                        mm = pe.matmul((SA, SB)[u % 2][:, at:at + SEQ], qx[r, 2 * mp + m2, b, :, :].rearrange("p c q -> p (c q)"),
                                       kT[r, b * SEQ:(b + 1) * SEQ], start=True, stop=True, skip_group_check=True)
                mm.then_inc(*c.give("big_scores"))

            def transposes(u):
                pe.wait_ge(*c.next("big_probs_normed"))
                if u == 0:
                    pe.wait_ge(*c.next("big_v_blocks"))
                else:
                    pe.wait_ge(*c.next("big_probsT_taken"))
                for b in range(BT):
                    mm = pe.transpose(TP[:, b * P:(b + 1) * P], probs[:, u % 2, b * P:(b + 1) * P], C("ident"))
                mm.then_inc(*c.give("big_probsT"))

            def weigh(u):
                if u == 3:
                    pe.wait_ge(*c.next("big_probsT_taken"))
                if u >= 1:
                    pe.wait_ge(*c.next("big_contextT_taken"))
                for b in range(BT):
                    mm = pe.matmul(OY[:, b * P:(b + 1) * P], vdiag[:, b, :], probsT[:, u % 2, b * P:(b + 1) * P],
                                   start=True, stop=True)
                mm.then_inc(*c.give("big_context"))

            for k in range(7):
                if k < 4:
                    scores(k)
                if 2 <= k < 6:
                    transposes(k - 2)
                if k >= 3:
                    weigh(k - 3)
                yield
            for ch in range(4):
                if ch >= 2:
                    pe.wait_ge(*c.next("big_hidden_done"))
                S = (SA, SB)[ch % 2]
                pe.matmul(S[:, 0:T], Wt("ffx", 2 * ch), xn[:, :], start=True, stop=True)
                pe.matmul(S[:, T:], Wt("ffx", 2 * ch + 1), xn[:, :], start=True, stop=True)\
                  .then_inc(*c.give("big_hidden"))
                yield
            pe.wait_ge(*c.next("big_contextT_taken"))
            for u in range(4):
                for c2 in range(2):
                    rhs = otx[:, u, :].rearrange("p (b c q) -> p b c q", b=BT, c=2)[:, :, c2, :]
                    pe.matmul(TP[:, 0:T], Wt("ox", 2 * u + c2), rhs, start=(u + c2 == 0), stop=False)
            for ch in range(4):
                if ch >= 2:
                    pe.wait_ge(*c.next("big_hidden_done"))
                mm = pe.matmul(TP[:, 0:T], Wt("ff2x", ch), fact[:, ch, :], start=False, stop=(ch == 3))
            mm.then_inc(*c.give("projected"))
            yield

        def wide_act(c):
            a = nc.scalar
            a.wait_ge(*c.next("big_proj_k"))
            a.activation(qk[:, T:], OY[:, 0:T], ACT.Copy).then_inc(*c.give("big_k_taken"))
            a.wait_ge(*c.next("big_proj_q"))
            a.activation(qx[:, 0, :, :, :], by_chunk(SA), ACT.Copy, scale=0.125)\
             .then_inc(*c.give("big_q_heads"))
            c.next("big_proj_q")
            yield
            a.wait_ge(*c.next("big_proj_q"))
            a.activation(qx[:, 2, :, :, :], by_chunk(SA), ACT.Copy, scale=0.125)\
             .then_inc(*c.give("big_q_heads"))
            c.next("big_proj_q")
            yield
            for k in range(7):
                if 2 <= k < 6:
                    a.wait_ge(*c.next("big_probsT"))
                    a.activation(probsT[:, k % 2, :], TP[:, :], ACT.Copy).then_inc(*c.give("big_probsT_taken"))
                if k >= 3:
                    a.wait_ge(*c.next("big_context"))
                    a.activation(otx[:, k - 3, :], OY[:, :], ACT.Copy).then_inc(*c.give("big_contextT_taken"))
                if k < 4:
                    a.wait_ge(*c.next("big_shifted"))
                    a.activation(probs[:, k % 2, :], probs[:, k % 2, :], ACT.Exp).then_inc(*c.give("big_exped"))
                yield
            for ch in range(4):
                a.wait_ge(*c.next("big_hidden"))
                a.activation(fx[:, ch % 2, :], (SA, SB)[ch % 2][:, T:], ACT.Tanh, scale=0.5)\
                 .then_inc(*c.give("big_hidden_tanh"))
                yield
            a.wait_ge(*c.next("projected"))
            a.activation(upd[:, :], TP[:, 0:T], ACT.Copy, scale=tg[:, 2:3]).then_inc(*c.give("gated"))
            yield

        def wide_dve(c):
            dve = nc.vector
            dve.wait_ge(*c.next("big_proj_v"))
            for h in range(2):
                r = slice(64 * h, 64 * h + 64)
                v = dve.tensor_copy(vdiag[r, :, 64 * h:64 * h + 64], TP[r, 0:T].rearrange("p (b d) -> p b d", b=BT))
            v.then_inc(*c.give("big_v_blocks"))
            for p in (1, 3):
                c.next("big_proj_q")
                dve.wait_ge(*c.next("big_proj_q"))
                dve.tensor_scalar(qx[:, p, :, :, :], by_chunk(SB), 0.125, None,
                                  ALU.mult).then_inc(*c.give("big_q_heads_dve"))
                yield
            for k in range(7):
                if 1 <= k < 5:
                    p3 = probs[:, (k - 1) % 2, :].rearrange("p (a k) -> p a k", k=SEQ)
                    s8 = mx[:, (k - 1) % 2, :]
                    dve.wait_ge(*c.next("big_exped"))
                    link(c, dve.tensor_reduce(s8, p3, AX.X, ALU.add))
                    link(c, dve.reciprocal(s8, s8))
                    dve.tensor_tensor(p3, p3, s8.unsqueeze(2).to_broadcast([P, 8, SEQ]), ALU.mult)\
                       .then_inc(*c.give("big_probs_normed"))
                if k < 4:
                    p = probs[:, k % 2, :]
                    p3 = p.rearrange("p (a k) -> p a k", k=SEQ)
                    p4 = p.rearrange("p (b m k) -> p b m k", b=BT, m=2)
                    dve.wait_ge(*c.next("big_scores"))
                    if k >= 2:
                        dve.wait_ge(*c.next("big_probsT"))
                    mk = addmask.rearrange("p (b k) -> p b k", b=BT).unsqueeze(2).to_broadcast([P, BT, 2, SEQ])
                    link(c, dve.tensor_tensor(p4, (SA, SB)[k % 2][:, :].rearrange("p (b m k) -> p b m k", b=BT, m=2),
                                              mk, ALU.add))
                    link(c, dve.tensor_reduce(mx[:, k % 2, :], p3, AX.X, ALU.max))
                    dve.tensor_tensor(p3, p3, mx[:, k % 2, :].unsqueeze(2).to_broadcast([P, 8, SEQ]), ALU.subtract)\
                       .then_inc(*c.give("big_shifted"))
                yield
            for ch in range(4):
                S = (SA, SB)[ch % 2]
                dve.wait_ge(*c.next("big_hidden_tanh"))
                link(c, dve.scalar_tensor_tensor(out=fx[:, ch % 2, :], in0=fx[:, ch % 2, :], scalar=1.0, in1=S[:, T:],
                                                 op0=ALU.add, op1=ALU.mult))
                dve.scalar_tensor_tensor(out=fact[:, ch, :], in0=fx[:, ch % 2, :], scalar=0.5, in1=S[:, 0:T],
                                         op0=ALU.mult, op1=ALU.mult).then_inc(*c.give("big_hidden_done"))
                yield
            dve.wait_ge(*c.next("gated"))
            dve.tensor_tensor(xF, xF, upd[:, :], ALU.add).then_inc(*c.give("x_new"))
            yield

        def route_pe(c, src, kind, gate, nearest=False):
            pe = nc.tensor
            yield from norm_pe(c, MNORM, kind, src)
            pe.wait_ge(*c.next("m_normed"))
            if nearest:
                pe.wait_ge(*c.next("m_rowsq"))
            for s in range(2):
                o = H1[:, s * NE:(s + 1) * NE]
                t = slice(s * P, (s + 1) * P)
                mm = pe.matmul(o, my[:, t], gate, start=True, stop=not nearest)
                if nearest:
                    pe.matmul(o, msq[:, t], negones[:, :], start=False, stop=False)
                    mm = pe.matmul(o, C("mean"), centsq[:, :], start=False, stop=True)
            mm.then_inc(*c.give("m_logits"))
            yield
            yield
            pe.wait_ge(*c.next("m_comb"))
            for s in range(2):
                mm = pe.transpose(H0[0:NE, s * P:(s + 1) * P], comb[:, s, :], C("ident"))
            mm.then_inc(*c.give("m_combT"))
            yield

        def route_act(c, src, kind, nearest=False):
            a = nc.scalar
            yield from norm_act(c, MNORM, kind, src)
            if nearest:
                a.wait_ge(*c.next("m_normed"))
                a.activation(msq[:, :], my[:, :], ACT.Square).then_inc(*c.give("m_rowsq"))
            yield
            if not nearest:
                a.wait_ge(*c.next("m_gap"))
                a.activation(gapx[:, :], gap[:, :], ACT.Exp).then_inc(*c.give("m_gap_exp"))
            yield
            a.wait_ge(*c.next("m_combT"))
            a.activation(combT[:, :], H0[0:NE, 0:T], ACT.Copy, scale=0.5).then_inc(*c.give("m_combT_taken"))
            yield

        def route_pool(c, kind):
            yield from norm_pool(c, MNORM, kind)
            yield from idle(3)

        def route_dve(c, src, kind, g, b=None, nearest=False):
            dve = nc.vector
            lk = lambda ins: link(c, ins, "m_chain")
            yield from norm_dve(c, MNORM, kind, src, y=my[:, :], g=g, b=b, eps2=1e-6)
            dve.wait_ge(*c.next("m_logits"))
            lk(dve.tensor_copy(lg[:, :, :].rearrange("p s e -> p (s e)"), H1[:, 0:2 * NE]))
            dve.max(top[:, 0, :], lg[:, 0, :])
            lk(dve.max(top[:, 1, :], lg[:, 1, :]))
            if not nearest:
                dve.tensor_tensor(gap[:, :], top[:, :, 1], top[:, :, 0], ALU.subtract).then_inc(*c.give("m_gap"))
            dve.max_index(topi[:, 0, :], top[:, 0, :], lg[:, 0, :])
            lk(dve.max_index(topi[:, 1, :], top[:, 1, :], lg[:, 1, :]))
            lk(dve.tensor_copy(topf[:, :, :], topi[:, :, :]))
            yield
            iota = C("iota8").unsqueeze(1).to_broadcast([P, 2, NE])
            if nearest:
                dve.tensor_tensor(comb[:, :, :], iota, topf[:, :, 0:1].to_broadcast([P, 2, NE]), ALU.is_equal)\
                   .then_inc(*c.give("m_comb"))
                yield
                yield
                return
            dve.wait_ge(*c.next("m_gap_exp"))
            lk(dve.tensor_scalar(w01[:, 0, :], gapx[:, :], 1.0, None, ALU.add))
            lk(dve.reciprocal(w01[:, 0, :], w01[:, 0, :]))
            dve.tensor_tensor(w01[:, 1, :], gapx[:, :], w01[:, 0, :], ALU.mult)
            for i in range(2):
                last = dve.tensor_tensor(pick[:, i, :, :], iota, topf[:, :, i:i + 1].to_broadcast([P, 2, NE]), ALU.is_equal)
            lk(last)
            for i in range(2):
                last = dve.tensor_tensor(pick[:, i, :, :], pick[:, i, :, :],
                                         w01[:, i, :].unsqueeze(2).to_broadcast([P, 2, NE]), ALU.mult)
            lk(last)
            dve.tensor_tensor(comb[:, :, :], pick[:, 0, :, :], pick[:, 1, :, :], ALU.add).then_inc(*c.give("m_comb"))
            yield
            yield

        def row(e):
            return C("ident")[0:NE, e:e + 1].to_broadcast([NE, P])

        N1 = NE * 2

        def gelu_pe(c):
            pe = nc.tensor
            for n in range(N1 + 2):
                if n == 0:
                    pe.wait_ge(*c.next("m_combT_taken"))
                    pe.matmul(YM[:, 0:T], b2x2[:, :], combT[:, :], start=True, stop=False)
                if n < N1:
                    if n % 2 == 0:
                        if n:
                            pe.wait_ge(*c.next("m_weight_taken"))
                        pe.matmul(WB[:, 0:T], row(n // 2), combT[:, :], start=True, stop=True)\
                          .then_inc(*c.give("m_weight"))
                    if n >= 2:
                        pe.wait_ge(*c.next("m_up_free"))
                    for i in range(2):
                        mm = pe.matmul(H[n % 2][:, i * T:(i + 1) * T], Wt("up1", 2 * n + i), my[:, :],
                                       start=True, stop=True)
                    mm.then_inc(*c.give("m_up"))
                if n >= 2:
                    pe.wait_ge(*c.next("m_act"))
                    for i in range(2):
                        mm = pe.matmul(YM[:, 0:T], Wt("dn1", 2 * (n - 2) + i), act[:, (n - 2) % 3, i * T:(i + 1) * T],
                                       start=False, stop=(n == N1 + 1 and i == 1))
                    mm.then_inc(*c.give("m_down"))
                yield
            yield

        def gelu_act(c):
            a = nc.scalar
            for n in range(N1 + 2):
                if 1 <= n <= N1:
                    a.wait_ge(*c.next("m_cubic"))
                    a.activation(hp[:, (n - 1) % 2, :], hp[:, (n - 1) % 2, :], ACT.Tanh, scale=GELU_C)\
                     .then_inc(*c.give("m_tanh"))
                if n < N1:
                    if n % 2 == 0:
                        a.wait_ge(*c.next("m_weight"))
                        a.activation(wexp[:, n // 2 % 2, :], WB[:, 0:T], ACT.Copy).then_inc(*c.give("m_weight_taken"))
                    a.wait_ge(*c.next("m_up"))
                    for i in range(2):
                        h = a.activation(hb[:, n % 3, i * T:(i + 1) * T], H[n % 2][:, i * T:(i + 1) * T], ACT.Identity,
                                         bias=V("b1", 2 * n + i))
                    h.then_inc(*c.give("m_up_free"))
                    a.wait_ge(*c.next("m_up_free"))
                    a.activation(hp[:, n % 2, :], hb[:, n % 3, :], ACT.Square).then_inc(*c.give("m_square"))
                yield
            yield

        def gelu_pool(c):
            for n in range(N1 + 2):
                if n < N1:
                    nc.gpsimd.wait_ge(*c.next("m_square"))
                    nc.gpsimd.tensor_scalar(hp[:, n % 2, :], hp[:, n % 2, :], 0.044715, 1.0, ALU.mult, ALU.add)\
                             .then_inc(*c.give("m_poly"))
                yield
            yield

        def gelu_dve(c):
            dve = nc.vector
            for n in range(N1 + 2):
                if 1 <= n <= N1:
                    m = n - 1
                    dve.wait_ge(*c.next("m_tanh"))
                    link(c, dve.scalar_tensor_tensor(out=hp[:, m % 2, :], in0=hp[:, m % 2, :], scalar=1.0,
                                                     in1=hb[:, m % 3, :], op0=ALU.add, op1=ALU.mult), "m_chain")
                    if m % 2 == 0:
                        dve.wait_ge(*c.next("m_weight_taken"))
                    if m >= 3:
                        dve.wait_ge(*c.next("m_down"))
                    dve.tensor_tensor(act[:, m % 3, :].rearrange("p (i t) -> p i t", i=2),
                                      hp[:, m % 2, :].rearrange("p (i t) -> p i t", i=2),
                                      wexp[:, m // 2 % 2, :].unsqueeze(1).to_broadcast([P, 2, T]), ALU.mult)\
                       .then_inc(*c.give("m_act"))
                if n < N1:
                    dve.wait_ge(*c.next("m_poly"))
                    dve.tensor_tensor(hp[:, n % 2, :], hp[:, n % 2, :], hb[:, n % 3, :], ALU.mult)\
                       .then_inc(*c.give("m_cubic"))
                yield
            finish_dve(c, N1, hF[:, :], 5, xF)
            yield

        def finish_dve(c, steps, skip, gate, x):
            dve = nc.vector
            have = c.seen.get("m_down", 0)
            for _ in range(steps - have):
                last = c.next("m_down")
            dve.wait_ge(*last)
            link(c, dve.tensor_tensor(msq[:, :], YM[:, 0:T], skip, ALU.add), "m_chain")
            dve.scalar_tensor_tensor(out=x, in0=msq[:, :], scalar=tg[:, gate:gate + 1], in1=x, op0=ALU.mult,
                                     op1=ALU.add).then_inc(*c.give("m_out"))

        def glu_pe(c, up, down, chunks):
            pe = nc.tensor
            N = NE * chunks

            def weight(e):
                pe.matmul(WB[:, 0:T], row(e), combT[:, :], start=True, stop=True)\
                  .then_inc(*c.give("m_weight"))

            for n in range(N + 2):
                e, ch = divmod(n, chunks)
                if n == 0:
                    pe.wait_ge(*c.next("m_combT_taken"))
                    weight(0)
                if n >= 2:
                    pe.wait_ge(*c.next("m_act"))
                if n < N:
                    S = H[n % 2]
                    pe.matmul(S[:, 0:T], Wt(up, 2 * n), my[:, :], start=True, stop=True)
                    if ch == 0:
                        pe.wait_ge(*c.next("m_weight_taken"))
                    pe.matmul(S[:, T:], Wt(up, 2 * n + 1), wexp[:, e % 2, :], start=True, stop=True)\
                      .then_inc(*c.give("m_up"))
                    if ch == 0 and e + 1 < NE:
                        weight(e + 1)
                if n >= 2:
                    pe.matmul(YM[:, 0:T], Wt(down, n - 2), act[:, (n - 2) % 3, 0:T], start=(n == 2), stop=(n == N + 1))\
                      .then_inc(*c.give("m_down"))
                yield
            yield

        def glu_act(c, chunks):
            for n in range(NE * chunks + 2):
                if n < NE * chunks:
                    nc.scalar.wait_ge(*c.next("m_up"))
                    nc.scalar.activation(hp[:, n % 2, 0:T], H[n % 2][:, 0:T], ACT.Tanh, scale=0.5)\
                             .then_inc(*c.give("m_tanh"))
                yield
            yield

        def glu_dve(c, chunks, skip, gate):
            dve = nc.vector
            N = NE * chunks

            def weigh_input(e):
                dve.wait_ge(*c.next("m_weight"))
                dve.tensor_tensor(wexp[:, e % 2, :], WB[:, 0:T], my[:, :], ALU.mult).then_inc(*c.give("m_weight_taken"))

            for n in range(N + 2):
                e, ch = divmod(n, chunks)
                if n == 0:
                    weigh_input(0)
                if n < N:
                    S = H[n % 2]
                    dve.wait_ge(*c.next("m_tanh"))
                    link(c, dve.scalar_tensor_tensor(out=hb[:, n % 2, 0:T], in0=hp[:, n % 2, 0:T], scalar=1.0,
                                                     in1=S[:, 0:T], op0=ALU.add, op1=ALU.mult), "m_chain")
                    dve.tensor_tensor(act[:, n % 3, 0:T], S[:, T:], hb[:, n % 2, 0:T], ALU.mult)\
                       .then_inc(*c.give("m_act"))
                    if ch == 0 and e + 1 < NE:
                        weigh_input(e + 1)
                yield
            finish_dve(c, N, skip, gate, xS[:, :])
            yield

        def idle(slots):
            for _ in range(slots):
                yield

        LAYER, BOTH = 3, 4
        ROUTE, HEADS, SINGLE, FF0, WIDE = 3, 9, 6, 1, 14
        wo = lambda name: (lambda h2: Wt(name, h2, 1, 64))
        bq = lambda l: (lambda i: bq4[:, l, i:i + 1])
        causal = C("causal")

        def f1_pe(c):
            yield from norm_pe(c, ANORM, "layer", xF)
            yield from heads_pe(c, Wt("q0"), Wt("k0"), Wt("v0"), wo("o0"), un[:, 0:T], ctxF)
            yield from norm_pe(c, ANORM, "layer", xF, fresh=True)
            yield from ff0_pe(c)
            yield from norm_pe(c, ANORM, "layer", xF, fresh=True)
            yield from single_pe(c)
            yield from norm_pe(c, ANORM, "both", xF, fresh=True)
            yield from heads_pe(c, Wt("qa"), Wt("ka"), Wt("va"), wo("oa"), xn[:, :], xn[:, :], inner=True)

        def f1_act(c):
            yield from norm_act(c, ANORM, "layer")
            yield from heads_act(c, bq(0), gate=(tg[:, 0:1], bog[:, 0:1]))
            yield from norm_act(c, ANORM, "layer")
            yield from ff0_act(c)
            yield from norm_act(c, ANORM, "layer")
            yield from single_act(c)
            yield from norm_act(c, ANORM, "both")
            yield from heads_act(c, bq(1))

        def f1_dve(c):
            yield from norm_dve(c, ANORM, "layer")
            yield from heads_dve(c, V("bk0"), maskA[:, :, :], xF)
            yield from norm_dve(c, ANORM, "layer")
            yield from ff0_dve(c)
            yield from norm_dve(c, ANORM, "layer")
            yield from single_dve(c)
            yield from norm_dve(c, ANORM, "both", y=xn[:, :], g=V("ln1w"), b=V("ln1b"), eps2=1e-5)
            yield from heads_dve(c, V("bka"), None, None, inner=(hF[:, :], un[:, 0:T], bo[:, 2:3]))

        def s1_pe(c):
            yield from route_pe(c, hS[:, :], "rms", V("router2", 0, NE))
            yield from glu_pe(c, "up2", "dn2", 3)

        def s1_act(c):
            yield from route_act(c, hS[:, :], "rms")
            yield from glu_act(c, 3)

        def s1_dve(c):
            yield from route_dve(c, hS[:, :], "rms", V("g2"))
            yield from glu_dve(c, 3, hS[:, :], 6)

        def s2_pe(c):
            yield from norm_pe(c, ANORM, "layer", xS[:, :])
            yield from heads_pe(c, Wt("q3"), Wt("k3"), Wt("v3"), wo("o3"), un[:, 0:T], ctxS[:, :])

        def s2_act(c):
            yield from norm_act(c, ANORM, "layer")
            yield from heads_act(c, bq(2), gate=(tg[:, 3:4], bog[:, 3:4]))

        def s2_dve(c):
            link(c, nc.vector.tensor_tensor(maskA[:, :, :], causal.unsqueeze(1).to_broadcast([P, BT, SEQ]),
                                            rowS[:, :].unsqueeze(2).to_broadcast([P, BT, SEQ]), ALU.min))
            yield from norm_dve(c, ANORM, "layer")
            yield from heads_dve(c, V("bk3"), maskA[:, :, :], xS[:, :])

        def f2_pe(c):
            yield from route_pe(c, hF[:, :], "layer", V("gate1", 0, NE))
            yield from gelu_pe(c)

        def f2_act(c):
            yield from route_act(c, hF[:, :], "layer")
            yield from gelu_act(c)

        def f2_pool(c):
            yield from route_pool(c, "layer")
            yield from gelu_pool(c)

        def f2_dve(c):
            yield from route_dve(c, hF[:, :], "layer", V("ln2w"), V("ln2b"))
            yield from gelu_dve(c)

        def f3_pe(c):
            yield from norm_pe(c, ANORM, "both", xF, second=ctxF)
            yield from wide_pe(c)
            yield from norm_pe(c, ANORM, "both", xF, fresh=True)
            yield from heads_pe(c, Wt("q2"), Wt("k2"), Wt("v2"), wo("o2"), xn[:, :], xn[:, :],
                                rope=(Wt("qr2"), Wt("kr2")), inner=True)

        def f3_act(c):
            yield from norm_act(c, ANORM, "both", w=W2T)
            yield from wide_act(c)
            yield from norm_act(c, ANORM, "both")
            yield from heads_act(c, None, rope=True)

        def f3_dve(c):
            yield from norm_dve(c, ANORM, "both", y=xn[:, :], g=V("lng"), b=V("lnb"), eps2=1e-5, w=W2T,
                                ctx_gb=(V("clng"), V("clnb")))
            yield from wide_dve(c)
            yield from norm_dve(c, ANORM, "both", y=xn[:, :], g=V("g1"), eps2=1e-6)
            yield from heads_dve(c, None, causal, None, inner=(hF[:, :], un[:, 0:T], 0.0), rope=True)

        def s3_pe(c):
            yield from route_pe(c, xS[:, :], "both", cent2[:, :], nearest=True)
            yield from glu_pe(c, "up3", "dn3", 2)

        def s3_act(c):
            yield from route_act(c, xS[:, :], "both", nearest=True)
            yield from glu_act(c, 2)

        def s3_dve(c):
            yield from route_dve(c, xS[:, :], "both", V("scale3"), nearest=True)
            yield from glu_dve(c, 2, mu[:, :], 7)

        def f1_pool(c):
            yield from norm_pool(c, ANORM, "layer")
            yield from idle(HEADS)
            yield from norm_pool(c, ANORM, "layer")
            yield from idle(FF0)
            yield from norm_pool(c, ANORM, "layer")
            yield from idle(SINGLE)
            yield from norm_pool(c, ANORM, "both")
            yield from idle(HEADS)

        def s1_pool(c):
            yield from route_pool(c, "rms")
            yield from idle(NE * 3 + 3)

        def s2_pool(c):
            yield from norm_pool(c, ANORM, "layer")
            yield from idle(HEADS)

        def f3_pool(c):
            yield from norm_pool(c, ANORM, "both", W2T)
            yield from idle(WIDE)
            yield from norm_pool(c, ANORM, "both")
            yield from idle(HEADS)

        def s3_pool(c):
            yield from route_pool(c, "both")
            yield from idle(NE * 2 + 3)

        A1, A2, A3 = 3 * LAYER + BOTH + 2 * HEADS + FF0 + SINGLE, LAYER + HEADS, 2 * BOTH + WIDE + HEADS
        M1, M2, M3 = LAYER + ROUTE + NE * 3 + 3, LAYER + ROUTE + N1 + 3, BOTH + ROUTE + NE * 2 + 3
        phases = [
            ((A1, f1_pe, f1_act, f1_dve, f1_pool), (M1, s1_pe, s1_act, s1_dve, s1_pool), "F"),
            ((A2, s2_pe, s2_act, s2_dve, s2_pool), (M2, f2_pe, f2_act, f2_dve, f2_pool), "S"),
            ((A3, f3_pe, f3_act, f3_dve, f3_pool), (M3, s3_pe, s3_act, s3_dve, s3_pool), "F"),
        ]

        def clear_resting(parity):
            nums = sorted(s.num for s in sets[1 - parity].values())
            assert nums == list(range(nums[0], nums[0] + len(nums)))
            nc.gpsimd.sem_clear(range(nums[0], nums[-1] + 1))

        def handoff(parity, first, second, load=None):
            sems = sets[parity]
            with nc.Block() as block:
                @block.gpsimd
                def _(pool):
                    clear_resting(parity)
                    if second:
                        nc.gpsimd.tensor_copy(ctxS[:, :], ctxF).then_inc(sems["x_new"], 1)
                        pool.wait_ge(sems["x_new"], 1)
                    if first:
                        if second:
                            pool.wait_ge(sems["normed"], 1)
                        nc.gpsimd.tensor_copy(tile_f[:, :], stage_f[:, :])

                @block.vector
                def _(dve):
                    c = Counts(sems)
                    if second:
                        dve.tensor_copy(xS[:, :], xF).then_inc(sems["normed"], 1)
                        dve.tensor_copy(hS[:, :], hF[:, :])
                        link(c, dve.tensor_copy(rowS[:, :], rowF[:, :]))
                    if first:
                        flat = maskA[:, :, :].rearrange("p b k -> p (b k)")
                        dve.tensor_scalar(flat, stage_i[:, IM0:IM0 + T], 0.0, 0.5, ALU.is_equal, ALU.subtract)
                        dve.tensor_scalar(mask1[:, 0, :], stage_i[:, IM1:IM1 + P], 0.0, None, ALU.not_equal)
                        dve.tensor_scalar(mask1[:, 1, :], stage_i[:, IM1:IM1 + P], 0.0, -10000.0, ALU.is_equal, ALU.mult)
                        link(c, dve.tensor_scalar(rowF[:, :], stage_i[:, IM3:IM3 + BT], 0.0, 0.5, ALU.is_equal,
                                                  ALU.subtract))
                        dve.tensor_scalar(flat, flat, -2e9, None, ALU.mult)
                        dve.tensor_scalar(rowF[:, :], rowF[:, :], -2e9, None, ALU.mult)

        def phase(parity, which, first, second, load_at=None, store_at=None, need_weights=()):
            attn, moe, attn_half = phases[which]
            if not (first if attn_half == "F" else second):
                attn = (0, None, None, None, None)
            if not (second if attn_half == "F" else first):
                moe = (0, None, None, None, None)
            order = take_turns(attn[0], moe[0])
            sems = sets[parity]

            def run(engine):
                c = [Counts(sems), Counts(sems)]
                gens = []
                for k, half in enumerate((attn, moe)):
                    gen = half[engine]
                    gens.append(gen(c[k]) if gen else (idle(half[0]) if half[0] else None))
                side_by_side(gens[0], gens[1], order)

            with nc.Block() as block:
                @block.tensor
                def _(pe):
                    for g in need_weights:
                        pe.wait_ge(dma_w[g], 16)
                    run(1)

                @block.scalar
                def _(a):
                    run(2)

                @block.vector
                def _(dve):
                    run(3)

                @block.gpsimd
                def _(pool):
                    clear_resting(parity)
                    run(4)

                @block.sync
                def _(sp):
                    if load_at is not None:
                        sp.dma_start(stage_f[:, :], fin[:, bass.ds(load_at * FCOLS, FCOLS)]).then_inc(sems["tile_in"], 16)
                        sp.dma_start(stage_i[:, :], iin[:, bass.ds(load_at * ICOLS, ICOLS)]).then_inc(sems["tile_in"], 16)
                        sp.wait_ge(sems["tile_in"], 32)
                    if store_at is not None:
                        sp.wait_ge(sems["m_out"], 1)
                        sp.dma_start(out[:, bass.ds(store_at * T, T)], xS[:, :]).then_inc(sems["out_store"], 16)
                        sp.wait_ge(sems["out_store"], 16)

        def setup():
            with nc.Block() as block:
                @block.sync
                def _(sp):
                    sp.dma_start(vsb[:, :], vecs).then_inc(dma_vec, 16)
                    sp.dma_start(wsb["early"][:, :], weights["early"]).then_inc(dma_w["early"], 16)
                    sp.dma_start(csb[:, :], consts).then_inc(dma_const, 16)
                    sp.dma_start(stage_f[:, :], fin[:, 0:FCOLS]).then_inc(dma_first, 16)
                    sp.dma_start(stage_i[:, :], iin[:, 0:ICOLS]).then_inc(dma_first, 16)
                    sp.dma_start(wsb["ff0"], weights["ff0"]).then_inc(dma_w["ff0"], 16)
                    for g, _ in W_PARTS[2:]:
                        sp.dma_start(wsb[g][:, :], weights[g]).then_inc(dma_w[g], 16)
                    sp.wait_ge(dma_const, 16)
                    sp.wait_ge(dma_first, 32)

                @block.scalar
                def _(a):
                    a.wait_ge(dma_vec, 16)
                    a.activation(tg[:, :], V("gx", 0, 8), ACT.Tanh).then_inc(setup_tanh, 1)
                    a.wait_ge(setup_pe, 2)
                    a.activation(a12, SA[:, 0:P], ACT.Copy).then_inc(setup_act, 1)
                    a.wait_ge(setup_pe, 3)
                    a.activation(ff0[:, :], SB[:, 0:P], ACT.Copy)

                @block.tensor
                def _(pe):
                    pe.wait_ge(dma_vec, 16)
                    pe.wait_ge(dma_w["early"], 16)
                    pe.wait_ge(dma_w["ff0"], 16)
                    for l, (w, b) in enumerate((("o0", "bv0"), ("o1", "bv1"), ("oa", "bva"))):
                        if w == "o1":
                            mm = pe.matmul(OY[:, l:l + 1], Wt(w), V(b), start=True, stop=True)
                            continue
                        for h2 in range(2):
                            mm = pe.matmul(OY[:, l:l + 1], Wt(w, h2, 1, 64), V(b, h2)[0:64, :], start=(h2 == 0), stop=(h2 == 1))
                    mm.then_inc(setup_pe, 1)
                    pe.matmul(SA[:, 0:P], Wt("a1T"), Wt("a2"), start=True, stop=True).then_inc(setup_pe, 1)
                    pe.wait_ge(setup_act, 1)
                    pe.matmul(SB[:, 0:P], Wt("wT"), a12, start=True, stop=True).then_inc(setup_pe, 1)

                @block.vector
                def _(dve):
                    dve.memset(vdiag[:, :, :], 0.0)
                    dve.memset(negones[:, :], -1.0)
                    dve.memset(neghalf[:, :], -0.5)
                    dve.wait_ge(dma_vec, 16)
                    dve.tensor_scalar(cent2[:, :], V("cent", 0, NE), 2.0, None, ALU.mult)
                    dve.scalar_tensor_tensor(out=centsq[:, :], in0=V("cent", 0, NE), scalar=-float(P), in1=V("cent", 0, NE),
                                             op0=ALU.mult, op1=ALU.mult)
                    dve.tensor_scalar(b2x2[:, :], V("b2", 0, P)[0:NE, :], 2.0, None, ALU.mult)
                    dve.wait_ge(setup_pe, 1)
                    for l, b in enumerate(("bo0", "bo1", "boa")):
                        last = dve.tensor_tensor(bo[:, l:l + 1], OY[:, l:l + 1], V(b), ALU.add)
                    last.then_inc(setup_dve, 1)
                    dve.wait_ge(setup_dve, 1)
                    dve.wait_ge(setup_tanh, 1)
                    dve.tensor_tensor(bog[:, 0:2], bo[:, 0:2], tg[:, 0:2], ALU.mult)
                    dve.wait_ge(dma_const, 16)
                    a, _ = cplace["headsel"]
                    for l, b in enumerate(("bq0", "bqa", "bq3")):
                        dve.tensor_scalar(bq4[:, l, :], csb[:, a:a + 4], V(b), None, ALU.mult)

        def setup_late():
            with nc.Block() as block:
                @block.tensor
                def _(pe):
                    pe.wait_ge(dma_w["late"], 16)
                    for h2 in range(2):
                        mm = pe.matmul(OY[:, 3:4], Wt("o3", h2, 1, 64), V("bv3", h2)[0:64, :], start=(h2 == 0), stop=(h2 == 1))
                    mm.then_inc(late_pe, 1)

                @block.vector
                def _(dve):
                    dve.wait_ge(late_pe, 1)
                    dve.tensor_tensor(bo[:, 3:4], OY[:, 3:4], V("bo3"), ALU.add).then_inc(late_dve, 1)
                    dve.wait_ge(late_dve, 1)
                    dve.tensor_tensor(bog[:, 3:4], bo[:, 3:4], tg[:, 3:4], ALU.mult)

        setup()
        handoff(0, True, False)
        phase(1, 0, True, False)
        phase(0, 1, True, False, load_at=1, need_weights=("moe1",))
        phase(1, 2, True, False, need_weights=("mid",))
        setup_late()
        with nc.Fori(1, NT) as i:
            handoff(0, True, True)
            phase(1, 0, True, True, need_weights=("moe2",))
            phase(0, 1, True, True, load_at=i + 1, need_weights=("late",))
            phase(1, 2, True, True, store_at=i - 1, need_weights=("moe3",))
        handoff(0, False, True)
        phase(1, 0, False, True)
        phase(0, 1, False, True)
        phase(1, 2, False, True, store_at=NT - 1)


def _constants():
    p = np.arange(P)
    ident = np.eye(P, dtype=np.float32)
    d = p % DK
    inv = 1.0 / 10000.0 ** (np.arange(0, DK, 2, dtype=np.float32) / DK)
    ang = np.einsum("i,j->ij", np.arange(SEQ, dtype=np.float32), inv)[:, d % 4].T.astype(np.float32)
    cos, sin = np.cos(ang), np.sin(ang) * np.where(d < 4, -1.0, 1.0)[:, None]
    q, k = p % SEQ, np.arange(SEQ)
    parts = {
        "ident": ident, "center": ident - 1.0 / P, "mean": np.full((P, P), 1.0 / P),
        "cos": cos, "sin": sin,
        "causal": np.where(k[None, :] > q[:, None], -3e38, 3e38),
        "headsel": np.where((p % 32 // DK)[:, None] == np.arange(4)[None, :], DK ** -0.5, 0.0),
        "halves": np.where((p // SEQ)[:, None] == (np.arange(32) // 16)[None, :], 1.0, 0.0),
        "iota8": np.tile(np.arange(NE), (P, 1)),
    }
    return np.concatenate([parts[n].astype(np.float32) for n, _ in CONST_PARTS], axis=1)


def _rows(a):
    return a if a.shape[0] == P else np.concatenate([a, np.zeros((P - a.shape[0], *a.shape[1:]), a.dtype)])


def kernel(**inputs):
    import concourse.bacc as bacc
    from concourse.bass_utils import run_bass_kernel_spmd

    x = {k: np.asarray(v) for k, v in inputs.items()}
    col = lambda n: x[n].reshape(P, 1)
    across = lambda a: np.broadcast_to(a[None, :], (P, a.shape[0]))
    by_parity = lambda a: a.reshape(8, 2, DK, -1).transpose(0, 2, 1, 3).reshape(64, -1)
    swap = lambda w: w.reshape(P, 16, 2, 4)[:, :, ::-1, :].reshape(P, P)
    experts = lambda w: w.transpose(1, 0, 2).reshape(P, -1)
    down = lambda w: w.reshape(NE, -1, P, P).transpose(2, 0, 1, 3).reshape(P, -1)
    pairs = lambda g, u: np.stack([g.reshape(NE, P, -1, P), u.reshape(NE, P, -1, P)], axis=3)\
        .transpose(1, 0, 2, 3, 4).reshape(P, -1)

    vec = {
        "gx": across(x["g_xattn"]), "gf": across(x["g_ffn"]),
        "bq0": col("L0_xattn_bq"), "bk0": col("L0_xattn_bk"), "bv0": _rows(by_parity(x["L0_xattn_bv"])),
        "bo0": col("L0_xattn_bo"), "bf0": col("L0_ffn_bias"),
        "bq1": col("L1_xattn_bq"), "bk1": col("L1_xattn_bk"), "bv1": col("L1_xattn_bv"), "bo1": col("L1_xattn_bo"),
        "ln1w": col("L1_ffn_ln1_w"), "ln1b": col("L1_ffn_ln1_b"), "ln2w": col("L1_ffn_ln2_w"), "ln2b": col("L1_ffn_ln2_b"),
        "bqa": x["L1_ffn_b_qkv"][0:P].reshape(P, 1), "bka": x["L1_ffn_b_qkv"][P:2 * P].reshape(P, 1),
        "bva": _rows(by_parity(x["L1_ffn_b_qkv"][2 * P:])), "boa": col("L1_ffn_b_o"),
        "b1": x["L1_ffn_b1"].reshape(NE * 4, P).T, "g1": col("L2_ffn_g1"), "g2": col("L2_ffn_g2"),
        "lng": col("L2_xattn_ln_g"), "lnb": col("L2_xattn_ln_b"), "clng": col("L2_xattn_cln_g"), "clnb": col("L2_xattn_cln_b"),
        "bq3": col("L3_xattn_bq"), "bk3": col("L3_xattn_bk"), "bv3": _rows(by_parity(x["L3_xattn_bv"])),
        "bo3": col("L3_xattn_bo"), "scale3": col("L3_ffn_scale"), "cent": x["L3_ffn_centroids"].T,
        "gate1": x["L1_ffn_w_gate"], "router2": x["L2_ffn_w_router"], "b2": _rows(x["L1_ffn_b2"]),
    }
    qkv, kv, up3 = x["L1_ffn_w_qkv"], x["L2_xattn_Wkv"], x["L3_ffn_up_w"]
    mats = {
        "q0": x["L0_xattn_Wq"], "k0": x["L0_xattn_Wk"], "v0": x["L0_xattn_Wv"], "o0": _rows(by_parity(x["L0_xattn_Wo"])),
        "wT": x["L0_ffn_weight"].T, "a1T": x["L0_ffn_aux_weight1"].T, "a2": x["L0_ffn_aux_weight2"],
        "q1": x["L1_xattn_Wq"], "k1": x["L1_xattn_Wk"], "v1": x["L1_xattn_Wv"], "o1": x["L1_xattn_Wo"],
        "qa": qkv[:, 0:P], "ka": qkv[:, P:2 * P], "va": qkv[:, 2 * P:], "oa": _rows(by_parity(x["L1_ffn_w_o"])),
        "up1": experts(x["L1_ffn_w1"]), "dn1": down(x["L1_ffn_w2"]),
        "qx": x["L2_xattn_Wq"], "kx": np.concatenate([kv[:, 0:64], kv[:, 0:64]], axis=1), "vx": kv[:, 64:],
        "ox": x["L2_xattn_Wout"].reshape(2, 2, 2, 2, 64, P).transpose(1, 4, 3, 0, 2, 5).reshape(P, 8 * P),
        "ffx": x["L2_xattn_W1"].reshape(P, 2, 4, P).transpose(0, 2, 1, 3).reshape(P, 8 * P),
        "ff2x": x["L2_xattn_W2"].reshape(4, P, P).transpose(1, 0, 2).reshape(P, 4 * P),
        "q2": x["L2_ffn_wq"], "qr2": swap(x["L2_ffn_wq"]), "k2": x["L2_ffn_wk"], "kr2": swap(x["L2_ffn_wk"]),
        "v2": x["L2_ffn_wv"], "o2": _rows(by_parity(x["L2_ffn_wo"])),
        "up2": pairs(x["L2_ffn_wg"], x["L2_ffn_wu"]), "dn2": down(x["L2_ffn_wd"]),
        "q3": x["L3_xattn_Wq"].T, "k3": x["L3_xattn_Wk"].T, "v3": x["L3_xattn_Wv"].T, "o3": _rows(by_parity(x["L3_xattn_Wo"].T)),
        "up3": pairs(up3[:, :, 2 * P:], up3[:, :, 0:2 * P]), "dn3": down(x["L3_ffn_down_w"]),
    }
    tiles = lambda a: a.reshape(P, NT, -1)
    twice = lambda m: np.concatenate([m, m]).reshape(P, NT, -1)
    floats = np.concatenate([tiles(x["x"].reshape(-1, P).T), tiles(x["ctx_1024"].reshape(-1, P).T),
                             twice(x["mask_BxSxS2_ff0"].transpose(1, 0, 2))], axis=2)
    keys = x["mask_BxS2_ik0"].reshape(NT, 2, 2, 1, SEQ).transpose(2, 3, 0, 1, 4)
    keys = np.broadcast_to(keys, (2, SEQ, NT, 2, SEQ)).reshape(P, NT, 2 * SEQ)
    ints = np.concatenate([twice(x["mask_Bx1xSxS2_ik1"].reshape(NSEQ, SEQ, SEQ).transpose(1, 0, 2)), keys,
                           twice(x["mask_BxS2_ik0"].T)], axis=2)
    floats = np.concatenate([floats, floats[:, 0:1]], axis=1).reshape(P, -1)
    ints = np.concatenate([ints, ints[:, 0:1]], axis=1).reshape(P, -1)

    arrays = {"fin": floats, "iin": ints, "consts": _constants(),
              "vecs": np.concatenate([vec[n] for n, _ in VEC_PARTS], axis=1)}
    for g, parts in W_PARTS:
        arrays[f"w_{g}"] = np.concatenate([mats[n] for n, _ in parts], axis=1)
    arrays = {f"in_{k}": np.ascontiguousarray(v) for k, v in arrays.items()}
    nc = bacc.Bacc("TRN2", target_bir_lowering=False, num_devices=1)
    aps = {k[3:]: nc.dram_tensor(k, v.shape, mybir.dt.from_np(v.dtype), kind="ExternalInput").ap()
           for k, v in arrays.items()}
    out = nc.dram_tensor("out_0", (P, NSEQ * SEQ), F32, kind="ExternalOutput").ap()
    build(nc, aps["fin"], aps["iin"], aps["consts"], aps["vecs"], {g: aps[f"w_{g}"] for g, _ in W_PARTS}, out)
    r = run_bass_kernel_spmd(nc, [arrays], core_ids=[0])
    y = r.results[0]["out_0"]
    return np.ascontiguousarray(y.T).reshape(NSEQ, SEQ, P)
```

```python
from contextlib import ExitStack

import concourse.bass as bass
import numpy as np
from concourse import mybir

F32 = mybir.dt.float32
I32 = mybir.dt.int32
U32 = mybir.dt.uint32
ALU = mybir.AluOpType
ACT = mybir.ActivationFunctionType
AX = mybir.AxisListType

P = 128
SEQ = 64
NSEQ = 32
BT = 4
T = BT * SEQ
NT = NSEQ // BT
W2T = 2 * T
NE = 8
DK = 8
GELU_C = float(np.sqrt(2.0 / np.pi))

FX, FC, FM, FCOLS = 0, T, 2 * T, 3 * T
IM0, IM1, IM3, ICOLS = 0, 2 * SEQ, 4 * SEQ, 4 * SEQ + 2


def columns(parts):
    at, place = 0, {}
    for name, n in parts:
        place[name] = (at, at + n)
        at += n
    return place, at


CONST_PARTS = [("ident", P), ("center", P), ("mean", P), ("cos", SEQ), ("sin", SEQ), ("causal", SEQ),
               ("headsel", 4), ("halves", 32), ("iota8", 8)]
VEC_PARTS = [("gx", 4), ("gf", 4), ("bq0", 1), ("bk0", 1), ("bv0", 1), ("bo0", 1), ("bf0", 1),
             ("bq1", 1), ("bk1", 1), ("bv1", 1), ("bo1", 1), ("ln1w", 1), ("ln1b", 1), ("ln2w", 1), ("ln2b", 1),
             ("bqa", 1), ("bka", 1), ("bva", 1), ("boa", 1), ("b1", NE * 4), ("g1", 1), ("g2", 1),
             ("lng", 1), ("lnb", 1), ("clng", 1), ("clnb", 1), ("bq3", 1), ("bk3", 1), ("bv3", 1), ("bo3", 1),
             ("scale3", 1), ("cent", NE), ("gate1", NE), ("router2", NE), ("b2", P)]
W_PARTS = [
    ("early", [("q0", P), ("k0", P), ("v0", P), ("o0", P),
               ("q1", P), ("k1", P), ("v1", P), ("o1", P), ("qa", P), ("ka", P), ("va", P), ("oa", P)]),
    ("ff0", [("wT", P), ("a1T", P), ("a2", P)]),
    ("moe1", [("up1", NE * 4 * P), ("dn1", NE * 4 * P)]),
    ("mid", [("qx", 8 * P), ("kx", P), ("vx", 64), ("ox", 8 * P), ("ffx", 8 * P), ("ff2x", 4 * P),
             ("q2", P), ("qr2", P), ("k2", P), ("kr2", P), ("v2", P), ("o2", P)]),
    ("moe2", [("up2", NE * 6 * P), ("dn2", NE * 3 * P)]),
    ("late", [("q3", P), ("k3", P), ("v3", P), ("o3", P)]),
    ("moe3", [("up3", NE * 4 * P), ("dn3", NE * 2 * P)]),
]

NORM_SIGNALS = ["centred", "squared", "copied", "meansq", "stat", "first", "second", "rooted", "spread", "normed",
                "chain"]
ATTN_SIGNALS = NORM_SIGNALS + [
    "context", "contextT", "contextT_taken", "context_normed", "exped", "gated", "q_taken", "probsT", "probsT_taken",
    "proj_k", "proj_q", "proj_v", "projected", "projected_inner", "k_heads", "roped", "scores", "shifted", "v_blocks",
    "x_new"]
FF_SIGNALS = ["ff_hidden", "ff_hidden_tanh"]
BIG_SIGNALS = ["big_" + name for name in (
    "added", "context", "contextT_taken", "exped", "hidden", "hidden_done", "hidden_tanh", "k_taken", "probsT",
    "probsT_taken", "probs_normed", "proj_k", "proj_q", "proj_v", "q_heads", "q_heads_dve", "scores", "shifted",
    "v_blocks")]
MOE_SIGNALS = ["m_" + name for name in NORM_SIGNALS + [
    "logits", "gap", "gap_exp", "comb", "combT", "combT_taken", "weight_even", "weight_odd", "up", "up_free", "tanh", "act", "down",
    "out"]]
GELU_SIGNALS = ["m_square", "m_poly", "m_cubic"]
GLU_SIGNALS = ["m_weight_taken", "m_rowsq"]


PACE = {1: 1.0, 2: 1.0, 3: 1.0}


def choose_order(attn, moe, pace):
    order, left = [], [attn is not None, moe is not None]
    due = 0
    while left[0] or left[1]:
        half = 1 if left[1] and (due > 0 or not left[0]) else 0
        got = next((attn, moe)[half], "end")
        if got == "end":
            left[half] = False
            continue
        order.append(half)
        due = due + pace * (got or 0) if half == 0 else due - (got or 0)
    return order


def side_by_side(attn, moe, order):
    halves = [attn, moe]
    for half in order:
        next(halves[half])
    for half in halves:
        if half is not None:
            assert next(half, "end") == "end", "a half has more slots on this engine than on TensorE"


def build(nc, fin, iin, consts, vecs, weights, out):
    cplace, ccols = columns(CONST_PARTS)
    vplace, vcols = columns(VEC_PARTS)
    wplace = {}
    for group, parts in W_PARTS:
        place, _ = columns(parts)
        wplace.update({name: (group, *ab) for name, ab in place.items()})

    with ExitStack() as ctx:
        def sb(name, shape, dt=F32):
            return ctx.enter_context(nc.sbuf_tensor(name, shape, dt))

        def bank(name):
            return ctx.enter_context(nc.psum_tensor(name, [P, W2T], F32))

        def sem(name):
            return ctx.enter_context(nc.semaphore(name))

        csb = sb("csb", [P, ccols])
        vsb = sb("vsb", [P, vcols])
        wsb = {g: sb(f"w_{g}", [P, columns(parts)[1]]) for g, parts in W_PARTS if g != "ff0"}

        def C(name):
            a, b = cplace[name]
            return csb[:, a:b]

        def V(name, i=0, n=1):
            a, _ = vplace[name]
            return vsb[:, a + i:a + i + n]

        def Wt(name, i=0, n=1, rows=P):
            g, a, _ = wplace[name]
            return wsb[g][0:rows, a + i * P:a + (i + n) * P]

        ff0 = sb("ff0", [P, P])
        tg = sb("tg", [P, 8])
        bo = sb("bo", [P, 4])
        bog = sb("bog", [P, 4])
        bk4 = sb("bk4", [P, 3, 4])
        cent2 = sb("cent2", [P, NE])
        centsq = sb("centsq", [P, NE])
        b2x2 = sb("b2x2", [NE, P])
        negones = sb("negones", [P, NE])

        stage_f = sb("stage_f", [P, FCOLS])
        stage_i = sb("stage_i", [P, ICOLS], I32)
        tile_f = sb("tile_f", [P, FCOLS])
        xN, ctxN = stage_f[:, FX:FX + T], stage_f[:, FC:FC + T]
        xF, ctxF, addmask = tile_f[:, FX:FX + T], tile_f[:, FC:FC + T], tile_f[:, FM:FM + T]
        xS = sb("xS", [P, T])
        ctxS = sb("ctxS", [P, T])
        hF = sb("hF", [P, T])
        hS = sb("hS", [P, T])
        rowF = sb("rowF", [P, 2])
        rowS = sb("rowS", [P, 2])

        SA, SB, TP, OY = bank("SA"), bank("SB"), bank("TP"), bank("OY")
        fx = sb("fx", [P, 2, T])
        un = sb("un", [P, W2T])
        small = sb("small", [P, 24])
        msmall = sb("msmall", [P, 24])
        neghalf = sb("neghalf", [P, 4])
        xn = sb("xn", [P, T])
        k4 = sb("k4", [P, BT, 4, SEQ])
        qk = sb("qk", [P, W2T])
        qkr = sb("qkr", [P, W2T])
        vblk = sb("vblk", [P, W2T])
        probs = sb("probs", [P, 2, W2T])
        probsT = sb("probsT", [P, 2, W2T])
        mx = sb("mx", [P, 2, 8])
        sums = sb("sums", [P, 2, 4, 4])
        rinv = sb("rinv", [P, 32])
        maskA = sb("maskA", [P, 2, SEQ])
        mask1 = sb("mask1", [P, 2, 2 * SEQ])
        upd = sb("upd", [P, T])
        qx = sb("qx", [P, 4, BT, 2, SEQ])
        vdiag = sb("vdiag", [P, BT, P])
        otx = sb("otx", [P, 4, W2T])
        sq = qkr
        onorm = upd
        fact = k4[:, :, :, :].rearrange("p a b q -> p a (b q)")

        H0, H1, WB, YM = bank("H0"), bank("H1"), bank("WB"), bank("YM")
        H = [H0, H1, WB]
        msq = sb("msq", [P, T])
        mu = sb("mu", [P, T])
        my = sb("my", [P, T])
        lg = sb("lg", [P, 2, NE])
        top = sb("top", [P, 2, 8])
        topi = sb("topi", [P, 2, 8], U32)
        topf = sb("topf", [P, 2, 8])
        gap = sb("gap", [P, 2])
        gapx = sb("gapx", [P, 2])
        w01 = sb("w01", [P, 2, 2])
        pick = sb("pick", [P, 2, 2, NE])
        comb = sb("comb", [P, 2, NE])
        combT = sb("combT", [NE, T])
        wexp = sb("wexp", [P, 2, T])
        hb = sb("hb", [P, 3, W2T])
        hp = sb("hp", [P, 3, W2T])
        act = sb("act", [P, 3, W2T])

        wsb["ff0"] = act[:, 0:2, :].rearrange("p a n -> p (a n)")[:, 0:3 * P]
        a12 = act[:, 2, 0:P]

        dma_const = sem("dma_const")
        dma_vec = sem("dma_vec")
        dma_w = {g: sem(f"dma_w_{g}") for g, _ in W_PARTS}
        dma_first = sem("dma_first")
        sets = [{n: sem(f"{n}_0") for n in ATTN_SIGNALS + FF_SIGNALS + MOE_SIGNALS + GELU_SIGNALS},
                {n: sem(f"{n}_1") for n in ATTN_SIGNALS + BIG_SIGNALS + MOE_SIGNALS + GLU_SIGNALS
                 + ["tile_in", "out_store"]}]
        setup_tanh, setup_pe, setup_act, setup_dve = (sets[1][n] for n in ("big_hidden_tanh", "big_hidden", "copied", "stat"))
        late_pe, late_dve = sets[1]["projected"], sets[1]["gated"]

        class Counts:

            def __init__(self, sems):
                self.sems, self.seen, self.given = sems, {}, {}

            def next(self, name):
                self.seen[name] = self.seen.get(name, 0) + 1
                return self.sems[name], self.seen[name]

            def skip(self, name, n):
                self.seen[name] = self.seen.get(name, 0) + n

            def give(self, name):
                self.given[name] = self.given.get(name, 0) + 1
                return self.sems[name], 1

        class Norm:
            def __init__(self, prefix, centred, stat, spread, spread2, squares, u, small):
                self.sig = lambda name: prefix + name
                self.centred, self.stat, self.spread, self.spread2 = centred, stat, spread, spread2
                self.squares, self.u, self.small = squares, u, small

            def col(self, what, n):
                return self.small[:, 4 * what:4 * what + n]

        ANORM = Norm("", SA, SB, TP, OY, sq, un, small)
        MNORM = Norm("m_", H0, H1, WB, None, msq, mu, msmall)

        def norm_pe(c, k, kind, src, fresh=False, second=None):
            pe = nc.tensor
            n = 2 if second is None else 4
            if fresh:
                pe.wait_ge(*c.next("x_new"))
            if kind != "rms":
                mm = pe.matmul(k.centred[:, 0:T], C("center"), src, start=True, stop=True)
                if second is not None:
                    mm = pe.matmul(k.centred[:, T:], C("center"), second, start=True, stop=True)
                mm.then_inc(*c.give(k.sig("centred")))
            yield 2
            pe.wait_ge(*c.next(k.sig("squared")))
            for s in range(n):
                mm = pe.matmul(k.stat[:, s:s + 1], k.squares[:, s * P:(s + 1) * P], C("mean")[:, 0:1],
                               start=True, stop=True, skip_group_check=True)
            mm.then_inc(*c.give(k.sig("meansq")))
            yield 3
            if kind == "both":
                yield 4
            pe.wait_ge(*c.next(k.sig("rooted")))
            for s in range(2):
                if kind == "both":
                    pe.matmul(k.spread[:, T + s * P:T + (s + 1) * P], k.col(5, 4)[:, s:s + 1].to_broadcast([P, P]),
                              C("ident"), start=True, stop=True)
                if n == 4:
                    pe.matmul(k.spread2[:, s * P:(s + 1) * P], k.col(2, 4)[:, 2 + s:3 + s].to_broadcast([P, P]),
                              C("ident"), start=True, stop=True)
                mm = pe.matmul(k.spread[:, s * P:(s + 1) * P], k.col(2, 4)[:, s:s + 1].to_broadcast([P, P]),
                               C("ident"), start=True, stop=True)
            mm.then_inc(*c.give(k.sig("spread")))
            yield 2 if kind == "layer" else 3

        def norm_act(c, k, kind, src=None, w=T):
            a = nc.scalar
            if kind == "rms":
                a.activation(k.squares[:, 0:w], src, ACT.Square).then_inc(*c.give(k.sig("squared")))
            else:
                a.wait_ge(*c.next(k.sig("centred")))
                a.activation(k.squares[:, 0:w], k.centred[:, 0:w], ACT.Square).then_inc(*c.give(k.sig("squared")))
                a.activation(k.u[:, 0:w], k.centred[:, 0:w], ACT.Copy).then_inc(*c.give(k.sig("copied")))
            yield
            yield
            if kind == "both":
                yield
            yield

        def norm_pool(c, k, kind, w=T):
            g, n = nc.gpsimd, w // P
            yield
            g.wait_ge(*c.next(k.sig("stat")))
            g.tensor_tensor(k.col(2, n), k.col(1, n), neghalf[:, 0:n], ALU.pow)\
             .then_inc(*c.give(k.sig("rooted" if kind != "both" else "first")))
            yield
            if kind == "both":
                g.wait_ge(*c.next(k.sig("stat")))
                g.tensor_tensor(k.col(4, 2), k.col(3, 2), neghalf[:, 0:2], ALU.pow).then_inc(*c.give(k.sig("second")))
                yield
            yield

        def link(c, ins, name="chain"):
            ins.then_inc(*c.give(name))
            nc.vector.wait_ge(*c.next(name))

        def norm_dve(c, k, kind, src=None, y=None, g=None, b=None, eps2=None, w=T, ctx_gb=None):
            dve, n = nc.vector, w // P
            lk = lambda ins: link(c, ins, k.sig("chain"))
            yield
            dve.wait_ge(*c.next(k.sig("meansq")))
            if kind == "both":
                dve.tensor_copy(k.col(0, 2), k.stat[:, 0:2])
            dve.tensor_scalar(k.col(1, n), k.stat[:, 0:n], eps2 if kind == "rms" else 1e-5, None, ALU.add)\
               .then_inc(*c.give(k.sig("stat")))
            yield
            if kind == "both":
                r = k.col(2, 2)
                dve.wait_ge(*c.next(k.sig("first")))
                lk(dve.tensor_tensor(k.col(3, 2), k.col(0, 2), r, ALU.mult))
                lk(dve.tensor_tensor(k.col(3, 2), k.col(3, 2), r, ALU.mult))
                dve.tensor_scalar(k.col(3, 2), k.col(3, 2), eps2, None, ALU.add).then_inc(*c.give(k.sig("stat")))
                dve.wait_ge(*c.next(k.sig("second")))
                dve.tensor_tensor(k.col(5, 2), k.col(4, 2), r, ALU.mult).then_inc(*c.give(k.sig("rooted")))
                yield
            dve.wait_ge(*c.next(k.sig("spread")))
            if kind == "rms":
                dve.scalar_tensor_tensor(out=y, in0=src, scalar=g, in1=k.spread[:, 0:T], op0=ALU.mult, op1=ALU.mult)\
                   .then_inc(*c.give(k.sig("normed")))
                yield
                return
            dve.wait_ge(*c.next(k.sig("copied")))
            if kind == "both":
                ins = dve.scalar_tensor_tensor(out=y, in0=k.u[:, 0:T], scalar=g, in1=k.spread[:, T:], op0=ALU.mult,
                                               op1=ALU.mult)
                if b is not None:
                    lk(ins)
                    ins = dve.tensor_scalar(y, y, b, None, ALU.add)
                lk(ins)
            if ctx_gb is not None:
                lk(dve.scalar_tensor_tensor(out=k.u[:, T:], in0=k.u[:, T:], scalar=ctx_gb[0], in1=k.spread2[:, 0:T],
                                            op0=ALU.mult, op1=ALU.mult))
                dve.tensor_scalar(k.u[:, T:], k.u[:, T:], ctx_gb[1], None, ALU.add)
            ins = dve.tensor_tensor(k.u[:, 0:T], k.u[:, 0:T], k.spread[:, 0:T], ALU.mult)
            if kind == "layer" and y is not None:
                lk(ins)
                ins = dve.tensor_scalar(y, k.u[:, 0:T], g, b, ALU.mult, ALU.add)
            ins.then_inc(*c.give(k.sig("normed")))
            yield

        def heads_pe(c, wq, wk, wv, wo, xq, xkv, rope=None, inner=False):
            pe = nc.tensor
            pe.wait_ge(*c.next("normed"))
            if rope is None:
                pe.matmul(SA[:, 0:T], wk, xkv, start=True, stop=True).then_inc(*c.give("proj_k"))
                pe.matmul(SB[:, 0:T], wq, xq, start=True, stop=True).then_inc(*c.give("proj_q"))
            else:
                pe.matmul(SA[:, 0:T], wk, xkv, start=True, stop=True)
                pe.matmul(SA[:, T:], wq, xq, start=True, stop=True)
                pe.matmul(SB[:, 0:T], rope[1], xkv, start=True, stop=True)
                pe.matmul(SB[:, T:], rope[0], xq, start=True, stop=True).then_inc(*c.give("proj_q"))
            for b in range(BT):
                to = TP[:, b // 2 * T:(b // 2 + 1) * T].rearrange("p (a c n) -> p a c n", c=2, n=2 * DK)[:, :, b % 2, :]
                for half in (0, SEQ):
                    mm = pe.matmul(to[half:half + SEQ], xkv[:, b * SEQ:(b + 1) * SEQ],
                                   wv.rearrange("p (a n) -> p a n", n=2 * DK), start=True, stop=True,
                                   skip_group_check=True)
            mm.then_inc(*c.give("proj_v"))
            yield 1 if rope is None else 4
            qT = qk[:, T:]

            def scores(g):
                if g == 0:
                    pe.wait_ge(*c.next("k_heads"))
                    if rope is None:
                        pe.wait_ge(*c.next("q_taken"))
                S = (SA, SB)[g % 2]
                r = slice(32 * g, 32 * g + 32)
                for b in range(BT):
                    half = b % 2 * SEQ
                    mm = pe.matmul(S[half:half + SEQ, b // 2 * T:(b // 2 + 1) * T], qT[r, b * SEQ:(b + 1) * SEQ],
                                   k4[r, b, :, :].rearrange("p h k -> p (h k)"), start=True, stop=True,
                                   skip_group_check=True)
                mm.then_inc(*c.give("scores"))

            def transposes(g):
                pe.wait_ge(*c.next("exped"))
                if g == 0:
                    pe.wait_ge(*c.next("v_blocks"))
                for b in range(BT):
                    mm = pe.transpose(TP[:, b * P:(b + 1) * P], probs[:, g % 2, b * P:(b + 1) * P], C("ident"))
                mm.then_inc(*c.give("probsT"))

            def weigh(g):
                pe.wait_ge(*c.next("probsT_taken"))
                for mh in range(4):
                    at = mh // 2 * T + g * 64 + mh % 2 * 32
                    mm = pe.matmul(OY[:, at:at + 32], probsT[:, g % 2, mh * P:(mh + 1) * P], vblk[:, at:at + 32],
                                   start=True, stop=True, skip_group_check=True)
                if g == 3:
                    mm.then_inc(*c.give("context"))

            for k in range(5):
                if k == 0:
                    scores(0)
                if k < 3:
                    if k >= 1:
                        pe.wait_ge(*c.next("shifted"))
                    scores(k + 1)
                yield 1
                if k >= 1:
                    transposes(k - 1)
                yield 2
                if k >= 1:
                    weigh(k - 1)
                yield 1 if k < 4 else 4
            c.skip("shifted", 2)
            pe.wait_ge(*c.next("context_normed"))
            for m in range(2):
                mm = pe.transpose(TP[:, m * P:(m + 1) * P], onorm[:, m * P:(m + 1) * P], C("ident"))
            mm.then_inc(*c.give("contextT"))
            yield 2
            pe.wait_ge(*c.next("contextT_taken"))
            mm = pe.matmul(SA[:, 0:T], wo, qkr[:, 0:T], start=True, stop=True)
            mm.then_inc(*c.give("projected_inner" if inner else "projected"))
            yield 2 if inner else 4

        def heads_act(c, bias4, gate=None, rope=False):
            a = nc.scalar
            if rope:
                a.wait_ge(*c.next("roped"))
                src = qk[:, 0:T]
            else:
                a.wait_ge(*c.next("proj_k"))
                src = SA[:, 0:T]
            for i in range(4):
                q = a.activation(k4[:, :, i, :], src.rearrange("p (b q) -> p b q", b=BT), ACT.Identity, scale=csb[:, cplace["headsel"][0] + i:][:, 0:1],
                                 bias=bias4(i) if bias4 else 0.0)
            q.then_inc(*c.give("k_heads"))
            yield
            for k in range(5):
                yield
                if k >= 1:
                    a.wait_ge(*c.next("probsT"))
                    a.activation(probsT[:, (k - 1) % 2, :], TP[:, :], ACT.Copy).then_inc(*c.give("probsT_taken"))
                yield
                if k < 4:
                    a.wait_ge(*c.next("shifted"))
                    a.activation(probs[:, k % 2, :], probs[:, k % 2, :], ACT.Exp).then_inc(*c.give("exped"))
                yield
            a.wait_ge(*c.next("contextT"))
            a.activation(qkr[:, 0:T], TP[:, 0:T], ACT.Copy)\
             .then_inc(*c.give("contextT_taken"))
            yield
            if gate is not None:
                a.wait_ge(*c.next("projected"))
                a.activation(upd[:, :], SA[:, 0:T], ACT.Identity, scale=gate[0], bias=gate[1])\
                 .then_inc(*c.give("gated"))
            yield

        def heads_dve(c, qbias, mask, x, inner=None, rope=False):
            dve = nc.vector
            qT = qk[:, T:]
            if rope:
                dve.wait_ge(*c.next("proj_q"))
                cs = C("cos").unsqueeze(1).to_broadcast([P, 8, SEQ])
                sn = C("sin").unsqueeze(1).to_broadcast([P, 8, SEQ])
                by_seq = lambda t: t.rearrange("p (a t) -> p a t", t=SEQ)
                dve.tensor_tensor(by_seq(qk[:, :]), by_seq(SA[:, :]), cs, ALU.mult)
                link(c, dve.tensor_tensor(by_seq(qkr[:, :]), by_seq(SB[:, :]), sn, ALU.mult))
                dve.tensor_tensor(qk[:, :], qk[:, :], qkr[:, :], ALU.add).then_inc(*c.give("roped"))
            else:
                dve.wait_ge(*c.next("proj_q"))
                dve.tensor_scalar(qT, SB[:, 0:T], qbias, None, ALU.add).then_inc(*c.give("q_taken"))
            dve.wait_ge(*c.next("proj_v"))
            halves = C("halves").unsqueeze(1).to_broadcast([P, 16, 32])
            dve.tensor_tensor(vblk[:, :].rearrange("p (a n) -> p a n", n=32),
                              TP[:, :].rearrange("p (a n) -> p a n", n=32), halves, ALU.mult)\
               .then_inc(*c.give("v_blocks"))
            yield

            def add_up(k):
                dve.wait_ge(*c.next("exped"))
                return dve.tensor_reduce(sums[:, :, k, :], probs[:, k % 2, :].rearrange("p (m h k) -> p m h k", m=2, h=4),
                                         AX.X, ALU.add)

            for k in range(5):
                if k < 4:
                    dve.wait_ge(*c.next("scores"))
                    if k >= 2:
                        dve.wait_ge(*c.next("probsT"))
                    S = (SA, SB)[k % 2][:, :]
                    p = probs[:, k % 2, :]
                    p3 = p.rearrange("p (a k) -> p a k", k=SEQ)
                    if mask is None:
                        src = S
                    else:
                        m = mask
                        if len(m.shape) == 2:
                            m = m.unsqueeze(1).to_broadcast([P, 8, SEQ])
                            link(c, dve.tensor_tensor(p3, S.rearrange("p (a k) -> p a k", k=SEQ), m, ALU.min))
                        else:
                            m = m.unsqueeze(2).to_broadcast([P, 2, 4, SEQ])
                            link(c, dve.tensor_tensor(p.rearrange("p (m h k) -> p m h k", m=2, h=4),
                                                      S.rearrange("p (m h k) -> p m h k", m=2, h=4), m, ALU.min))
                        src = p
                    s3 = src.rearrange("p (a k) -> p a k", k=SEQ)
                    link(c, dve.tensor_reduce(mx[:, k % 2, :], s3, AX.X, ALU.max))
                yield
                if k < 4:
                    sh = dve.tensor_tensor(p3, s3, mx[:, k % 2, :].unsqueeze(2).to_broadcast([P, 8, SEQ]), ALU.subtract)
                    sh.then_inc(*c.give("shifted"))
                yield
                if k >= 1:
                    link(c, add_up(k - 1))
                if k == 4:
                    link(c, dve.reciprocal(rinv[:, :], sums[:, :, :, :].rearrange("p m g h -> p (m g h)")))
                if k == 4:
                    dve.wait_ge(*c.next("context"))
                    for b2 in range(2):
                        r = slice(SEQ * b2, SEQ * b2 + SEQ)
                        o = dve.tensor_tensor(
                            onorm[r, :].rearrange("p (a h d) -> p a h d", h=2, d=DK),
                            OY[r, :].rearrange("p (a c h d) -> p a c h d", c=2, h=2, d=DK)[:, :, b2, :, :],
                            rinv[r, :].rearrange("p (a h) -> p a h", h=2).unsqueeze(3).to_broadcast([SEQ, 16, 2, DK]),
                            ALU.mult)
                    o.then_inc(*c.give("context_normed"))
                yield
            c.skip("probsT", 2)
            yield
            if inner is None:
                dve.wait_ge(*c.next("gated"))
                dve.tensor_tensor(x, x, upd[:, :], ALU.add).then_inc(*c.give("x_new"))
            else:
                h, base, bias = inner
                dve.wait_ge(*c.next("projected_inner"))
                dve.scalar_tensor_tensor(out=h, in0=SA[:, 0:T], scalar=bias, in1=base, op0=ALU.add,
                                         op1=ALU.add).then_inc(*c.give("x_new"))
            yield

        def single_pe(c):
            pe = nc.tensor
            kT = qk[:, T:]
            pe.wait_ge(*c.next("normed"))
            pe.matmul(SA[:, 0:T], Wt("q1"), un[:, 0:T], start=True, stop=True).then_inc(*c.give("big_proj_q"))
            pe.matmul(SB[:, 0:T], Wt("k1"), ctxF, start=True, stop=True).then_inc(*c.give("big_proj_k"))
            yield 2
            pe.wait_ge(*c.next("big_q_heads"))
            pe.wait_ge(*c.next("big_k_taken"))
            for b in range(BT):
                t = slice(b * SEQ, (b + 1) * SEQ)
                r = slice(SEQ * (b % 2), SEQ * (b % 2) + SEQ)
                mm = pe.matmul(SA[r, SEQ * (b // 2):SEQ * (b // 2) + SEQ], k4[:, b, 0, :], kT[:, t],
                               start=True, stop=True, skip_group_check=True)
            mm.then_inc(*c.give("big_scores"))
            for b in range(BT):
                mm = pe.matmul(TP[0:SEQ, b * P:(b + 1) * P], kT[:, b * SEQ:(b + 1) * SEQ], Wt("v1"),
                               start=True, stop=True)
            mm.then_inc(*c.give("big_proj_v"))
            yield 4
            yield 4
            pe.wait_ge(*c.next("big_probs_normed"))
            for m in range(2):
                mm = pe.transpose(OY[0:SEQ, m * P:(m + 1) * P], probs[:, 0, m * SEQ:(m + 1) * SEQ], C("ident"))
            mm.then_inc(*c.give("big_probsT"))
            yield 2
            pe.wait_ge(*c.next("big_v_blocks"))
            pe.wait_ge(*c.next("big_probsT_taken"))
            for b in range(BT):
                mm = pe.matmul(SB[:, b * SEQ:(b + 1) * SEQ], vblk[0:SEQ, b * P:(b + 1) * P],
                               probsT[0:SEQ, 0, b * SEQ:(b + 1) * SEQ], start=True, stop=True, skip_group_check=True)
            mm.then_inc(*c.give("big_context"))
            yield 2
            pe.wait_ge(*c.next("big_contextT_taken"))
            pe.matmul(SA[:, 0:T], Wt("o1"), qkr[:, 0:T], start=True, stop=True).then_inc(*c.give("projected"))
            yield 4

        def single_act(c):
            a = nc.scalar
            a.wait_ge(*c.next("big_proj_q"))
            a.activation(k4[:, :, 0, :], SA[:, 0:T].rearrange("p (b q) -> p b q", b=BT), ACT.Identity, bias=V("bq1")).then_inc(*c.give("big_q_heads"))
            yield
            a.wait_ge(*c.next("big_proj_v"))
            a.activation(vblk[0:SEQ, :], TP[0:SEQ, :], ACT.Copy)\
             .then_inc(*c.give("big_v_blocks"))
            a.wait_ge(*c.next("big_shifted"))
            a.activation(probs[:, 0, 0:P], probs[:, 0, 0:P], ACT.Exp).then_inc(*c.give("big_exped"))
            yield
            yield
            a.wait_ge(*c.next("big_probsT"))
            a.activation(probsT[0:SEQ, 0, 0:T], OY[0:SEQ, 0:T], ACT.Copy).then_inc(*c.give("big_probsT_taken"))
            yield
            a.wait_ge(*c.next("big_context"))
            a.activation(qkr[:, 0:T], SB[:, 0:T], ACT.Copy).then_inc(*c.give("big_contextT_taken"))
            yield
            a.wait_ge(*c.next("projected"))
            a.activation(upd[:, :], SA[:, 0:T], ACT.Identity, scale=tg[:, 1:2], bias=bog[:, 1:2])\
             .then_inc(*c.give("gated"))
            yield

        def single_dve(c):
            dve = nc.vector
            s = probs[:, 0, 0:P]
            s2 = s.rearrange("p (m k) -> p m k", m=2)
            dve.wait_ge(*c.next("big_proj_k"))
            dve.tensor_scalar(qk[:, T:], SB[:, 0:T], V("bk1"), None, ALU.add).then_inc(*c.give("big_k_taken"))
            yield
            dve.wait_ge(*c.next("big_scores"))
            link(c, dve.tensor_tensor(s, SA[:, 0:P], mask1[:, 0, :], ALU.mult))
            link(c, dve.tensor_tensor(s, s, mask1[:, 1, :], ALU.add))
            link(c, dve.tensor_reduce(mx[:, 0, 0:2], s2, AX.X, ALU.max))
            dve.tensor_tensor(s2, s2, mx[:, 0, 0:2].unsqueeze(2).to_broadcast([P, 2, SEQ]), ALU.subtract)\
               .then_inc(*c.give("big_shifted"))
            yield
            dve.wait_ge(*c.next("big_exped"))
            link(c, dve.tensor_reduce(mx[:, 1, 0:2], s2, AX.X, ALU.add))
            link(c, dve.reciprocal(mx[:, 1, 0:2], mx[:, 1, 0:2]))
            dve.tensor_tensor(s2, s2, mx[:, 1, 0:2].unsqueeze(2).to_broadcast([P, 2, SEQ]), ALU.mult)\
               .then_inc(*c.give("big_probs_normed"))
            yield
            yield
            yield
            dve.wait_ge(*c.next("gated"))
            dve.tensor_tensor(xF, xF, upd[:, :], ALU.add).then_inc(*c.give("x_new"))
            yield

        def ff0_pe(c):
            nc.tensor.wait_ge(*c.next("normed"))
            nc.tensor.matmul(SA[:, 0:T], ff0[:, :], un[:, 0:T], start=True, stop=True).then_inc(*c.give("ff_hidden"))
            yield 3

        def ff0_act(c):
            nc.scalar.wait_ge(*c.next("ff_hidden"))
            nc.scalar.activation(upd[:, :], SA[:, 0:T], ACT.Tanh, bias=V("bf0")).then_inc(*c.give("ff_hidden_tanh"))
            yield

        def ff0_dve(c):
            nc.vector.wait_ge(*c.next("ff_hidden_tanh"))
            nc.vector.scalar_tensor_tensor(out=xN, in0=upd[:, :], scalar=tg[:, 4:5], in1=xN, op0=ALU.mult,
                                           op1=ALU.add).then_inc(*c.give("x_new"))
            yield

        def by_chunk(S):
            return S[:, :].rearrange("p (c b q) -> p b c q", c=2, b=BT)

        def wide_pe(c):
            pe = nc.tensor
            kT, cn = qk[:, T:], un[:, T:]
            pe.wait_ge(*c.next("normed"))
            pe.matmul(OY[:, 0:T], Wt("kx"), cn, start=True, stop=True).then_inc(*c.give("big_proj_k"))
            g, a, z = wplace["vx"]
            for b in range(BT):
                for half in (0, SEQ):
                    mm = pe.matmul(TP[half:half + SEQ, b * 64:(b + 1) * 64], cn[:, b * SEQ:(b + 1) * SEQ],
                                   wsb[g][:, a:z], start=True, stop=True, skip_group_check=True)
            mm.then_inc(*c.give("big_proj_v"))

            def queries(p):
                for i in range(2):
                    mm = pe.matmul((SA, SB)[p % 2][:, i * T:(i + 1) * T], Wt("qx", 2 * p + i), xn[:, :],
                                   start=True, stop=True)
                mm.then_inc(*c.give("big_proj_q"))

            queries(0)
            queries(1)
            yield 1
            pe.wait_ge(*c.next("big_q_heads"))
            queries(2)
            pe.wait_ge(*c.next("big_q_heads_dve"))
            queries(3)
            yield 2

            def scores(u):
                j, mp = u // 2, u % 2
                r = slice(64 * j, 64 * j + 64)
                if u == 0:
                    pe.wait_ge(*c.next("big_k_taken"))
                    pe.wait_ge(*c.next("big_q_heads"))
                    pe.wait_ge(*c.next("big_q_heads_dve"))
                if u >= 2:
                    pe.wait_ge(*c.next("big_added"))
                for b in range(BT):
                    for m2 in range(2):
                        at = (2 * b + m2) * SEQ
                        mm = pe.matmul((SA, SB)[u % 2][:, at:at + SEQ], qx[r, 2 * mp + m2, b, :, :].rearrange("p c q -> p (c q)"),
                                       kT[r, b * SEQ:(b + 1) * SEQ], start=True, stop=True, skip_group_check=True)
                mm.then_inc(*c.give("big_scores"))

            def transposes(u):
                pe.wait_ge(*c.next("big_probs_normed"))
                if u == 0:
                    pe.wait_ge(*c.next("big_v_blocks"))
                for b in range(BT):
                    mm = pe.transpose(TP[:, b * P:(b + 1) * P], probs[:, u % 2, b * P:(b + 1) * P], C("ident"))
                mm.then_inc(*c.give("big_probsT"))

            def weigh(u):
                pe.wait_ge(*c.next("big_probsT_taken"))
                if u >= 1:
                    pe.wait_ge(*c.next("big_contextT_taken"))
                for b in range(BT):
                    mm = pe.matmul(OY[:, b * P:(b + 1) * P], vdiag[:, b, :], probsT[:, u % 2, b * P:(b + 1) * P],
                                   start=True, stop=True)
                mm.then_inc(*c.give("big_context"))

            for k in range(6):
                if k == 0:
                    scores(0)
                if k < 3:
                    scores(k + 1)
                yield 1
                if k >= 2:
                    weigh(k - 2)
                yield 2 if k < 5 else 0
                yield 2 if k < 5 else 0
                if 1 <= k < 5:
                    transposes(k - 1)
                yield 1
            for ch in range(4):
                if ch >= 2:
                    pe.wait_ge(*c.next("big_hidden_done"))
                S = (SA, SB)[ch % 2]
                pe.matmul(S[:, 0:T], Wt("ffx", 2 * ch), xn[:, :], start=True, stop=True)
                pe.matmul(S[:, T:], Wt("ffx", 2 * ch + 1), xn[:, :], start=True, stop=True)\
                  .then_inc(*c.give("big_hidden"))
                yield 1
            pe.wait_ge(*c.next("big_contextT_taken"))
            for u in range(4):
                for c2 in range(2):
                    rhs = otx[:, u, :].rearrange("p (b c q) -> p b c q", b=BT, c=2)[:, :, c2, :]
                    pe.matmul(TP[:, 0:T], Wt("ox", 2 * u + c2), rhs, start=(u + c2 == 0), stop=False)
            for ch in range(4):
                if ch >= 2:
                    pe.wait_ge(*c.next("big_hidden_done"))
                mm = pe.matmul(TP[:, 0:T], Wt("ff2x", ch), fact[:, ch, :], start=False, stop=(ch == 3))
            mm.then_inc(*c.give("projected"))
            yield 4

        def wide_act(c):
            a = nc.scalar
            a.wait_ge(*c.next("big_proj_k"))
            a.activation(qk[:, T:], OY[:, 0:T], ACT.Copy).then_inc(*c.give("big_k_taken"))
            a.wait_ge(*c.next("big_proj_q"))
            a.activation(qx[:, 0, :, :, :], by_chunk(SA), ACT.Copy, scale=0.125)\
             .then_inc(*c.give("big_q_heads"))
            c.next("big_proj_q")
            yield
            a.wait_ge(*c.next("big_proj_q"))
            a.activation(qx[:, 2, :, :, :], by_chunk(SA), ACT.Copy, scale=0.125)\
             .then_inc(*c.give("big_q_heads"))
            c.next("big_proj_q")
            yield
            for k in range(6):
                yield
                yield
                if k < 4:
                    a.wait_ge(*c.next("big_shifted"))
                    a.activation(probs[:, k % 2, :], probs[:, k % 2, :], ACT.Exp).then_inc(*c.give("big_exped"))
                if k >= 2:
                    a.wait_ge(*c.next("big_context"))
                    a.activation(otx[:, k - 2, :], OY[:, :], ACT.Copy).then_inc(*c.give("big_contextT_taken"))
                yield
                if 1 <= k < 5:
                    a.wait_ge(*c.next("big_probsT"))
                    a.activation(probsT[:, (k - 1) % 2, :], TP[:, :], ACT.Copy).then_inc(*c.give("big_probsT_taken"))
                yield
            for ch in range(4):
                a.wait_ge(*c.next("big_hidden"))
                a.activation(fx[:, ch % 2, :], (SA, SB)[ch % 2][:, T:], ACT.Tanh, scale=0.5)\
                 .then_inc(*c.give("big_hidden_tanh"))
                yield
            a.wait_ge(*c.next("projected"))
            a.activation(upd[:, :], TP[:, 0:T], ACT.Copy, scale=tg[:, 2:3]).then_inc(*c.give("gated"))
            yield

        def wide_dve(c):
            dve = nc.vector
            dve.wait_ge(*c.next("big_proj_v"))
            for h in range(2):
                r = slice(64 * h, 64 * h + 64)
                v = dve.tensor_copy(vdiag[r, :, 64 * h:64 * h + 64], TP[r, 0:T].rearrange("p (b d) -> p b d", b=BT))
            v.then_inc(*c.give("big_v_blocks"))
            for p in (1, 3):
                c.next("big_proj_q")
                dve.wait_ge(*c.next("big_proj_q"))
                dve.tensor_scalar(qx[:, p, :, :, :], by_chunk(SB), 0.125, None,
                                  ALU.mult).then_inc(*c.give("big_q_heads_dve"))
                yield
            def added(k):
                p4 = probs[:, k % 2, :].rearrange("p (b m k) -> p b m k", b=BT, m=2)
                dve.wait_ge(*c.next("big_scores"))
                if k >= 2:
                    dve.wait_ge(*c.next("big_probsT"))
                mk = addmask.rearrange("p (b k) -> p b k", b=BT).unsqueeze(2).to_broadcast([P, BT, 2, SEQ])
                dve.tensor_tensor(p4, (SA, SB)[k % 2][:, :].rearrange("p (b m k) -> p b m k", b=BT, m=2), mk, ALU.add)\
                   .then_inc(*c.give("big_added"))
                dve.wait_ge(*c.next("big_added"))
                p3 = probs[:, k % 2, :].rearrange("p (a k) -> p a k", k=SEQ)
                link(c, dve.tensor_reduce(mx[:, k % 2, :], p3, AX.X, ALU.max))

            def shifted(k):
                p3 = probs[:, k % 2, :].rearrange("p (a k) -> p a k", k=SEQ)
                dve.tensor_tensor(p3, p3, mx[:, k % 2, :].unsqueeze(2).to_broadcast([P, 8, SEQ]), ALU.subtract)\
                   .then_inc(*c.give("big_shifted"))

            def normed(k):
                p3 = probs[:, k % 2, :].rearrange("p (a k) -> p a k", k=SEQ)
                s8 = mx[:, k % 2, :]
                dve.wait_ge(*c.next("big_exped"))
                link(c, dve.tensor_reduce(s8, p3, AX.X, ALU.add))
                link(c, dve.reciprocal(s8, s8))
                dve.tensor_tensor(p3, p3, s8.unsqueeze(2).to_broadcast([P, 8, SEQ]), ALU.mult)\
                   .then_inc(*c.give("big_probs_normed"))

            for k in range(6):
                if k < 4:
                    added(k)
                yield
                if k < 4:
                    shifted(k)
                yield
                if 1 <= k < 5:
                    normed(k - 1)
                yield
                yield
            for ch in range(4):
                S = (SA, SB)[ch % 2]
                dve.wait_ge(*c.next("big_hidden_tanh"))
                link(c, dve.scalar_tensor_tensor(out=fx[:, ch % 2, :], in0=fx[:, ch % 2, :], scalar=1.0, in1=S[:, T:],
                                                 op0=ALU.add, op1=ALU.mult))
                dve.scalar_tensor_tensor(out=fact[:, ch, :], in0=fx[:, ch % 2, :], scalar=0.5, in1=S[:, 0:T],
                                         op0=ALU.mult, op1=ALU.mult).then_inc(*c.give("big_hidden_done"))
                yield
            dve.wait_ge(*c.next("gated"))
            dve.tensor_tensor(xF, xF, upd[:, :], ALU.add).then_inc(*c.give("x_new"))
            yield

        def route_pe(c, src, kind, gate, nearest=False):
            pe = nc.tensor
            yield from norm_pe(c, MNORM, kind, src)
            pe.wait_ge(*c.next("m_normed"))
            if nearest:
                pe.wait_ge(*c.next("m_rowsq"))
            for s in range(2):
                o = H1[:, s * NE:(s + 1) * NE]
                t = slice(s * P, (s + 1) * P)
                mm = pe.matmul(o, my[:, t], gate, start=True, stop=not nearest)
                if nearest:
                    pe.matmul(o, msq[:, t], negones[:, :], start=False, stop=False)
                    mm = pe.matmul(o, C("mean"), centsq[:, :], start=False, stop=True)
            mm.then_inc(*c.give("m_logits"))
            yield 1
            yield 1
            pe.wait_ge(*c.next("m_comb"))
            for s in range(2):
                mm = pe.transpose(H0[0:NE, s * P:(s + 1) * P], comb[:, s, :], C("ident"))
            mm.then_inc(*c.give("m_combT"))
            yield 1

        def route_act(c, src, kind, nearest=False):
            a = nc.scalar
            yield from norm_act(c, MNORM, kind, src)
            if nearest:
                a.wait_ge(*c.next("m_normed"))
                a.activation(msq[:, :], my[:, :], ACT.Square).then_inc(*c.give("m_rowsq"))
            yield
            if not nearest:
                a.wait_ge(*c.next("m_gap"))
                a.activation(gapx[:, :], gap[:, :], ACT.Exp).then_inc(*c.give("m_gap_exp"))
            yield
            a.wait_ge(*c.next("m_combT"))
            a.activation(combT[:, :], H0[0:NE, 0:T], ACT.Copy, scale=0.5).then_inc(*c.give("m_combT_taken"))
            yield

        def route_pool(c, kind):
            yield from norm_pool(c, MNORM, kind)
            yield from idle(3)

        def route_dve(c, src, kind, g, b=None, nearest=False):
            dve = nc.vector
            lk = lambda ins: link(c, ins, "m_chain")
            yield from norm_dve(c, MNORM, kind, src, y=my[:, :], g=g, b=b, eps2=1e-6)
            dve.wait_ge(*c.next("m_logits"))
            lk(dve.tensor_copy(lg[:, :, :].rearrange("p s e -> p (s e)"), H1[:, 0:2 * NE]))
            dve.max(top[:, 0, :], lg[:, 0, :])
            lk(dve.max(top[:, 1, :], lg[:, 1, :]))
            if not nearest:
                dve.tensor_tensor(gap[:, :], top[:, :, 1], top[:, :, 0], ALU.subtract).then_inc(*c.give("m_gap"))
            dve.max_index(topi[:, 0, :], top[:, 0, :], lg[:, 0, :])
            lk(dve.max_index(topi[:, 1, :], top[:, 1, :], lg[:, 1, :]))
            lk(dve.tensor_copy(topf[:, :, :], topi[:, :, :]))
            yield
            iota = C("iota8").unsqueeze(1).to_broadcast([P, 2, NE])
            if nearest:
                dve.tensor_tensor(comb[:, :, :], iota, topf[:, :, 0:1].to_broadcast([P, 2, NE]), ALU.is_equal)\
                   .then_inc(*c.give("m_comb"))
                yield
                yield
                return
            dve.wait_ge(*c.next("m_gap_exp"))
            lk(dve.tensor_scalar(w01[:, 0, :], gapx[:, :], 1.0, None, ALU.add))
            lk(dve.reciprocal(w01[:, 0, :], w01[:, 0, :]))
            dve.tensor_tensor(w01[:, 1, :], gapx[:, :], w01[:, 0, :], ALU.mult)
            for i in range(2):
                last = dve.tensor_tensor(pick[:, i, :, :], iota, topf[:, :, i:i + 1].to_broadcast([P, 2, NE]), ALU.is_equal)
            lk(last)
            for i in range(2):
                last = dve.tensor_tensor(pick[:, i, :, :], pick[:, i, :, :],
                                         w01[:, i, :].unsqueeze(2).to_broadcast([P, 2, NE]), ALU.mult)
            lk(last)
            dve.tensor_tensor(comb[:, :, :], pick[:, 0, :, :], pick[:, 1, :, :], ALU.add).then_inc(*c.give("m_comb"))
            yield
            yield

        def weights_sp(c, free, steps):
            sp = nc.sync
            sp.wait_ge(*c.next("m_combT_taken"))
            for e in range(NE):
                if e >= 2:
                    c.skip(free, steps)
                    sp.wait_ge(c.sems[free], c.seen[free])
                sem, _ = c.give(("m_weight_even", "m_weight_odd")[e % 2])
                sp.dma_start(wexp[:, e % 2, :], combT[e:e + 1, :].unsqueeze(1).to_broadcast([1, P, T])).then_inc(sem, 16)

        def wait_weights(c, engine, e):
            sem, n = c.next(("m_weight_even", "m_weight_odd")[e % 2])
            engine.wait_ge(sem, 16 * n)

        N1 = NE * 2

        def gelu_pe(c):
            pe = nc.tensor
            for n in range(N1 + 3):
                if n == 0:
                    pe.wait_ge(*c.next("m_combT_taken"))
                    pe.matmul(YM[:, 0:T], b2x2[:, :], combT[:, :], start=True, stop=False)
                for i in range(2):
                    if n < N1:
                        if n >= 3 and i == 0:
                            pe.wait_ge(*c.next("m_up_free"))
                        mm = pe.matmul(H[n % 3][:, i * T:(i + 1) * T], Wt("up1", 2 * n + i), my[:, :],
                                       start=True, stop=True)
                        if i == 1:
                            mm.then_inc(*c.give("m_up"))
                    yield 1 if n < N1 else 0
                for i in range(2):
                    if n >= 3:
                        if i == 0:
                            pe.wait_ge(*c.next("m_act"))
                        mm = pe.matmul(YM[:, 0:T], Wt("dn1", 2 * (n - 3) + i), act[:, n % 3, i * T:(i + 1) * T],
                                       start=False, stop=(n == N1 + 2 and i == 1))
                        if i == 1:
                            mm.then_inc(*c.give("m_down"))
                    yield 1 if n >= 3 else 0
            yield

        def gelu_act(c):
            a = nc.scalar
            for n in range(N1 + 3):
                yield
                yield
                if n < N1:
                    if n >= 3:
                        a.wait_ge(*c.next("m_act"))
                    a.wait_ge(*c.next("m_up"))
                    for i in range(2):
                        h = a.activation(hb[:, n % 3, i * T:(i + 1) * T], H[n % 3][:, i * T:(i + 1) * T], ACT.Identity,
                                         bias=V("b1", 2 * n + i))
                    h.then_inc(*c.give("m_up_free"))
                    a.wait_ge(*c.next("m_up_free"))
                    a.activation(hp[:, n % 3, :], hb[:, n % 3, :], ACT.Square).then_inc(*c.give("m_square"))
                yield
                if 1 <= n <= N1:
                    a.wait_ge(*c.next("m_cubic"))
                    a.activation(hp[:, (n - 1) % 3, :], hp[:, (n - 1) % 3, :], ACT.Tanh, scale=GELU_C)\
                     .then_inc(*c.give("m_tanh"))
                yield
            yield

        def gelu_pool(c):
            for n in range(N1 + 3):
                yield
                if n < N1:
                    nc.gpsimd.wait_ge(*c.next("m_square"))
                    nc.gpsimd.tensor_scalar(hp[:, n % 3, :], hp[:, n % 3, :], 0.044715, 1.0, ALU.mult, ALU.add)\
                             .then_inc(*c.give("m_poly"))
                yield
                yield
                yield
            yield

        def gelu_dve(c):
            dve = nc.vector
            for n in range(N1 + 3):
                if 1 <= n <= N1:
                    dve.wait_ge(*c.next("m_poly"))
                    dve.tensor_tensor(hp[:, (n - 1) % 3, :], hp[:, (n - 1) % 3, :], hb[:, (n - 1) % 3, :], ALU.mult)\
                       .then_inc(*c.give("m_cubic"))
                yield
                if 2 <= n <= N1 + 1:
                    m = n - 2
                    dve.wait_ge(*c.next("m_tanh"))
                    link(c, dve.scalar_tensor_tensor(out=hp[:, m % 3, :], in0=hp[:, m % 3, :], scalar=1.0,
                                                     in1=hb[:, m % 3, :], op0=ALU.add, op1=ALU.mult), "m_chain")
                    if m % 2 == 0:
                        wait_weights(c, dve, m // 2)
                    if m >= 3:
                        dve.wait_ge(*c.next("m_down"))
                    dve.tensor_tensor(act[:, m % 3, :].rearrange("p (i t) -> p i t", i=2),
                                      hp[:, m % 3, :].rearrange("p (i t) -> p i t", i=2),
                                      wexp[:, m // 2 % 2, :].unsqueeze(1).to_broadcast([P, 2, T]), ALU.mult)\
                       .then_inc(*c.give("m_act"))
                yield
                yield
                yield
            finish_dve(c, N1, hF[:, :], 5, xF)
            yield

        def finish_dve(c, steps, skip, gate, x):
            dve = nc.vector
            have = c.seen.get("m_down", 0)
            for _ in range(steps - have):
                last = c.next("m_down")
            dve.wait_ge(*last)
            link(c, dve.tensor_tensor(msq[:, :], YM[:, 0:T], skip, ALU.add), "m_chain")
            dve.scalar_tensor_tensor(out=x, in0=msq[:, :], scalar=tg[:, gate:gate + 1], in1=x, op0=ALU.mult,
                                     op1=ALU.add).then_inc(*c.give("m_out"))

        def glu_pe(c, up, down, chunks):
            pe = nc.tensor
            N = NE * chunks

            for n in range(N + 3):
                e, ch = divmod(n, chunks)
                S = H[n % 3]
                if n == 0:
                    pe.wait_ge(*c.next("m_combT_taken"))
                if n < N:
                    if n >= 3:
                        pe.wait_ge(*c.next("m_up_free"))
                    pe.matmul(S[:, 0:T], Wt(up, 2 * n), my[:, :], start=True, stop=True)
                yield 1
                if n >= 3:
                    pe.wait_ge(*c.next("m_act"))
                    pe.matmul(YM[:, 0:T], Wt(down, n - 3), act[:, n % 3, 0:T], start=(n == 3), stop=(n == N + 2))\
                      .then_inc(*c.give("m_down"))
                yield 1 if n >= 3 else 0
                if n < N:
                    if ch == 0:
                        pe.wait_ge(*c.next("m_weight_taken"))
                    pe.matmul(S[:, T:], Wt(up, 2 * n + 1), hp[:, e % 2, T:], start=True, stop=True)\
                      .then_inc(*c.give("m_up"))
                yield 1
            yield

        def glu_act(c, chunks):
            a = nc.scalar
            for n in range(NE * chunks + 3):
                if 1 <= n <= NE * chunks:
                    m = n - 1
                    if m >= 3:
                        a.wait_ge(*c.next("m_act"))
                    a.wait_ge(*c.next("m_up"))
                    a.activation(hb[:, m % 3, :], H[m % 3][:, :], ACT.Copy).then_inc(*c.give("m_up_free"))
                yield
                if 1 <= n <= NE * chunks:
                    m = n - 1
                    a.wait_ge(*c.next("m_up_free"))
                    a.activation(hp[:, m % 3, 0:T], hb[:, m % 3, 0:T], ACT.Tanh, scale=0.5).then_inc(*c.give("m_tanh"))
                yield
                yield
            yield

        def glu_dve(c, chunks, skip, gate):
            dve = nc.vector
            N = NE * chunks

            def weigh_input(e):
                wait_weights(c, dve, e)
                dve.tensor_tensor(hp[:, e % 2, T:], wexp[:, e % 2, :], my[:, :], ALU.mult)\
                   .then_inc(*c.give("m_weight_taken"))

            for n in range(N + 3):
                if n == 0:
                    weigh_input(0)
                yield
                yield
                if 1 <= n <= N:
                    e, ch = divmod(n - 1, chunks)
                    m = n - 1
                    dve.wait_ge(*c.next("m_tanh"))
                    link(c, dve.scalar_tensor_tensor(out=hp[:, m % 3, 0:T], in0=hp[:, m % 3, 0:T], scalar=1.0,
                                                     in1=hb[:, m % 3, 0:T], op0=ALU.add, op1=ALU.mult), "m_chain")
                    if m >= 3:
                        dve.wait_ge(*c.next("m_down"))
                    dve.tensor_tensor(act[:, m % 3, 0:T], hp[:, m % 3, 0:T], hb[:, m % 3, T:], ALU.mult)\
                       .then_inc(*c.give("m_act"))
                    if ch == 0 and e + 1 < NE:
                        weigh_input(e + 1)
                yield
            finish_dve(c, N, skip, gate, xS[:, :])
            yield

        def idle(slots):
            for _ in range(slots):
                yield

        LAYER, BOTH = 3, 4
        HEADS, SINGLE, FF0, WIDE = 18, 6, 1, 31
        bk = lambda l: (lambda i: bk4[:, l, i:i + 1])
        causal = C("causal")

        def f1_pe(c):
            yield from norm_pe(c, ANORM, "layer", xF)
            yield from single_pe(c)
            yield from norm_pe(c, ANORM, "both", xF, fresh=True)
            yield from heads_pe(c, Wt("qa"), Wt("ka"), Wt("va"), Wt("oa"), xn[:, :], xn[:, :], inner=True)

        def f1_act(c):
            yield from norm_act(c, ANORM, "layer")
            yield from single_act(c)
            yield from norm_act(c, ANORM, "both")
            yield from heads_act(c, bk(1))

        def f1_dve(c):
            yield from norm_dve(c, ANORM, "layer")
            yield from single_dve(c)
            yield from norm_dve(c, ANORM, "both", y=xn[:, :], g=V("ln1w"), b=V("ln1b"), eps2=1e-5)
            yield from heads_dve(c, V("bqa"), None, None, inner=(hF[:, :], un[:, 0:T], bo[:, 2:3]))

        def f1_pool(c):
            yield from norm_pool(c, ANORM, "layer")
            yield from idle(SINGLE)
            yield from norm_pool(c, ANORM, "both")
            yield from idle(HEADS)

        def s1_pe(c):
            yield from route_pe(c, hS[:, :], "rms", V("router2", 0, NE))
            yield from glu_pe(c, "up2", "dn2", 3)

        def s1_act(c):
            yield from route_act(c, hS[:, :], "rms")
            yield from glu_act(c, 3)

        def s1_dve(c):
            yield from route_dve(c, hS[:, :], "rms", V("g2"))
            yield from glu_dve(c, 3, hS[:, :], 6)

        def n2_pe(c, fresh):
            yield from norm_pe(c, ANORM, "layer", xN, fresh=fresh)
            yield from heads_pe(c, Wt("q0"), Wt("k0"), Wt("v0"), Wt("o0"), un[:, 0:T], ctxN)
            yield from norm_pe(c, ANORM, "layer", xN, fresh=True)
            yield from ff0_pe(c)

        def n2_act(c):
            yield from norm_act(c, ANORM, "layer")
            yield from heads_act(c, bk(0), gate=(tg[:, 0:1], bog[:, 0:1]))
            yield from norm_act(c, ANORM, "layer")
            yield from ff0_act(c)

        def n2_dve(c):
            flat = maskA[:, :, :].rearrange("p b k -> p (b k)")
            link(c, nc.vector.tensor_scalar(flat, stage_i[:, IM0:IM0 + 2 * SEQ], 0.0, 0.5, ALU.is_equal, ALU.subtract))
            link(c, nc.vector.tensor_scalar(flat, flat, -2e9, None, ALU.mult))
            yield from norm_dve(c, ANORM, "layer")
            yield from heads_dve(c, V("bq0"), maskA[:, :, :], xN)
            yield from norm_dve(c, ANORM, "layer")
            yield from ff0_dve(c)

        def n2_pool(c):
            yield from norm_pool(c, ANORM, "layer")
            yield from idle(HEADS)
            yield from norm_pool(c, ANORM, "layer")
            yield from idle(FF0)

        def s2_pe(c):
            yield from norm_pe(c, ANORM, "layer", xS[:, :])
            yield from heads_pe(c, Wt("q3"), Wt("k3"), Wt("v3"), Wt("o3"), un[:, 0:T], ctxS[:, :])

        def s2_act(c):
            yield from norm_act(c, ANORM, "layer")
            yield from heads_act(c, bk(2), gate=(tg[:, 3:4], bog[:, 3:4]))

        def s2_dve(c):
            link(c, nc.vector.tensor_tensor(maskA[:, :, :], causal.unsqueeze(1).to_broadcast([P, 2, SEQ]),
                                            rowS[:, :].unsqueeze(2).to_broadcast([P, 2, SEQ]), ALU.min))
            yield from norm_dve(c, ANORM, "layer")
            yield from heads_dve(c, V("bq3"), maskA[:, :, :], xS[:, :])

        def f2_pe(c):
            yield from route_pe(c, hF[:, :], "layer", V("gate1", 0, NE))
            yield from gelu_pe(c)

        def f2_act(c):
            yield from route_act(c, hF[:, :], "layer")
            yield from gelu_act(c)

        def f2_pool(c):
            yield from route_pool(c, "layer")
            yield from gelu_pool(c)

        def f2_dve(c):
            yield from route_dve(c, hF[:, :], "layer", V("ln2w"), V("ln2b"))
            yield from gelu_dve(c)

        def f3_pe(c):
            yield from norm_pe(c, ANORM, "both", xF, second=ctxF)
            yield from wide_pe(c)
            yield from norm_pe(c, ANORM, "both", xF, fresh=True)
            yield from heads_pe(c, Wt("q2"), Wt("k2"), Wt("v2"), Wt("o2"), xn[:, :], xn[:, :],
                                rope=(Wt("qr2"), Wt("kr2")), inner=True)

        def f3_act(c):
            yield from norm_act(c, ANORM, "both", w=W2T)
            yield from wide_act(c)
            yield from norm_act(c, ANORM, "both")
            yield from heads_act(c, None, rope=True)

        def f3_dve(c):
            yield from norm_dve(c, ANORM, "both", y=xn[:, :], g=V("lng"), b=V("lnb"), eps2=1e-5, w=W2T,
                                ctx_gb=(V("clng"), V("clnb")))
            yield from wide_dve(c)
            yield from norm_dve(c, ANORM, "both", y=xn[:, :], g=V("g1"), eps2=1e-6)
            yield from heads_dve(c, None, causal, None, inner=(hF[:, :], un[:, 0:T], 0.0), rope=True)

        def s3_pe(c):
            yield from route_pe(c, xS[:, :], "both", cent2[:, :], nearest=True)
            yield from glu_pe(c, "up3", "dn3", 2)

        def s3_act(c):
            yield from route_act(c, xS[:, :], "both", nearest=True)
            yield from glu_act(c, 2)

        def s3_dve(c):
            yield from route_dve(c, xS[:, :], "both", V("scale3"), nearest=True)
            yield from glu_dve(c, 2, mu[:, :], 7)

        def s1_pool(c):
            yield from route_pool(c, "rms")
            yield from idle(3 * (NE * 3 + 3) + 1)

        def s2_pool(c):
            yield from norm_pool(c, ANORM, "layer")
            yield from idle(HEADS)

        def f3_pool(c):
            yield from norm_pool(c, ANORM, "both", W2T)
            yield from idle(WIDE)
            yield from norm_pool(c, ANORM, "both")
            yield from idle(HEADS)

        def s3_pool(c):
            yield from route_pool(c, "both")
            yield from idle(3 * (NE * 2 + 3) + 1)

        def gelu_sp(c):
            weights_sp(c, "m_act", 2)

        def glu_sp(c):
            weights_sp(c, "m_weight_taken", 1)

        def after(a, b):
            def run(c):
                yield from a(c)
                yield from b(c)
            return run if a and b else a or b

        def phase_halves(which, first, second, following):
            if which == 1:
                return (first and (f1_pe, f1_act, f1_dve, f1_pool)), (second and (s1_pe, s1_act, s1_dve, s1_pool, glu_sp))
            if which == 3:
                return (first and (f3_pe, f3_act, f3_dve, f3_pool)), (second and (s3_pe, s3_act, s3_dve, s3_pool, glu_sp))
            s2 = (s2_pe, s2_act, s2_dve, s2_pool) if second else 4 * (None,)
            n2 = (lambda c: n2_pe(c, fresh=second), n2_act, n2_dve, n2_pool) if following else 4 * (None,)
            attn = (second or following) and [after(a, b) for a, b in zip(s2, n2)]
            return attn, (first and (f2_pe, f2_act, f2_dve, f2_pool, gelu_sp))

        def clear_resting(parity):
            nums = sorted(s.num for s in sets[1 - parity].values())
            assert nums == list(range(nums[0], nums[0] + len(nums)))
            nc.gpsimd.sem_clear(range(nums[0], nums[-1] + 1))

        def handoff(parity, first, second, load=None):
            sems = sets[parity]
            with nc.Block() as block:
                @block.gpsimd
                def _(pool):
                    clear_resting(parity)
                    if second:
                        nc.gpsimd.tensor_copy(ctxS[:, :], ctxF).then_inc(sems["x_new"], 1)
                        pool.wait_ge(sems["x_new"], 1)
                    if first:
                        if second:
                            pool.wait_ge(sems["normed"], 1)
                        nc.gpsimd.tensor_copy(tile_f[:, :], stage_f[:, :])

                @block.vector
                def _(dve):
                    c = Counts(sems)
                    if second:
                        dve.tensor_copy(xS[:, :], xF).then_inc(sems["normed"], 1)
                        dve.tensor_copy(hS[:, :], hF[:, :])
                        link(c, dve.tensor_copy(rowS[:, :], rowF[:, :]))
                    if first:
                        dve.tensor_scalar(mask1[:, 0, :], stage_i[:, IM1:IM1 + P], 0.0, None, ALU.not_equal)
                        dve.tensor_scalar(mask1[:, 1, :], stage_i[:, IM1:IM1 + P], 0.0, -10000.0, ALU.is_equal, ALU.mult)
                        link(c, dve.tensor_scalar(rowF[:, :], stage_i[:, IM3:IM3 + 2], 0.0, 0.5, ALU.is_equal,
                                                  ALU.subtract))
                        dve.tensor_scalar(rowF[:, :], rowF[:, :], -2e9, None, ALU.mult)

        def phase(which, first, second, following=False, load_at=None, store_at=None, need_weights=()):
            parity = 0 if which == 2 else 1
            attn, moe = phase_halves(which, first, second, following)
            sems = sets[parity]
            order = []

            def run(engine):
                gens = [half[engine](Counts(sems)) if half else None for half in (attn, moe)]
                if engine == 0:
                    order.extend(choose_order(*gens, PACE[which]))
                else:
                    side_by_side(*gens, order)

            with nc.Block() as block:
                @block.tensor
                def _(pe):
                    for g in need_weights:
                        pe.wait_ge(dma_w[g], 16)
                    run(0)

                @block.scalar
                def _(a):
                    run(1)

                @block.vector
                def _(dve):
                    run(2)

                @block.gpsimd
                def _(pool):
                    clear_resting(parity)
                    run(3)

                @block.sync
                def _(sp):
                    if load_at is not None:
                        sp.dma_start(stage_f[:, :], fin[:, bass.ds(load_at * FCOLS, FCOLS)]).then_inc(sems["tile_in"], 16)
                        sp.dma_start(stage_i[:, :], iin[:, bass.ds(load_at * ICOLS, ICOLS)]).then_inc(sems["tile_in"], 16)
                        sp.wait_ge(sems["tile_in"], 32)
                    if moe:
                        moe[4](Counts(sems))
                    if store_at is not None:
                        sp.wait_ge(sems["m_out"], 1)
                        sp.dma_start(out[:, bass.ds(store_at * T, T)], xS[:, :]).then_inc(sems["out_store"], 16)
                        sp.wait_ge(sems["out_store"], 16)

        def setup():
            with nc.Block() as block:
                @block.sync
                def _(sp):
                    sp.dma_start(vsb[:, :], vecs).then_inc(dma_vec, 16)
                    sp.dma_start(wsb["early"][:, :], weights["early"]).then_inc(dma_w["early"], 16)
                    sp.dma_start(csb[:, :], consts).then_inc(dma_const, 16)
                    sp.dma_start(stage_f[:, :], fin[:, 0:FCOLS]).then_inc(dma_first, 16)
                    sp.dma_start(stage_i[:, :], iin[:, 0:ICOLS]).then_inc(dma_first, 16)
                    sp.dma_start(wsb["ff0"], weights["ff0"]).then_inc(dma_w["ff0"], 16)
                    for g, _ in W_PARTS[2:]:
                        sp.dma_start(wsb[g][:, :], weights[g]).then_inc(dma_w[g], 16)
                    sp.wait_ge(dma_const, 16)
                    sp.wait_ge(dma_first, 32)

                @block.scalar
                def _(a):
                    a.wait_ge(dma_vec, 16)
                    a.activation(tg[:, :], V("gx", 0, 8), ACT.Tanh).then_inc(setup_tanh, 1)
                    a.wait_ge(setup_pe, 2)
                    a.activation(a12, SA[:, 0:P], ACT.Copy).then_inc(setup_act, 1)
                    a.wait_ge(setup_pe, 3)
                    a.activation(ff0[:, :], SB[:, 0:P], ACT.Copy)

                @block.tensor
                def _(pe):
                    pe.wait_ge(dma_vec, 16)
                    pe.wait_ge(dma_w["early"], 16)
                    pe.wait_ge(dma_w["ff0"], 16)
                    for l, (w, b) in enumerate((("o0", "bv0"), ("o1", "bv1"), ("oa", "bva"))):
                        mm = pe.matmul(OY[:, l:l + 1], Wt(w), V(b), start=True, stop=True)
                    mm.then_inc(setup_pe, 1)
                    pe.matmul(SA[:, 0:P], Wt("a1T"), Wt("a2"), start=True, stop=True).then_inc(setup_pe, 1)
                    pe.wait_ge(setup_act, 1)
                    pe.matmul(SB[:, 0:P], Wt("wT"), a12, start=True, stop=True).then_inc(setup_pe, 1)

                @block.vector
                def _(dve):
                    dve.memset(vdiag[:, :, :], 0.0)
                    dve.memset(negones[:, :], -1.0)
                    dve.memset(neghalf[:, :], -0.5)
                    dve.wait_ge(dma_vec, 16)
                    dve.tensor_scalar(cent2[:, :], V("cent", 0, NE), 2.0, None, ALU.mult)
                    dve.scalar_tensor_tensor(out=centsq[:, :], in0=V("cent", 0, NE), scalar=-float(P), in1=V("cent", 0, NE),
                                             op0=ALU.mult, op1=ALU.mult)
                    dve.tensor_scalar(b2x2[:, :], V("b2", 0, P)[0:NE, :], 2.0, None, ALU.mult)
                    dve.wait_ge(setup_pe, 1)
                    for l, b in enumerate(("bo0", "bo1", "boa")):
                        last = dve.tensor_tensor(bo[:, l:l + 1], OY[:, l:l + 1], V(b), ALU.add)
                    last.then_inc(setup_dve, 1)
                    dve.wait_ge(setup_dve, 1)
                    dve.wait_ge(setup_tanh, 1)
                    dve.tensor_tensor(bog[:, 0:2], bo[:, 0:2], tg[:, 0:2], ALU.mult)
                    dve.wait_ge(dma_const, 16)
                    a, _ = cplace["headsel"]
                    for l, b in enumerate(("bk0", "bka", "bk3")):
                        dve.tensor_scalar(bk4[:, l, :], csb[:, a:a + 4], V(b), None, ALU.mult)

        def setup_late():
            with nc.Block() as block:
                @block.gpsimd
                def _(pool):
                    clear_resting(1)

                @block.tensor
                def _(pe):
                    pe.wait_ge(dma_w["late"], 16)
                    pe.matmul(OY[:, 3:4], Wt("o3"), V("bv3"), start=True, stop=True).then_inc(late_pe, 1)

                @block.vector
                def _(dve):
                    dve.wait_ge(late_pe, 1)
                    dve.tensor_tensor(bo[:, 3:4], OY[:, 3:4], V("bo3"), ALU.add).then_inc(late_dve, 1)
                    dve.wait_ge(late_dve, 1)
                    dve.tensor_tensor(bog[:, 3:4], bo[:, 3:4], tg[:, 3:4], ALU.mult)

        setup()
        phase(2, False, False, following=True)
        setup_late()
        handoff(0, True, False)
        phase(1, True, False, load_at=1)
        phase(2, True, False, following=True, need_weights=("moe1",))
        phase(3, True, False, need_weights=("mid",))
        with nc.Fori(1, NT) as i:
            handoff(0, True, True)
            phase(1, True, True, load_at=i + 1, need_weights=("moe2",))
            phase(2, True, True, following=True, need_weights=("late",))
            phase(3, True, True, store_at=i - 1, need_weights=("moe3",))
        handoff(0, False, True)
        phase(1, False, True)
        phase(2, False, True)
        phase(3, False, True, store_at=NT - 1)


def _constants():
    p = np.arange(P)
    ident = np.eye(P, dtype=np.float32)
    d = p % DK
    inv = 1.0 / 10000.0 ** (np.arange(0, DK, 2, dtype=np.float32) / DK)
    ang = np.einsum("i,j->ij", np.arange(SEQ, dtype=np.float32), inv)[:, d % 4].T.astype(np.float32)
    cos, sin = np.cos(ang), np.sin(ang) * np.where(d < 4, -1.0, 1.0)[:, None]
    q, k = p % SEQ, np.arange(SEQ)
    parts = {
        "ident": ident, "center": ident - 1.0 / P, "mean": np.full((P, P), 1.0 / P),
        "cos": cos, "sin": sin,
        "causal": np.where(k[None, :] > q[:, None], -3e38, 3e38),
        "headsel": np.where((p % 32 // DK)[:, None] == np.arange(4)[None, :], DK ** -0.5, 0.0),
        "halves": np.where((p // SEQ)[:, None] == (np.arange(32) // DK % 2)[None, :], 1.0, 0.0),
        "iota8": np.tile(np.arange(NE), (P, 1)),
    }
    return np.concatenate([parts[n].astype(np.float32) for n, _ in CONST_PARTS], axis=1)


def _rows(a):
    return a if a.shape[0] == P else np.concatenate([a, np.zeros((P - a.shape[0], *a.shape[1:]), a.dtype)])


def kernel(**inputs):
    import concourse.bacc as bacc
    from concourse.bass_utils import run_bass_kernel_spmd

    x = {k: np.asarray(v) for k, v in inputs.items()}
    col = lambda n: x[n].reshape(P, 1)
    across = lambda a: np.broadcast_to(a[None, :], (P, a.shape[0]))
    swap = lambda w: w.reshape(P, 16, 2, 4)[:, :, ::-1, :].reshape(P, P)
    experts = lambda w: w.transpose(1, 0, 2).reshape(P, -1)
    down = lambda w: w.reshape(NE, -1, P, P).transpose(2, 0, 1, 3).reshape(P, -1)
    pairs = lambda g, u: np.stack([g.reshape(NE, P, -1, P), u.reshape(NE, P, -1, P)], axis=3)\
        .transpose(1, 0, 2, 3, 4).reshape(P, -1)

    vec = {
        "gx": across(x["g_xattn"]), "gf": across(x["g_ffn"]),
        "bq0": col("L0_xattn_bq"), "bk0": col("L0_xattn_bk"), "bv0": col("L0_xattn_bv"),
        "bo0": col("L0_xattn_bo"), "bf0": col("L0_ffn_bias"),
        "bq1": col("L1_xattn_bq"), "bk1": col("L1_xattn_bk"), "bv1": col("L1_xattn_bv"), "bo1": col("L1_xattn_bo"),
        "ln1w": col("L1_ffn_ln1_w"), "ln1b": col("L1_ffn_ln1_b"), "ln2w": col("L1_ffn_ln2_w"), "ln2b": col("L1_ffn_ln2_b"),
        "bqa": x["L1_ffn_b_qkv"][0:P].reshape(P, 1), "bka": x["L1_ffn_b_qkv"][P:2 * P].reshape(P, 1),
        "bva": x["L1_ffn_b_qkv"][2 * P:].reshape(P, 1), "boa": col("L1_ffn_b_o"),
        "b1": x["L1_ffn_b1"].reshape(NE * 4, P).T, "g1": col("L2_ffn_g1"), "g2": col("L2_ffn_g2"),
        "lng": col("L2_xattn_ln_g"), "lnb": col("L2_xattn_ln_b"), "clng": col("L2_xattn_cln_g"), "clnb": col("L2_xattn_cln_b"),
        "bq3": col("L3_xattn_bq"), "bk3": col("L3_xattn_bk"), "bv3": col("L3_xattn_bv"),
        "bo3": col("L3_xattn_bo"), "scale3": col("L3_ffn_scale"), "cent": x["L3_ffn_centroids"].T,
        "gate1": x["L1_ffn_w_gate"], "router2": x["L2_ffn_w_router"], "b2": _rows(x["L1_ffn_b2"]),
    }
    qkv, kv, up3 = x["L1_ffn_w_qkv"], x["L2_xattn_Wkv"], x["L3_ffn_up_w"]
    mats = {
        "q0": x["L0_xattn_Wq"], "k0": x["L0_xattn_Wk"], "v0": x["L0_xattn_Wv"], "o0": x["L0_xattn_Wo"],
        "wT": x["L0_ffn_weight"].T, "a1T": x["L0_ffn_aux_weight1"].T, "a2": x["L0_ffn_aux_weight2"],
        "q1": x["L1_xattn_Wq"], "k1": x["L1_xattn_Wk"], "v1": x["L1_xattn_Wv"], "o1": x["L1_xattn_Wo"],
        "qa": qkv[:, 0:P], "ka": qkv[:, P:2 * P], "va": qkv[:, 2 * P:], "oa": x["L1_ffn_w_o"],
        "up1": experts(x["L1_ffn_w1"]), "dn1": down(x["L1_ffn_w2"]),
        "qx": x["L2_xattn_Wq"], "kx": np.concatenate([kv[:, 0:64], kv[:, 0:64]], axis=1), "vx": kv[:, 64:],
        "ox": x["L2_xattn_Wout"].reshape(2, 2, 2, 2, 64, P).transpose(1, 4, 3, 0, 2, 5).reshape(P, 8 * P),
        "ffx": x["L2_xattn_W1"].reshape(P, 2, 4, P).transpose(0, 2, 1, 3).reshape(P, 8 * P),
        "ff2x": x["L2_xattn_W2"].reshape(4, P, P).transpose(1, 0, 2).reshape(P, 4 * P),
        "q2": x["L2_ffn_wq"], "qr2": swap(x["L2_ffn_wq"]), "k2": x["L2_ffn_wk"], "kr2": swap(x["L2_ffn_wk"]),
        "v2": x["L2_ffn_wv"], "o2": x["L2_ffn_wo"],
        "up2": pairs(x["L2_ffn_wg"], x["L2_ffn_wu"]), "dn2": down(x["L2_ffn_wd"]),
        "q3": x["L3_xattn_Wq"].T, "k3": x["L3_xattn_Wk"].T, "v3": x["L3_xattn_Wv"].T, "o3": x["L3_xattn_Wo"].T,
        "up3": pairs(up3[:, :, 2 * P:], up3[:, :, 0:2 * P]), "dn3": down(x["L3_ffn_down_w"]),
    }
    tiles = lambda a: a.reshape(P, NT, -1)
    twice = lambda m: np.concatenate([m, m]).reshape(P, NT, -1)
    floats = np.concatenate([tiles(x["x"].reshape(-1, P).T), tiles(x["ctx_1024"].reshape(-1, P).T),
                             twice(x["mask_BxSxS2_ff0"].transpose(1, 0, 2))], axis=2)
    pairs_of = lambda m: m.reshape(NT, 2, 2, SEQ, -1).transpose(2, 3, 0, 1, 4).reshape(P, NT, -1)
    keys = x["mask_BxS2_ik0"]
    ints = np.concatenate([pairs_of(x["mask_Bx1xSxS2_ik1"]), pairs_of(np.repeat(keys[:, None, :], SEQ, axis=1)),
                           pairs_of(keys)], axis=2)
    floats = np.concatenate([floats, floats[:, 0:1]], axis=1).reshape(P, -1)
    ints = np.concatenate([ints, ints[:, 0:1]], axis=1).reshape(P, -1)

    arrays = {"fin": floats, "iin": ints, "consts": _constants(),
              "vecs": np.concatenate([vec[n] for n, _ in VEC_PARTS], axis=1)}
    for g, parts in W_PARTS:
        arrays[f"w_{g}"] = np.concatenate([mats[n] for n, _ in parts], axis=1)
    arrays = {f"in_{k}": np.ascontiguousarray(v) for k, v in arrays.items()}
    nc = bacc.Bacc("TRN2", target_bir_lowering=False, num_devices=1)
    aps = {k[3:]: nc.dram_tensor(k, v.shape, mybir.dt.from_np(v.dtype), kind="ExternalInput").ap()
           for k, v in arrays.items()}
    out = nc.dram_tensor("out_0", (P, NSEQ * SEQ), F32, kind="ExternalOutput").ap()
    build(nc, aps["fin"], aps["iin"], aps["consts"], aps["vecs"], {g: aps[f"w_{g}"] for g, _ in W_PARTS}, out)
    r = run_bass_kernel_spmd(nc, [arrays], core_ids=[0])
    y = r.results[0]["out_0"]
    return np.ascontiguousarray(y.T).reshape(NSEQ, SEQ, P)
```

```python
from contextlib import ExitStack

import concourse.bass as bass
import numpy as np
from concourse import mybir

F32 = mybir.dt.float32
I32 = mybir.dt.int32
U32 = mybir.dt.uint32
ALU = mybir.AluOpType
ACT = mybir.ActivationFunctionType
AX = mybir.AxisListType

P = 128
SEQ = 64
NSEQ = 32
BT = 4
T = BT * SEQ
NT = NSEQ // BT
W2T = 2 * T
NE = 8
DK = 8
VCOLS = 2 * DK + 2
GELU_C = float(np.sqrt(2.0 / np.pi))
GELU_CUBE = float(np.sqrt(0.044715))

FX, FC, FM, FCOLS = 0, T, 2 * T, 3 * T
IM0, IM1, IM3, ICOLS = 0, 2 * SEQ, 4 * SEQ, 4 * SEQ + 2


def columns(parts):
    at, place = 0, {}
    for name, n in parts:
        place[name] = (at, at + n)
        at += n
    return place, at


CONST_PARTS = [("ident", P), ("center", P), ("mean", P), ("cos", SEQ), ("sin", SEQ), ("causal", SEQ),
               ("headsel", 4), ("halves", 2 * DK), ("iota8", 8)]
VEC_PARTS = [("gx", 4), ("gf", 4), ("bq0", 1), ("bk0", 1), ("bv0", 1), ("bo0", 1), ("bf0", 1),
             ("bq1", 1), ("bk1", 1), ("bv1", 1), ("bo1", 1), ("ln1w", 1), ("ln1b", 1), ("ln2w", 1), ("ln2b", 1),
             ("bqa", 1), ("bka", 1), ("bva", 1), ("boa", 1), ("b1", NE * 4), ("g1", 1), ("g2", 1),
             ("lng", 1), ("lnb", 1), ("clng", 1), ("clnb", 1), ("bq3", 1), ("bk3", 1), ("bv3", 1), ("bo3", 1),
             ("scale3", 1), ("cent", NE), ("gate1", NE), ("router2", NE), ("b2", P)]
W_PARTS = [
    ("early", [("q0", P), ("k0", P), ("v0", P), ("o0", P),
               ("q1", P), ("k1", P), ("v1", P), ("o1", P), ("qa", P), ("ka", P), ("va", P), ("oa", P)]),
    ("ff0", [("wT", P), ("a1T", P), ("a2", P)]),
    ("moe1", [("up1", NE * 4 * P), ("dn1", NE * 4 * P)]),
    ("mid", [("qx", 8 * P), ("kx", P), ("vx", 64), ("ox", 8 * P), ("ffx", 8 * P), ("ff2x", 4 * P),
             ("q2", P), ("qr2", P), ("k2", P), ("kr2", P), ("v2", P), ("o2", P)]),
    ("moe2", [("up2", NE * 6 * P), ("dn2", NE * 3 * P)]),
    ("late", [("q3", P), ("k3", P), ("v3", P), ("o3", P)]),
    ("moe3", [("up3", NE * 4 * P), ("dn3", NE * 2 * P)]),
]

NORM_SIGNALS = ["centred", "squared", "copied", "meansq", "stat", "rooted", "spread", "normed",
                "chain"]
ATTN_SIGNALS = NORM_SIGNALS + [
    "context", "contextT", "contextT_taken", "context_normed", "exped", "q_taken", "probsT", "probsT_taken",
    "proj_k", "proj_q", "proj_v", "projected", "projected_inner", "k_heads", "scores", "shifted", "v_blocks",
    "x_new"]
FF_SIGNALS = ["ff_hidden", "ff_hidden_tanh"]
BIG_SIGNALS = ["big_" + name for name in (
    "added", "context", "contextT_taken", "exped", "hidden", "hidden_done", "hidden_tanh", "k_taken", "probsT",
    "probsT_taken", "probs_normed", "proj_k", "proj_q", "proj_v", "q_heads", "q_heads_dve", "scores", "shifted",
    "v_blocks")]
MOE_SIGNALS = ["m_" + name for name in NORM_SIGNALS + [
    "logits", "gap", "gap_exp", "comb", "combT", "combT_taken", "weight_even", "weight_odd", "up",
    "up_free", "tanh", "act", "down",
    "out"]]
GELU_SIGNALS = ["m_square", "m_cubic"]
GLU_SIGNALS = ["m_weight_taken", "m_rowsq"]


GAPS = {
    "norm": (2, 3, 4),
    "heads": (1, 4, 1, 2, 0, 4, 2, 4),
    "single": (1, 4, 4, 2, 3, 4),
    "ff0": (3,),
    "wide": (1, 3, 1, 2, 2, 0, 0, 4),
    "route": (0, 2, 1),
}
PACE = {1: 1.125, 2: 0.99, 3: 0.8}


def choose_order(attn, moe, pace):
    order, left = [], [attn is not None, moe is not None]
    due = 0
    while left[0] or left[1]:
        half = 1 if left[1] and (due > 0 or not left[0]) else 0
        got = next((attn, moe)[half], "end")
        if got == "end":
            left[half] = False
            continue
        order.append(half)
        due = due + pace * (got or 0) if half == 0 else due - (got or 0)
    return order


def side_by_side(attn, moe, order):
    halves = [attn, moe]
    for half in order:
        next(halves[half])
    for half in halves:
        if half is not None:
            assert next(half, "end") == "end", "a stream has more slots on this engine than on TensorE"


def build(nc, fin, iin, consts, vecs, weights, out):
    cplace, ccols = columns(CONST_PARTS)
    vplace, vcols = columns(VEC_PARTS)
    wplace = {}
    for group, parts in W_PARTS:
        place, _ = columns(parts)
        wplace.update({name: (group, *ab) for name, ab in place.items()})

    with ExitStack() as ctx:
        def sb(name, shape, dt=F32):
            return ctx.enter_context(nc.sbuf_tensor(name, shape, dt))

        def bank(name):
            return ctx.enter_context(nc.psum_tensor(name, [P, W2T], F32))

        def sem(name):
            return ctx.enter_context(nc.semaphore(name))

        csb = sb("csb", [P, ccols])
        vsb = sb("vsb", [P, vcols])
        wsb = {g: sb(f"w_{g}", [P, columns(parts)[1]]) for g, parts in W_PARTS if g != "ff0"}

        def C(name):
            a, b = cplace[name]
            return csb[:, a:b]

        def V(name, i=0, n=1):
            a, _ = vplace[name]
            return vsb[:, a + i:a + i + n]

        def Wt(name, i=0, n=1, rows=P):
            g, a, _ = wplace[name]
            return wsb[g][0:rows, a + i * P:a + (i + n) * P]

        ff0 = sb("ff0", [P, P])
        tg = sb("tg", [P, 8])
        bo = sb("bo", [P, 4])
        bog = sb("bog", [P, 4])
        cent2 = sb("cent2", [P, NE])
        centsq = sb("centsq", [P, NE])
        b2x2 = sb("b2x2", [NE, P])
        negones = sb("negones", [P, NE])

        stage_f = sb("stage_f", [P, FCOLS])
        stage_i = sb("stage_i", [P, ICOLS], I32)
        tile_f = sb("tile_f", [P, FCOLS])
        xN, ctxN = stage_f[:, FX:FX + T], stage_f[:, FC:FC + T]
        xF, ctxF, addmask = tile_f[:, FX:FX + T], tile_f[:, FC:FC + T], tile_f[:, FM:FM + T]
        xS = sb("xS", [P, T])
        ctxS = sb("ctxS", [P, T])
        hF = sb("hF", [P, T])
        hS = sb("hS", [P, T])
        outS = sb("outS", [P, T])
        rowF = sb("rowF", [P, 2])
        rowS = sb("rowS", [P, 2])

        SA, SB, TP, OY = bank("SA"), bank("SB"), bank("TP"), bank("OY")
        fx = sb("fx", [P, 2, T])
        un = sb("un", [P, W2T])
        small = sb("small", [P, 24])
        msmall = sb("msmall", [P, 24])
        neghalf = sb("neghalf", [P, 6])
        xn = sb("xn", [P, T])
        k4 = sb("k4", [P, 4, BT, SEQ])
        qk = sb("qk", [P, W2T])
        qkr = sb("qkr", [P, W2T])
        vblk = sb("vblk", [P, BT, 8, VCOLS])
        probs = sb("probs", [P, 2, W2T])
        probsT = sb("probsT", [P, 2, W2T])
        mx = sb("mx", [P, 2, 8])
        rinv = sb("rinv", [P, 16, 2])
        maskA = sb("maskA", [P, 2, SEQ])
        mask1 = sb("mask1", [P, 2, 2 * SEQ])
        upd = sb("upd", [P, T])
        qx = sb("qx", [P, 4, BT, 2, SEQ])
        vdiag = sb("vdiag", [P, BT, P])
        otx = sb("otx", [P, 4, W2T])
        sq = qkr
        onorm = upd
        v1 = k4[:, 2:4, :, :].rearrange("p a b q -> p (a b q)")
        fact = k4[:, :, :, :].rearrange("p a b q -> p a (b q)")

        H0, H1, WB, YM = bank("H0"), bank("H1"), bank("WB"), bank("YM")
        H = [H0, H1, WB]
        msq = sb("msq", [P, T])
        mu = sb("mu", [P, T])
        my = sb("my", [P, T])
        lg = sb("lg", [P, 2, NE])
        top = sb("top", [P, 2, 8])
        topi = sb("topi", [P, 2, 8], U32)
        topf = sb("topf", [P, 2, 8])
        gap = sb("gap", [P, 2])
        gapx = sb("gapx", [P, 2])
        w01 = sb("w01", [P, 2, 2])
        pick = sb("pick", [P, 2, 2, NE])
        comb = sb("comb", [P, 2, NE])
        combT = sb("combT", [NE, T])
        wexp = sb("wexp", [P, 2, T])
        hb = sb("hb", [P, 3, W2T])
        hp = sb("hp", [P, 3, W2T])
        act = sb("act", [P, 3, W2T])

        wsb["ff0"] = act[:, 0:2, :].rearrange("p a n -> p (a n)")[:, 0:3 * P]
        a12 = act[:, 2, 0:P]

        dma_const = sem("dma_const")
        dma_vec = sem("dma_vec")
        dma_w = {g: sem(f"dma_w_{g}") for g, _ in W_PARTS}
        dma_first = sem("dma_first")
        sets = [{n: sem(f"{n}_0") for n in ATTN_SIGNALS + FF_SIGNALS + MOE_SIGNALS + GELU_SIGNALS},
                {n: sem(f"{n}_1") for n in ATTN_SIGNALS + BIG_SIGNALS + MOE_SIGNALS + GLU_SIGNALS
                 + ["tile_in"]}]
        out_free = sem("out_free")
        setup_tanh, setup_pe, setup_act, setup_dve = (
            sets[1][n] for n in ("big_hidden_tanh", "big_hidden", "copied", "stat"))
        late_pe, late_dve = sets[1]["projected"], sets[1]["x_new"]

        class Counts:

            def __init__(self, sems):
                self.sems, self.seen, self.given = sems, {}, {}

            def next(self, name):
                self.seen[name] = self.seen.get(name, 0) + 1
                return self.sems[name], self.seen[name]

            def skip(self, name, n):
                self.seen[name] = self.seen.get(name, 0) + n

            def give(self, name):
                self.given[name] = self.given.get(name, 0) + 1
                return self.sems[name], 1

        class Norm:
            def __init__(self, prefix, centred, stat, spread, spread2, squares, u, small):
                self.sig = lambda name: prefix + name
                self.centred, self.stat, self.spread, self.spread2 = centred, stat, spread, spread2
                self.squares, self.u, self.small = squares, u, small

            def col(self, what):
                return self.small[:, 8 * what:8 * what + 8]

        ANORM = Norm("", SA, SB, TP, OY, sq, un, small)
        MNORM = Norm("m_", H0, H1, WB, None, msq, mu, msmall)

        def norm_pe(c, k, kind, src, fresh=False, second=None):
            pe = nc.tensor
            n = 2 if second is None else 4
            if fresh:
                pe.wait_ge(*c.next("x_new"))
            if kind != "rms":
                mm = pe.matmul(k.centred[:, 0:T], C("center"), src, start=True, stop=True)
                if second is not None:
                    mm = pe.matmul(k.centred[:, T:], C("center"), second, start=True, stop=True)
                mm.then_inc(*c.give(k.sig("centred")))
            yield GAPS["norm"][0]
            pe.wait_ge(*c.next(k.sig("squared")))
            for s in range(n):
                mm = pe.matmul(k.stat[:, s:s + 1], k.squares[:, s * P:(s + 1) * P], C("mean")[:, 0:1],
                               start=True, stop=True, skip_group_check=True)
            mm.then_inc(*c.give(k.sig("meansq")))
            yield GAPS["norm"][1]
            pe.wait_ge(*c.next(k.sig("rooted")))
            for s in range(2):
                roots = [(k.spread, 0, s)] if second is None else []
                if kind == "both":
                    roots.append((k.spread, T, n + s))
                if n == 4:
                    roots.append((k.spread2, 0, 2 + s))
                for to, at, i in roots:
                    mm = pe.matmul(to[:, at + s * P:at + (s + 1) * P], k.col(1)[:, i:i + 1].to_broadcast([P, P]),
                                   C("ident"), start=True, stop=True)
            mm.then_inc(*c.give(k.sig("spread")))
            yield GAPS["norm"][2]

        def norm_act(c, k, kind, src=None, w=T):
            a = nc.scalar
            if kind == "rms":
                a.activation(k.squares[:, 0:w], src, ACT.Square).then_inc(*c.give(k.sig("squared")))
            else:
                a.wait_ge(*c.next(k.sig("centred")))
                a.activation(k.squares[:, 0:w], k.centred[:, 0:w], ACT.Square).then_inc(*c.give(k.sig("squared")))
                a.activation(k.u[:, 0:w], k.centred[:, 0:w], ACT.Copy).then_inc(*c.give(k.sig("copied")))
            yield
            yield
            yield

        def norm_pool(c, k, kind, w=T):
            g, n = nc.gpsimd, w // P + (2 if kind == "both" else 0)
            yield
            g.wait_ge(*c.next(k.sig("stat")))
            g.tensor_tensor(k.col(1)[:, 0:n], k.col(0)[:, 0:n], neghalf[:, 0:n], ALU.pow)\
             .then_inc(*c.give(k.sig("rooted")))
            yield
            yield

        def link(c, ins, name="chain"):
            ins.then_inc(*c.give(name))
            nc.vector.wait_ge(*c.next(name))

        def norm_dve(c, k, kind, src=None, y=None, g=None, b=None, eps2=None, w=T, ctx_gb=None):
            dve, n = nc.vector, w // P
            lk = lambda ins: link(c, ins, k.sig("chain"))
            yield
            dve.wait_ge(*c.next(k.sig("meansq")))
            if kind == "both":
                dve.tensor_scalar(k.col(0)[:, n:n + 2], k.stat[:, 0:2], 1.0 + eps2, 1e-5 * eps2, ALU.mult, ALU.add)
            dve.tensor_scalar(k.col(0)[:, 0:n], k.stat[:, 0:n], eps2 if kind == "rms" else 1e-5, None, ALU.add)\
               .then_inc(*c.give(k.sig("stat")))
            yield
            dve.wait_ge(*c.next(k.sig("spread")))
            if kind == "rms":
                dve.scalar_tensor_tensor(out=y, in0=src, scalar=g, in1=k.spread[:, 0:T], op0=ALU.mult, op1=ALU.mult)\
                   .then_inc(*c.give(k.sig("normed")))
                yield
                return
            dve.wait_ge(*c.next(k.sig("copied")))
            if kind == "both":
                ins = dve.scalar_tensor_tensor(out=y, in0=k.u[:, 0:T], scalar=g, in1=k.spread[:, T:], op0=ALU.mult,
                                               op1=ALU.mult)
                if b is not None:
                    lk(ins)
                    ins = dve.tensor_scalar(y, y, b, None, ALU.add)
                if ctx_gb is not None:
                    ins.then_inc(*c.give(k.sig("normed")))
                    lk(dve.scalar_tensor_tensor(out=k.u[:, T:], in0=k.u[:, T:], scalar=ctx_gb[0],
                                                in1=k.spread2[:, 0:T], op0=ALU.mult, op1=ALU.mult))
                    dve.tensor_scalar(k.u[:, T:], k.u[:, T:], ctx_gb[1], None, ALU.add)\
                       .then_inc(*c.give(k.sig("normed")))
                    yield
                    return
                lk(ins)
            ins = dve.tensor_tensor(k.u[:, 0:T], k.u[:, 0:T], k.spread[:, 0:T], ALU.mult)
            if kind == "layer" and y is not None:
                lk(ins)
                ins = dve.tensor_scalar(y, k.u[:, 0:T], g, b, ALU.mult, ALU.add)
            ins.then_inc(*c.give(k.sig("normed")))
            yield

        def heads_pe(c, wq, wk, wv, wo, xq, xkv, rope=None, inner=False):
            pe = nc.tensor
            pe.wait_ge(*c.next("normed"))
            if rope is None:
                pe.matmul(SA[:, 0:T], wk, xkv, start=True, stop=True).then_inc(*c.give("proj_k"))
                pe.matmul(SB[:, 0:T], wq, xq, start=True, stop=True).then_inc(*c.give("proj_q"))
            else:
                pe.matmul(SA[:, 0:T], wk, xkv, start=True, stop=True)
                pe.matmul(SA[:, T:], wq, xq, start=True, stop=True)
                pe.matmul(SB[:, 0:T], rope[1], xkv, start=True, stop=True)
                pe.matmul(SB[:, T:], rope[0], xq, start=True, stop=True).then_inc(*c.give("proj_q"))
            for b in range(BT):
                for half in (0, SEQ):
                    mm = pe.matmul(TP[half:half + SEQ, b * P:(b + 1) * P], xkv[:, b * SEQ:(b + 1) * SEQ], wv,
                                   start=True, stop=True, skip_group_check=True)
            mm.then_inc(*c.give("proj_v"))
            yield GAPS["heads"][0 if rope is None else 1]
            qT = qk[:, T:]

            def scores(g):
                if g == 0:
                    pe.wait_ge(*c.next("k_heads"))
                    if rope is None:
                        pe.wait_ge(*c.next("q_taken"))
                S = (SA, SB)[g % 2]
                r = slice(32 * g, 32 * g + 32)
                for b in range(BT):
                    half = b % 2 * SEQ
                    mm = pe.matmul(S[half:half + SEQ, b // 2 * T:(b // 2 + 1) * T], qT[r, b * SEQ:(b + 1) * SEQ],
                                   k4[r, :, b, :], start=True, stop=True,
                                   skip_group_check=True)
                mm.then_inc(*c.give("scores"))

            def transposes(g):
                pe.wait_ge(*c.next("exped"))
                if g == 0:
                    pe.wait_ge(*c.next("v_blocks"))
                for b in range(BT):
                    mm = pe.transpose(TP[:, b * P:(b + 1) * P], probs[:, g % 2, b * P:(b + 1) * P], C("ident"))
                mm.then_inc(*c.give("probsT"))

            def weigh(g):
                pe.wait_ge(*c.next("probsT_taken"))
                for m, hp, b2 in np.ndindex(2, 2, 2):
                    at = (m * 8 + g * 2 + hp) * VCOLS
                    q = (2 * m + hp) * P + b2 * SEQ
                    mm = pe.matmul(OY[b2 * SEQ:(b2 + 1) * SEQ, at:at + VCOLS], probsT[:, g % 2, q:q + SEQ],
                                   vblk[:, 2 * m + b2, 2 * g + hp, :], start=True, stop=True, skip_group_check=True)
                if g == 3:
                    mm.then_inc(*c.give("context"))

            for k in range(5):
                if k == 0:
                    scores(0)
                if k < 3:
                    if k >= 1:
                        pe.wait_ge(*c.next("shifted"))
                    scores(k + 1)
                yield GAPS["heads"][2]
                if k >= 1:
                    transposes(k - 1)
                yield GAPS["heads"][3]
                if k >= 1:
                    weigh(k - 1)
                yield GAPS["heads"][4 if k < 4 else 5]
            c.skip("shifted", 2)
            pe.wait_ge(*c.next("context_normed"))
            for m in range(2):
                mm = pe.transpose(TP[:, m * P:(m + 1) * P], onorm[:, m * P:(m + 1) * P], C("ident"))
            mm.then_inc(*c.give("contextT"))
            yield GAPS["heads"][6]
            pe.wait_ge(*c.next("contextT_taken"))
            mm = pe.matmul(SA[:, 0:T], wo, qkr[:, 0:T], start=True, stop=True)
            mm.then_inc(*c.give("projected_inner" if inner else "projected"))
            yield GAPS["heads"][7]

        def heads_act(c, qbias=None):
            a = nc.scalar
            if qbias is not None:
                a.wait_ge(*c.next("proj_q"))
                a.activation(qk[:, T:], SB[:, 0:T], ACT.Identity, bias=qbias).then_inc(*c.give("q_taken"))
            yield
            for k in range(5):
                yield
                if k >= 1:
                    a.wait_ge(*c.next("probsT"))
                    a.activation(probsT[:, (k - 1) % 2, :], TP[:, :], ACT.Copy).then_inc(*c.give("probsT_taken"))
                yield
                if k < 4:
                    a.wait_ge(*c.next("shifted"))
                    a.activation(probs[:, k % 2, :], probs[:, k % 2, :], ACT.Exp).then_inc(*c.give("exped"))
                yield
            a.wait_ge(*c.next("contextT"))
            a.activation(qkr[:, 0:T], TP[:, 0:T], ACT.Copy)\
             .then_inc(*c.give("contextT_taken"))
            yield
            yield

        def heads_dve(c, kbias, mask, x, gate=None, inner=None, rope=False):
            dve = nc.vector
            if rope:
                dve.wait_ge(*c.next("proj_q"))
                cs = C("cos").unsqueeze(1).to_broadcast([P, 8, SEQ])
                sn = C("sin").unsqueeze(1).to_broadcast([P, 8, SEQ])
                by_seq = lambda t: t.rearrange("p (a t) -> p a t", t=SEQ)
                dve.tensor_tensor(by_seq(qk[:, :]), by_seq(SA[:, :]), cs, ALU.mult)
                link(c, dve.tensor_tensor(by_seq(qkr[:, :]), by_seq(SB[:, :]), sn, ALU.mult))
                link(c, dve.tensor_tensor(qk[:, :], qk[:, :], qkr[:, :], ALU.add))
                keys = qk[:, 0:T]
            else:
                dve.wait_ge(*c.next("proj_k"))
                keys = SA[:, 0:T]
            dve.scalar_tensor_tensor(
                out=k4[:, :, :, :].rearrange("p h b k -> p h (b k)"), in0=keys.unsqueeze(1).to_broadcast([P, 4, T]),
                scalar=kbias, in1=C("headsel").unsqueeze(2).to_broadcast([P, 4, T]),
                op0=ALU.add, op1=ALU.mult).then_inc(*c.give("k_heads"))
            dve.wait_ge(*c.next("proj_v"))
            dve.tensor_tensor(vblk[:, :, :, 0:2 * DK].rearrange("p b a n -> p (b a) n"),
                              TP[:, :].rearrange("p (a n) -> p a n", n=2 * DK),
                              C("halves").unsqueeze(1).to_broadcast([P, 32, 2 * DK]), ALU.mult)\
               .then_inc(*c.give("v_blocks"))
            if gate is not None:
                link(c, dve.tensor_scalar(x, x, gate[1], None, ALU.add))
            yield

            for k in range(5):
                if k < 4:
                    dve.wait_ge(*c.next("scores"))
                    if k >= 2:
                        dve.wait_ge(*c.next("probsT"))
                    S = (SA, SB)[k % 2][:, :]
                    p = probs[:, k % 2, :]
                    p3 = p.rearrange("p (a k) -> p a k", k=SEQ)
                    if mask is None:
                        src = S
                    else:
                        m = mask
                        if len(m.shape) == 2:
                            m = m.unsqueeze(1).to_broadcast([P, 8, SEQ])
                            link(c, dve.tensor_tensor(p3, S.rearrange("p (a k) -> p a k", k=SEQ), m, ALU.min))
                        else:
                            m = m.unsqueeze(2).to_broadcast([P, 2, 4, SEQ])
                            link(c, dve.tensor_tensor(p.rearrange("p (m h k) -> p m h k", m=2, h=4),
                                                      S.rearrange("p (m h k) -> p m h k", m=2, h=4), m, ALU.min))
                        src = p
                    s3 = src.rearrange("p (a k) -> p a k", k=SEQ)
                    link(c, dve.tensor_reduce(mx[:, k % 2, :], s3, AX.X, ALU.max))
                yield
                if k < 4:
                    sh = dve.tensor_tensor(p3, s3, mx[:, k % 2, :].unsqueeze(2).to_broadcast([P, 8, SEQ]), ALU.subtract)
                    sh.then_inc(*c.give("shifted"))
                yield
                if k == 4:
                    dve.wait_ge(*c.next("context"))
                    ctx = OY[:, 0:16 * VCOLS].rearrange("p (a n) -> p a n", n=VCOLS)
                    link(c, dve.reciprocal(rinv[:, :, :], ctx[:, :, 2 * DK:]))
                    dve.tensor_tensor(onorm[:, :].rearrange("p (a h d) -> p a h d", h=2, d=DK),
                                      ctx[:, :, 0:2 * DK].rearrange("p a (h d) -> p a h d", h=2),
                                      rinv[:, :, :].unsqueeze(3).to_broadcast([P, 16, 2, DK]), ALU.mult)\
                       .then_inc(*c.give("context_normed"))
                yield
            c.skip("probsT", 2)
            yield
            if inner is None:
                dve.wait_ge(*c.next("projected"))
                dve.scalar_tensor_tensor(out=x, in0=SA[:, 0:T], scalar=gate[0], in1=x, op0=ALU.mult, op1=ALU.add)\
                   .then_inc(*c.give("x_new"))
            else:
                h, base, bias = inner
                dve.wait_ge(*c.next("projected_inner"))
                dve.scalar_tensor_tensor(out=h, in0=SA[:, 0:T], scalar=bias, in1=base, op0=ALU.add,
                                         op1=ALU.add).then_inc(*c.give("x_new"))
            yield

        def single_pe(c):
            pe = nc.tensor
            kT = qk[:, T:]
            pe.wait_ge(*c.next("normed"))
            pe.matmul(SA[:, 0:T], Wt("q1"), un[:, 0:T], start=True, stop=True).then_inc(*c.give("big_proj_q"))
            pe.matmul(SB[:, 0:T], Wt("k1"), ctxF, start=True, stop=True).then_inc(*c.give("big_proj_k"))
            yield GAPS["single"][0]
            pe.wait_ge(*c.next("big_q_heads"))
            pe.wait_ge(*c.next("big_k_taken"))
            for b in range(BT):
                t = slice(b * SEQ, (b + 1) * SEQ)
                r = slice(SEQ * (b % 2), SEQ * (b % 2) + SEQ)
                mm = pe.matmul(SA[r, SEQ * (b // 2):SEQ * (b // 2) + SEQ], k4[:, 0, b, :], kT[:, t],
                               start=True, stop=True, skip_group_check=True)
            mm.then_inc(*c.give("big_scores"))
            for b in range(BT):
                mm = pe.matmul(TP[0:SEQ, b * P:(b + 1) * P], kT[:, b * SEQ:(b + 1) * SEQ], Wt("v1"),
                               start=True, stop=True)
            mm.then_inc(*c.give("big_proj_v"))
            yield GAPS["single"][1]
            yield GAPS["single"][2]
            pe.wait_ge(*c.next("big_probs_normed"))
            for m in range(2):
                mm = pe.transpose(OY[0:SEQ, m * P:(m + 1) * P], probs[:, 0, m * SEQ:(m + 1) * SEQ], C("ident"))
            mm.then_inc(*c.give("big_probsT"))
            yield GAPS["single"][3]
            pe.wait_ge(*c.next("big_v_blocks"))
            pe.wait_ge(*c.next("big_probsT_taken"))
            for b in range(BT):
                mm = pe.matmul(SB[:, b * SEQ:(b + 1) * SEQ], v1[0:SEQ, b * P:(b + 1) * P],
                               probsT[0:SEQ, 0, b * SEQ:(b + 1) * SEQ], start=True, stop=True, skip_group_check=True)
            mm.then_inc(*c.give("big_context"))
            yield GAPS["single"][4]
            pe.wait_ge(*c.next("big_contextT_taken"))
            pe.matmul(SA[:, 0:T], Wt("o1"), qkr[:, 0:T], start=True, stop=True).then_inc(*c.give("projected"))
            yield GAPS["single"][5]

        def single_act(c):
            a = nc.scalar
            a.wait_ge(*c.next("big_proj_q"))
            a.activation(k4[:, 0, :, :], SA[:, 0:T].rearrange("p (b q) -> p b q", b=BT), ACT.Identity,
                         bias=V("bq1")).then_inc(*c.give("big_q_heads"))
            yield
            a.wait_ge(*c.next("big_proj_v"))
            a.activation(v1[0:SEQ, :], TP[0:SEQ, :], ACT.Copy)\
             .then_inc(*c.give("big_v_blocks"))
            a.wait_ge(*c.next("big_shifted"))
            a.activation(probs[:, 0, 0:P], probs[:, 0, 0:P], ACT.Exp).then_inc(*c.give("big_exped"))
            yield
            yield
            a.wait_ge(*c.next("big_probsT"))
            a.activation(probsT[0:SEQ, 0, 0:T], OY[0:SEQ, 0:T], ACT.Copy).then_inc(*c.give("big_probsT_taken"))
            yield
            a.wait_ge(*c.next("big_context"))
            a.activation(qkr[:, 0:T], SB[:, 0:T], ACT.Copy).then_inc(*c.give("big_contextT_taken"))
            yield
            yield

        def single_dve(c):
            dve = nc.vector
            s = probs[:, 0, 0:P]
            s2 = s.rearrange("p (m k) -> p m k", m=2)
            dve.wait_ge(*c.next("big_proj_k"))
            dve.tensor_scalar(qk[:, T:], SB[:, 0:T], V("bk1"), None, ALU.add).then_inc(*c.give("big_k_taken"))
            link(c, dve.tensor_scalar(xF, xF, bog[:, 1:2], None, ALU.add))
            yield
            dve.wait_ge(*c.next("big_scores"))
            link(c, dve.tensor_tensor(s, SA[:, 0:P], mask1[:, 0, :], ALU.mult))
            link(c, dve.tensor_tensor(s, s, mask1[:, 1, :], ALU.add))
            link(c, dve.tensor_reduce(mx[:, 0, 0:2], s2, AX.X, ALU.max))
            dve.tensor_tensor(s2, s2, mx[:, 0, 0:2].unsqueeze(2).to_broadcast([P, 2, SEQ]), ALU.subtract)\
               .then_inc(*c.give("big_shifted"))
            yield
            dve.wait_ge(*c.next("big_exped"))
            link(c, dve.tensor_reduce(mx[:, 1, 0:2], s2, AX.X, ALU.add))
            link(c, dve.reciprocal(mx[:, 1, 0:2], mx[:, 1, 0:2]))
            dve.tensor_tensor(s2, s2, mx[:, 1, 0:2].unsqueeze(2).to_broadcast([P, 2, SEQ]), ALU.mult)\
               .then_inc(*c.give("big_probs_normed"))
            yield
            yield
            yield
            dve.wait_ge(*c.next("projected"))
            dve.scalar_tensor_tensor(out=xF, in0=SA[:, 0:T], scalar=tg[:, 1:2], in1=xF, op0=ALU.mult, op1=ALU.add)\
               .then_inc(*c.give("x_new"))
            yield

        def ff0_pe(c):
            nc.tensor.wait_ge(*c.next("normed"))
            nc.tensor.matmul(SA[:, 0:T], ff0[:, :], un[:, 0:T], start=True, stop=True).then_inc(*c.give("ff_hidden"))
            yield GAPS["ff0"][0]

        def ff0_act(c):
            nc.scalar.wait_ge(*c.next("ff_hidden"))
            nc.scalar.activation(upd[:, :], SA[:, 0:T], ACT.Tanh, bias=V("bf0")).then_inc(*c.give("ff_hidden_tanh"))
            yield

        def ff0_dve(c):
            nc.vector.wait_ge(*c.next("ff_hidden_tanh"))
            nc.vector.scalar_tensor_tensor(out=xN, in0=upd[:, :], scalar=tg[:, 4:5], in1=xN, op0=ALU.mult,
                                           op1=ALU.add).then_inc(*c.give("x_new"))
            yield

        def by_chunk(S):
            return S[:, :].rearrange("p (c b q) -> p b c q", c=2, b=BT)

        def wide_pe(c):
            pe = nc.tensor
            kT, cn = qk[:, T:], un[:, T:]
            pe.wait_ge(*c.next("normed"))

            def queries(p):
                for i in range(2):
                    mm = pe.matmul((SA, SB)[p % 2][:, i * T:(i + 1) * T], Wt("qx", 2 * p + i), xn[:, :],
                                   start=True, stop=True)
                mm.then_inc(*c.give("big_proj_q"))

            queries(0)
            queries(1)
            pe.wait_ge(*c.next("normed"))
            pe.matmul(OY[:, 0:T], Wt("kx"), cn, start=True, stop=True).then_inc(*c.give("big_proj_k"))
            g, a, z = wplace["vx"]
            for b in range(BT):
                for half in (0, SEQ):
                    mm = pe.matmul(TP[half:half + SEQ, b * 64:(b + 1) * 64], cn[:, b * SEQ:(b + 1) * SEQ],
                                   wsb[g][:, a:z], start=True, stop=True, skip_group_check=True)
            mm.then_inc(*c.give("big_proj_v"))
            yield GAPS["wide"][0]
            pe.wait_ge(*c.next("big_q_heads"))
            queries(2)
            pe.wait_ge(*c.next("big_q_heads_dve"))
            queries(3)
            yield GAPS["wide"][1]

            def scores(u):
                j, mp = u // 2, u % 2
                r = slice(64 * j, 64 * j + 64)
                if u == 0:
                    pe.wait_ge(*c.next("big_k_taken"))
                    pe.wait_ge(*c.next("big_q_heads"))
                    pe.wait_ge(*c.next("big_q_heads_dve"))
                if u >= 2:
                    pe.wait_ge(*c.next("big_added"))
                for b in range(BT):
                    for m2 in range(2):
                        at = (2 * b + m2) * SEQ
                        mm = pe.matmul((SA, SB)[u % 2][:, at:at + SEQ],
                                       qx[r, 2 * mp + m2, b, :, :].rearrange("p c q -> p (c q)"),
                                       kT[r, b * SEQ:(b + 1) * SEQ], start=True, stop=True, skip_group_check=True)
                mm.then_inc(*c.give("big_scores"))

            def transposes(u):
                pe.wait_ge(*c.next("big_probs_normed"))
                if u == 0:
                    pe.wait_ge(*c.next("big_v_blocks"))
                for b in range(BT):
                    mm = pe.transpose(TP[:, b * P:(b + 1) * P], probs[:, u % 2, b * P:(b + 1) * P], C("ident"))
                mm.then_inc(*c.give("big_probsT"))

            def weigh(u):
                pe.wait_ge(*c.next("big_probsT_taken"))
                if u >= 1:
                    pe.wait_ge(*c.next("big_contextT_taken"))
                for b in range(BT):
                    mm = pe.matmul(OY[:, b * P:(b + 1) * P], vdiag[:, b, :], probsT[:, u % 2, b * P:(b + 1) * P],
                                   start=True, stop=True)
                mm.then_inc(*c.give("big_context"))

            def hidden(ch):
                if ch >= 2:
                    pe.wait_ge(*c.next("big_hidden_done"))
                else:
                    pe.wait_ge(*c.next("big_added"))
                S = (SA, SB)[ch % 2]
                pe.matmul(S[:, 0:T], Wt("ffx", 2 * ch), xn[:, :], start=True, stop=True)
                pe.matmul(S[:, T:], Wt("ffx", 2 * ch + 1), xn[:, :], start=True, stop=True)\
                  .then_inc(*c.give("big_hidden"))

            def project(u):
                for c2 in range(2):
                    rhs = otx[:, u, :].rearrange("p (b c q) -> p b c q", b=BT, c=2)[:, :, c2, :]
                    pe.matmul(TP[:, 0:T], Wt("ox", 2 * u + c2), rhs, start=(u + c2 == 0), stop=False)

            for k in range(6):
                if k == 0:
                    scores(0)
                if k < 3:
                    scores(k + 1)
                yield GAPS["wide"][2]
                if k >= 2:
                    weigh(k - 2)
                if k == 5:
                    hidden(1)
                yield GAPS["wide"][3] if k < 5 else GAPS["wide"][6]
                if k == 4:
                    hidden(0)
                yield GAPS["wide"][4] if k < 5 else 0
                if 1 <= k < 5:
                    transposes(k - 1)
                yield GAPS["wide"][5]
            for ch in (2, 3):
                project(ch - 2)
                hidden(ch)
                yield GAPS["wide"][6]
            project(2)
            pe.wait_ge(*c.next("big_contextT_taken"))
            project(3)
            for ch in range(4):
                if ch >= 2:
                    pe.wait_ge(*c.next("big_hidden_done"))
                mm = pe.matmul(TP[:, 0:T], Wt("ff2x", ch), fact[:, ch, :], start=False, stop=(ch == 3))
            mm.then_inc(*c.give("projected"))
            yield GAPS["wide"][7]

        def wide_act(c):
            a = nc.scalar
            a.wait_ge(*c.next("big_proj_q"))
            a.activation(qx[:, 0, :, :, :], by_chunk(SA), ACT.Copy, scale=0.125)\
             .then_inc(*c.give("big_q_heads"))
            a.wait_ge(*c.next("big_proj_k"))
            a.activation(qk[:, T:], OY[:, 0:T], ACT.Copy).then_inc(*c.give("big_k_taken"))
            c.next("big_proj_q")
            yield
            a.wait_ge(*c.next("big_proj_q"))
            a.activation(qx[:, 2, :, :, :], by_chunk(SA), ACT.Copy, scale=0.125)\
             .then_inc(*c.give("big_q_heads"))
            c.next("big_proj_q")
            yield
            def hidden(ch):
                a.wait_ge(*c.next("big_hidden"))
                a.activation(fx[:, ch % 2, :], (SA, SB)[ch % 2][:, T:], ACT.Tanh, scale=0.5)\
                 .then_inc(*c.give("big_hidden_tanh"))

            for k in range(6):
                yield
                yield
                if k < 4:
                    a.wait_ge(*c.next("big_shifted"))
                    a.activation(probs[:, k % 2, :], probs[:, k % 2, :], ACT.Exp).then_inc(*c.give("big_exped"))
                if k >= 2:
                    a.wait_ge(*c.next("big_context"))
                    a.activation(otx[:, k - 2, :], OY[:, :], ACT.Copy).then_inc(*c.give("big_contextT_taken"))
                yield
                if 1 <= k < 5:
                    a.wait_ge(*c.next("big_probsT"))
                    a.activation(probsT[:, (k - 1) % 2, :], TP[:, :], ACT.Copy).then_inc(*c.give("big_probsT_taken"))
                if k >= 4:
                    hidden(k - 4)
                yield
            for ch in (2, 3):
                hidden(ch)
                yield
            yield

        def wide_dve(c):
            dve = nc.vector
            for p in (1, 3):
                c.next("big_proj_q")
                dve.wait_ge(*c.next("big_proj_q"))
                dve.tensor_scalar(qx[:, p, :, :, :], by_chunk(SB), 0.125, None,
                                  ALU.mult).then_inc(*c.give("big_q_heads_dve"))
                if p == 1:
                    dve.wait_ge(*c.next("big_proj_v"))
                    for h in range(2):
                        r = slice(64 * h, 64 * h + 64)
                        v = dve.tensor_copy(vdiag[r, :, 64 * h:64 * h + 64], TP[r, 0:T].rearrange("p (b d) -> p b d", b=BT))
                    v.then_inc(*c.give("big_v_blocks"))
                yield
            def added(k):
                p4 = probs[:, k % 2, :].rearrange("p (b m k) -> p b m k", b=BT, m=2)
                dve.wait_ge(*c.next("big_scores"))
                if k >= 2:
                    dve.wait_ge(*c.next("big_probsT"))
                mk = addmask.rearrange("p (b k) -> p b k", b=BT).unsqueeze(2).to_broadcast([P, BT, 2, SEQ])
                dve.tensor_tensor(p4, (SA, SB)[k % 2][:, :].rearrange("p (b m k) -> p b m k", b=BT, m=2), mk, ALU.add)\
                   .then_inc(*c.give("big_added"))
                dve.wait_ge(*c.next("big_added"))
                p3 = probs[:, k % 2, :].rearrange("p (a k) -> p a k", k=SEQ)
                link(c, dve.tensor_reduce(mx[:, k % 2, :], p3, AX.X, ALU.max))

            def shifted(k):
                p3 = probs[:, k % 2, :].rearrange("p (a k) -> p a k", k=SEQ)
                dve.tensor_tensor(p3, p3, mx[:, k % 2, :].unsqueeze(2).to_broadcast([P, 8, SEQ]), ALU.subtract)\
                   .then_inc(*c.give("big_shifted"))

            def hidden(ch):
                S = (SA, SB)[ch % 2]
                dve.wait_ge(*c.next("big_hidden_tanh"))
                link(c, dve.scalar_tensor_tensor(out=fx[:, ch % 2, :], in0=fx[:, ch % 2, :], scalar=1.0, in1=S[:, T:],
                                                 op0=ALU.add, op1=ALU.mult))
                dve.scalar_tensor_tensor(out=fact[:, ch, :], in0=fx[:, ch % 2, :], scalar=0.5, in1=S[:, 0:T],
                                         op0=ALU.mult, op1=ALU.mult).then_inc(*c.give("big_hidden_done"))

            def normed(k):
                p3 = probs[:, k % 2, :].rearrange("p (a k) -> p a k", k=SEQ)
                s8 = mx[:, k % 2, :]
                dve.wait_ge(*c.next("big_exped"))
                link(c, dve.tensor_reduce(s8, p3, AX.X, ALU.add))
                link(c, dve.reciprocal(s8, s8))
                dve.tensor_tensor(p3, p3, s8.unsqueeze(2).to_broadcast([P, 8, SEQ]), ALU.mult)\
                   .then_inc(*c.give("big_probs_normed"))

            for k in range(6):
                if k < 4:
                    added(k)
                yield
                if k < 4:
                    shifted(k)
                yield
                if 1 <= k < 5:
                    normed(k - 1)
                yield
                if k >= 4:
                    hidden(k - 4)
                yield
            for ch in (2, 3):
                hidden(ch)
                yield
            dve.wait_ge(*c.next("projected"))
            dve.scalar_tensor_tensor(out=xF, in0=TP[:, 0:T], scalar=tg[:, 2:3], in1=xF, op0=ALU.mult, op1=ALU.add)\
               .then_inc(*c.give("x_new"))
            yield

        def route_pe(c, src, kind, gate, nearest=False):
            pe = nc.tensor
            yield from norm_pe(c, MNORM, kind, src)
            pe.wait_ge(*c.next("m_normed"))
            if nearest:
                pe.wait_ge(*c.next("m_rowsq"))
            for s in range(2):
                o = H1[:, s * NE:(s + 1) * NE]
                t = slice(s * P, (s + 1) * P)
                mm = pe.matmul(o, my[:, t], gate, start=True, stop=not nearest)
                if nearest:
                    pe.matmul(o, msq[:, t], negones[:, :], start=False, stop=False)
                    mm = pe.matmul(o, C("mean"), centsq[:, :], start=False, stop=True)
            mm.then_inc(*c.give("m_logits"))
            yield GAPS["route"][0]
            yield GAPS["route"][1]
            pe.wait_ge(*c.next("m_comb"))
            for s in range(2):
                mm = pe.transpose(H0[0:NE, s * P:(s + 1) * P], comb[:, s, :], C("ident"))
            mm.then_inc(*c.give("m_combT"))
            yield GAPS["route"][2]

        def route_act(c, src, kind, nearest=False):
            a = nc.scalar
            yield from norm_act(c, MNORM, kind, src)
            if nearest:
                a.wait_ge(*c.next("m_normed"))
                a.activation(msq[:, :], my[:, :], ACT.Square).then_inc(*c.give("m_rowsq"))
            yield
            if not nearest:
                a.wait_ge(*c.next("m_gap"))
                a.activation(gapx[:, :], gap[:, :], ACT.Exp).then_inc(*c.give("m_gap_exp"))
            yield
            a.wait_ge(*c.next("m_combT"))
            a.activation(combT[:, :], H0[0:NE, 0:T], ACT.Copy, scale=0.5).then_inc(*c.give("m_combT_taken"))
            yield

        def route_pool(c, kind):
            yield from norm_pool(c, MNORM, kind)
            yield from idle(3)

        def route_dve(c, src, kind, g, b=None, nearest=False):
            dve = nc.vector
            lk = lambda ins: link(c, ins, "m_chain")
            yield from norm_dve(c, MNORM, kind, src, y=my[:, :], g=g, b=b, eps2=1e-6)
            dve.wait_ge(*c.next("m_logits"))
            lk(dve.tensor_copy(lg[:, :, :].rearrange("p s e -> p (s e)"), H1[:, 0:2 * NE]))
            dve.max(top[:, 0, :], lg[:, 0, :])
            lk(dve.max(top[:, 1, :], lg[:, 1, :]))
            if not nearest:
                dve.tensor_tensor(gap[:, :], top[:, :, 1], top[:, :, 0], ALU.subtract).then_inc(*c.give("m_gap"))
            dve.max_index(topi[:, 0, :], top[:, 0, :], lg[:, 0, :])
            lk(dve.max_index(topi[:, 1, :], top[:, 1, :], lg[:, 1, :]))
            lk(dve.tensor_copy(topf[:, :, :], topi[:, :, :]))
            yield
            iota = C("iota8").unsqueeze(1).to_broadcast([P, 2, NE])
            if nearest:
                dve.tensor_tensor(comb[:, :, :], iota, topf[:, :, 0:1].to_broadcast([P, 2, NE]), ALU.is_equal)\
                   .then_inc(*c.give("m_comb"))
                yield
                yield
                return
            dve.wait_ge(*c.next("m_gap_exp"))
            lk(dve.tensor_scalar(w01[:, 0, :], gapx[:, :], 1.0, None, ALU.add))
            lk(dve.reciprocal(w01[:, 0, :], w01[:, 0, :]))
            dve.tensor_tensor(w01[:, 1, :], gapx[:, :], w01[:, 0, :], ALU.mult)
            for i in range(2):
                last = dve.tensor_tensor(pick[:, i, :, :], iota, topf[:, :, i:i + 1].to_broadcast([P, 2, NE]),
                                         ALU.is_equal)
            lk(last)
            for i in range(2):
                last = dve.tensor_tensor(pick[:, i, :, :], pick[:, i, :, :],
                                         w01[:, i, :].unsqueeze(2).to_broadcast([P, 2, NE]), ALU.mult)
            lk(last)
            dve.tensor_tensor(comb[:, :, :], pick[:, 0, :, :], pick[:, 1, :, :], ALU.add).then_inc(*c.give("m_comb"))
            yield
            yield

        def weights_sp(c, free, steps):
            sp = nc.sync
            sp.wait_ge(*c.next("m_combT_taken"))
            for e in range(NE):
                if e >= 2:
                    c.skip(free, steps)
                    sp.wait_ge(c.sems[free], c.seen[free])
                sem, _ = c.give(("m_weight_even", "m_weight_odd")[e % 2])
                sp.dma_start(wexp[:, e % 2, :], combT[e:e + 1, :].unsqueeze(1).to_broadcast([1, P, T])).then_inc(sem, 16)

        def wait_weights(c, engine, e):
            sem, n = c.next(("m_weight_even", "m_weight_odd")[e % 2])
            engine.wait_ge(sem, 16 * n)

        N1 = NE * 2

        def gelu_pe(c):
            pe = nc.tensor
            for n in range(N1 + 3):
                if n == 0:
                    pe.wait_ge(*c.next("m_combT_taken"))
                    pe.matmul(YM[:, 0:T], b2x2[:, :], combT[:, :], start=True, stop=False)
                for i in range(2):
                    if n < N1:
                        if n >= 3 and i == 0:
                            pe.wait_ge(*c.next("m_up_free"))
                        mm = pe.matmul(H[n % 3][:, i * T:(i + 1) * T], Wt("up1", 2 * n + i), my[:, :],
                                       start=True, stop=True)
                        if i == 1:
                            mm.then_inc(*c.give("m_up"))
                    yield 1 if n < N1 else 0
                for i in range(2):
                    if n >= 3:
                        if i == 0:
                            pe.wait_ge(*c.next("m_act"))
                        mm = pe.matmul(YM[:, 0:T], Wt("dn1", 2 * (n - 3) + i), act[:, n % 3, i * T:(i + 1) * T],
                                       start=False, stop=(n == N1 + 2 and i == 1))
                        if i == 1:
                            mm.then_inc(*c.give("m_down"))
                    yield 1 if n >= 3 else 0
            yield

        def gelu_act(c):
            a = nc.scalar
            for n in range(N1 + 3):
                yield
                yield
                if n < N1:
                    if n >= 3:
                        a.wait_ge(*c.next("m_act"))
                    a.wait_ge(*c.next("m_up"))
                    for i in range(2):
                        h = a.activation(hb[:, n % 3, i * T:(i + 1) * T], H[n % 3][:, i * T:(i + 1) * T], ACT.Identity,
                                         bias=V("b1", 2 * n + i))
                    h.then_inc(*c.give("m_up_free"))
                    a.wait_ge(*c.next("m_up_free"))
                    a.activation(hp[:, n % 3, :], hb[:, n % 3, :], ACT.Square, scale=GELU_CUBE)\
                     .then_inc(*c.give("m_square"))
                yield
                if 1 <= n <= N1:
                    a.wait_ge(*c.next("m_cubic"))
                    a.activation(hp[:, (n - 1) % 3, :], hp[:, (n - 1) % 3, :], ACT.Tanh, scale=GELU_C)\
                     .then_inc(*c.give("m_tanh"))
                yield
            yield

        def gelu_dve(c):
            dve = nc.vector
            for n in range(N1 + 3):
                if 1 <= n <= N1:
                    m = n - 1
                    dve.wait_ge(*c.next("m_square"))
                    dve.scalar_tensor_tensor(out=hp[:, m % 3, :], in0=hp[:, m % 3, :], scalar=1.0, in1=hb[:, m % 3, :],
                                             op0=ALU.add, op1=ALU.mult).then_inc(*c.give("m_cubic"))
                yield
                if 2 <= n <= N1 + 1:
                    m = n - 2
                    dve.wait_ge(*c.next("m_tanh"))
                    link(c, dve.scalar_tensor_tensor(out=hp[:, m % 3, :], in0=hp[:, m % 3, :], scalar=1.0,
                                                     in1=hb[:, m % 3, :], op0=ALU.add, op1=ALU.mult), "m_chain")
                    if m % 2 == 0:
                        wait_weights(c, dve, m // 2)
                    if m >= 3:
                        dve.wait_ge(*c.next("m_down"))
                    dve.tensor_tensor(act[:, m % 3, :].rearrange("p (i t) -> p i t", i=2),
                                      hp[:, m % 3, :].rearrange("p (i t) -> p i t", i=2),
                                      wexp[:, m // 2 % 2, :].unsqueeze(1).to_broadcast([P, 2, T]), ALU.mult)\
                       .then_inc(*c.give("m_act"))
                yield
                yield
                yield
            finish_dve(c, N1, hF[:, :], 5, xF)
            yield

        def finish_dve(c, steps, skip, gate, x, y=None):
            dve = nc.vector
            have = c.seen.get("m_down", 0)
            for _ in range(steps - have):
                last = c.next("m_down")
            dve.wait_ge(*last)
            link(c, dve.tensor_tensor(msq[:, :], YM[:, 0:T], skip, ALU.add), "m_chain")
            dve.scalar_tensor_tensor(out=x if y is None else y, in0=msq[:, :], scalar=tg[:, gate:gate + 1], in1=x,
                                     op0=ALU.mult, op1=ALU.add).then_inc(*c.give("m_out"))

        def glu_pe(c, up, down, chunks):
            pe = nc.tensor
            N = NE * chunks

            for n in range(N + 3):
                e, ch = divmod(n, chunks)
                S = H[n % 3]
                if n == 0:
                    pe.wait_ge(*c.next("m_combT_taken"))
                if n < N:
                    if n >= 3:
                        pe.wait_ge(*c.next("m_up_free"))
                    pe.matmul(S[:, 0:T], Wt(up, 2 * n), my[:, :], start=True, stop=True)
                yield 1
                if n >= 3:
                    pe.wait_ge(*c.next("m_act"))
                    pe.matmul(YM[:, 0:T], Wt(down, n - 3), act[:, n % 3, 0:T], start=(n == 3), stop=(n == N + 2))\
                      .then_inc(*c.give("m_down"))
                yield 1 if n >= 3 else 0
                if n < N:
                    if ch == 0:
                        pe.wait_ge(*c.next("m_weight_taken"))
                    pe.matmul(S[:, T:], Wt(up, 2 * n + 1), hp[:, e % 2, T:], start=True, stop=True)\
                      .then_inc(*c.give("m_up"))
                yield 1
            yield

        def glu_act(c, chunks):
            a = nc.scalar
            for n in range(NE * chunks + 3):
                if 1 <= n <= NE * chunks:
                    m = n - 1
                    if m >= 3:
                        a.wait_ge(*c.next("m_act"))
                    a.wait_ge(*c.next("m_up"))
                    a.activation(hb[:, m % 3, :], H[m % 3][:, :], ACT.Copy).then_inc(*c.give("m_up_free"))
                yield
                if 1 <= n <= NE * chunks:
                    m = n - 1
                    a.wait_ge(*c.next("m_up_free"))
                    a.activation(hp[:, m % 3, 0:T], hb[:, m % 3, 0:T], ACT.Tanh, scale=0.5).then_inc(*c.give("m_tanh"))
                yield
                yield
            yield

        def glu_dve(c, chunks, skip, gate, y=None):
            dve = nc.vector
            N = NE * chunks

            def weigh_input(e):
                wait_weights(c, dve, e)
                dve.tensor_tensor(hp[:, e % 2, T:], wexp[:, e % 2, :], my[:, :], ALU.mult)\
                   .then_inc(*c.give("m_weight_taken"))

            for n in range(N + 3):
                if n == 0:
                    weigh_input(0)
                yield
                yield
                if 1 <= n <= N:
                    e, ch = divmod(n - 1, chunks)
                    m = n - 1
                    dve.wait_ge(*c.next("m_tanh"))
                    link(c, dve.scalar_tensor_tensor(out=hp[:, m % 3, 0:T], in0=hp[:, m % 3, 0:T], scalar=1.0,
                                                     in1=hb[:, m % 3, 0:T], op0=ALU.add, op1=ALU.mult), "m_chain")
                    if m >= 3:
                        dve.wait_ge(*c.next("m_down"))
                    dve.tensor_tensor(act[:, m % 3, 0:T], hp[:, m % 3, 0:T], hb[:, m % 3, T:], ALU.mult)\
                       .then_inc(*c.give("m_act"))
                    if ch == 0 and e + 1 < NE:
                        weigh_input(e + 1)
                yield
            finish_dve(c, N, skip, gate, xS[:, :], y)
            yield

        def idle(slots):
            for _ in range(slots):
                yield

        HEADS, SINGLE, FF0, WIDE = 18, 6, 1, 29
        causal = C("causal")

        def f1_pe(c):
            yield from norm_pe(c, ANORM, "layer", xF)
            yield from single_pe(c)
            yield from norm_pe(c, ANORM, "both", xF, fresh=True)
            yield from heads_pe(c, Wt("qa"), Wt("ka"), Wt("va"), Wt("oa"), xn[:, :], xn[:, :], inner=True)

        def f1_act(c):
            yield from norm_act(c, ANORM, "layer")
            yield from single_act(c)
            yield from norm_act(c, ANORM, "both")
            yield from heads_act(c, V("bqa"))

        def f1_dve(c):
            yield from norm_dve(c, ANORM, "layer")
            yield from single_dve(c)
            yield from norm_dve(c, ANORM, "both", y=xn[:, :], g=V("ln1w"), b=V("ln1b"), eps2=1e-5)
            yield from heads_dve(c, V("bka"), None, None, inner=(hF[:, :], un[:, 0:T], bo[:, 2:3]))

        def f1_pool(c):
            yield from norm_pool(c, ANORM, "layer")
            yield from idle(SINGLE)
            yield from norm_pool(c, ANORM, "both")
            yield from idle(HEADS)

        def s1_pe(c):
            yield from route_pe(c, hS[:, :], "rms", V("router2", 0, NE))
            yield from glu_pe(c, "up2", "dn2", 3)

        def s1_act(c):
            yield from route_act(c, hS[:, :], "rms")
            yield from glu_act(c, 3)

        def s1_dve(c):
            yield from route_dve(c, hS[:, :], "rms", V("g2"))
            yield from glu_dve(c, 3, hS[:, :], 6)

        def n2_pe(c, fresh):
            yield from norm_pe(c, ANORM, "layer", xN, fresh=fresh)
            yield from heads_pe(c, Wt("q0"), Wt("k0"), Wt("v0"), Wt("o0"), un[:, 0:T], ctxN)
            yield from norm_pe(c, ANORM, "layer", xN, fresh=True)
            yield from ff0_pe(c)

        def n2_act(c):
            yield from norm_act(c, ANORM, "layer")
            yield from heads_act(c, V("bq0"))
            yield from norm_act(c, ANORM, "layer")
            yield from ff0_act(c)

        def n2_dve(c):
            flat = maskA[:, :, :].rearrange("p b k -> p (b k)")
            link(c, nc.vector.tensor_scalar(flat, stage_i[:, IM0:IM0 + 2 * SEQ], 0.0, 0.5, ALU.is_equal, ALU.subtract))
            link(c, nc.vector.tensor_scalar(flat, flat, -2e9, None, ALU.mult))
            yield from norm_dve(c, ANORM, "layer")
            yield from heads_dve(c, V("bk0"), maskA[:, :, :], xN, gate=(tg[:, 0:1], bog[:, 0:1]))
            yield from norm_dve(c, ANORM, "layer")
            yield from ff0_dve(c)

        def n2_pool(c):
            yield from norm_pool(c, ANORM, "layer")
            yield from idle(HEADS)
            yield from norm_pool(c, ANORM, "layer")
            yield from idle(FF0)

        def s2_pe(c):
            yield from norm_pe(c, ANORM, "layer", xS[:, :])
            yield from heads_pe(c, Wt("q3"), Wt("k3"), Wt("v3"), Wt("o3"), un[:, 0:T], ctxS[:, :])

        def s2_act(c):
            yield from norm_act(c, ANORM, "layer")
            yield from heads_act(c, V("bq3"))

        def s2_dve(c):
            link(c, nc.vector.tensor_tensor(maskA[:, :, :], causal.unsqueeze(1).to_broadcast([P, 2, SEQ]),
                                            rowS[:, :].unsqueeze(2).to_broadcast([P, 2, SEQ]), ALU.min))
            yield from norm_dve(c, ANORM, "layer")
            yield from heads_dve(c, V("bk3"), maskA[:, :, :], xS[:, :], gate=(tg[:, 3:4], bog[:, 3:4]))

        def f2_pe(c):
            yield from route_pe(c, hF[:, :], "layer", V("gate1", 0, NE))
            yield from gelu_pe(c)

        def f2_act(c):
            yield from route_act(c, hF[:, :], "layer")
            yield from gelu_act(c)

        def f2_pool(c):
            yield from route_pool(c, "layer")
            yield from idle(4 * (N1 + 3) + 1)

        def f2_dve(c):
            yield from route_dve(c, hF[:, :], "layer", V("ln2w"), V("ln2b"))
            yield from gelu_dve(c)

        def f3_pe(c):
            yield from norm_pe(c, ANORM, "both", xF, second=ctxF)
            yield from wide_pe(c)
            yield from norm_pe(c, ANORM, "both", xF, fresh=True)
            yield from heads_pe(c, Wt("q2"), Wt("k2"), Wt("v2"), Wt("o2"), xn[:, :], xn[:, :],
                                rope=(Wt("qr2"), Wt("kr2")), inner=True)

        def f3_act(c):
            yield from norm_act(c, ANORM, "both", w=W2T)
            yield from wide_act(c)
            yield from norm_act(c, ANORM, "both")
            yield from heads_act(c)

        def f3_dve(c):
            yield from norm_dve(c, ANORM, "both", y=xn[:, :], g=V("lng"), b=V("lnb"), eps2=1e-5, w=W2T,
                                ctx_gb=(V("clng"), V("clnb")))
            yield from wide_dve(c)
            yield from norm_dve(c, ANORM, "both", y=xn[:, :], g=V("g1"), eps2=1e-6)
            yield from heads_dve(c, 0.0, causal, None, inner=(hF[:, :], un[:, 0:T], 0.0), rope=True)

        def s3_pe(c):
            yield from route_pe(c, xS[:, :], "both", cent2[:, :], nearest=True)
            yield from glu_pe(c, "up3", "dn3", 2)

        def s3_act(c):
            yield from route_act(c, xS[:, :], "both", nearest=True)
            yield from glu_act(c, 2)

        def s3_dve(c):
            yield from route_dve(c, xS[:, :], "both", V("scale3"), nearest=True)
            yield from glu_dve(c, 2, mu[:, :], 7, outS[:, :])

        def s1_pool(c):
            yield from route_pool(c, "rms")
            yield from idle(3 * (NE * 3 + 3) + 1)

        def s2_pool(c):
            yield from norm_pool(c, ANORM, "layer")
            yield from idle(HEADS)

        def f3_pool(c):
            yield from norm_pool(c, ANORM, "both", W2T)
            yield from idle(WIDE)
            yield from norm_pool(c, ANORM, "both")
            yield from idle(HEADS)

        def s3_pool(c):
            yield from route_pool(c, "both")
            yield from idle(3 * (NE * 2 + 3) + 1)

        def gelu_sp(c):
            weights_sp(c, "m_act", 2)

        def glu_sp(c):
            weights_sp(c, "m_weight_taken", 1)

        def after(a, b):
            def run(c):
                yield from a(c)
                yield from b(c)
            return run if a and b else a or b

        def streams(which, first, second, following):
            if which == 1:
                return (first and (f1_pe, f1_act, f1_dve, f1_pool)), (second and (s1_pe, s1_act, s1_dve, s1_pool, glu_sp))
            if which == 3:
                return (first and (f3_pe, f3_act, f3_dve, f3_pool)), (second and (s3_pe, s3_act, s3_dve, s3_pool, glu_sp))
            s2 = (s2_pe, s2_act, s2_dve, s2_pool) if second else 4 * (None,)
            n2 = (lambda c: n2_pe(c, fresh=second), n2_act, n2_dve, n2_pool) if following else 4 * (None,)
            attn = (second or following) and [after(a, b) for a, b in zip(s2, n2)]
            return attn, (first and (f2_pe, f2_act, f2_dve, f2_pool, gelu_sp))

        def clear_resting(parity):
            nums = sorted(s.num for s in sets[1 - parity].values())
            assert nums == list(range(nums[0], nums[0] + len(nums)))
            nc.gpsimd.sem_clear(range(nums[0], nums[-1] + 1))

        def handoff(parity, first, second):
            sems = sets[parity]
            with nc.Block() as block:
                @block.gpsimd
                def _(pool):
                    clear_resting(parity)
                    if first:
                        if second:
                            pool.wait_ge(sems["normed"], 1)
                        nc.gpsimd.tensor_copy(xF, xN)

                @block.scalar
                def _(a):
                    if second:
                        nc.scalar.activation(ctxS[:, :], ctxF, ACT.Copy).then_inc(sems["copied"], 1)
                    if first:
                        if second:
                            a.wait_ge(sems["copied"], 1)
                        nc.scalar.activation(tile_f[:, FC:], stage_f[:, FC:], ACT.Copy)

                @block.vector
                def _(dve):
                    c = Counts(sems)
                    if second:
                        dve.tensor_copy(xS[:, :], xF).then_inc(sems["normed"], 1)
                        dve.tensor_copy(hS[:, :], hF[:, :])
                        link(c, dve.tensor_copy(rowS[:, :], rowF[:, :]))
                    if first:
                        dve.tensor_scalar(mask1[:, 0, :], stage_i[:, IM1:IM1 + P], 0.0, None, ALU.not_equal)
                        dve.tensor_scalar(mask1[:, 1, :], stage_i[:, IM1:IM1 + P], 0.0, -10000.0, ALU.is_equal, ALU.mult)
                        link(c, dve.tensor_scalar(rowF[:, :], stage_i[:, IM3:IM3 + 2], 0.0, 0.5, ALU.is_equal,
                                                  ALU.subtract))
                        dve.tensor_scalar(rowF[:, :], rowF[:, :], -2e9, None, ALU.mult)

        def phase(which, first, second, following=False, load_at=None, store_at=None, last=False, need_weights=()):
            parity = 0 if which == 2 else 1
            attn, moe = streams(which, first, second, following)
            sems = sets[parity]
            order = []

            def run(engine):
                gens = [half[engine](Counts(sems)) if half else None for half in (attn, moe)]
                if engine == 0:
                    order.extend(choose_order(*gens, PACE[which]))
                else:
                    side_by_side(*gens, order)

            with nc.Block() as block:
                @block.tensor
                def _(pe):
                    for g in need_weights:
                        pe.wait_ge(dma_w[g], 16)
                    run(0)

                @block.scalar
                def _(a):
                    run(1)

                @block.vector
                def _(dve):
                    run(2)

                @block.gpsimd
                def _(pool):
                    clear_resting(parity)
                    if which == 2 and second:
                        nc.gpsimd.sem_clear(range(out_free.num, out_free.num + 1))
                    run(3)

                @block.sync
                def _(sp):
                    if which == 1 and second:
                        sp.wait_ge(out_free, 16)
                    if load_at is not None:
                        sp.dma_start(stage_f[:, :], fin[:, bass.ds(load_at * FCOLS, FCOLS)]).then_inc(sems["tile_in"], 16)
                        sp.dma_start(stage_i[:, :], iin[:, bass.ds(load_at * ICOLS, ICOLS)]).then_inc(sems["tile_in"], 16)
                        sp.wait_ge(sems["tile_in"], 32)
                    if moe:
                        moe[4](Counts(sems))
                    if store_at is not None:
                        sp.wait_ge(sems["m_out"], 1)
                        sp.dma_start(out[:, bass.ds(store_at * T, T)], outS[:, :]).then_inc(out_free, 16)
                        if last:
                            sp.wait_ge(out_free, 16)

        def setup():
            with nc.Block() as block:
                @block.sync
                def _(sp):
                    sp.dma_start(vsb[:, :], vecs).then_inc(dma_vec, 16)
                    sp.dma_start(wsb["early"][:, :], weights["early"]).then_inc(dma_w["early"], 16)
                    sp.dma_start(csb[:, :], consts).then_inc(dma_const, 16)
                    sp.dma_start(stage_f[:, :], fin[:, 0:FCOLS]).then_inc(dma_first, 16)
                    sp.dma_start(stage_i[:, :], iin[:, 0:ICOLS]).then_inc(dma_first, 16)
                    sp.dma_start(wsb["ff0"], weights["ff0"]).then_inc(dma_w["ff0"], 16)
                    for g, _ in W_PARTS[2:]:
                        sp.dma_start(wsb[g][:, :], weights[g]).then_inc(dma_w[g], 16)
                    sp.wait_ge(dma_const, 16)
                    sp.wait_ge(dma_first, 32)

                @block.scalar
                def _(a):
                    a.wait_ge(dma_vec, 16)
                    a.activation(tg[:, :], V("gx", 0, 8), ACT.Tanh).then_inc(setup_tanh, 1)
                    a.wait_ge(setup_pe, 2)
                    a.activation(a12, SA[:, 0:P], ACT.Copy).then_inc(setup_act, 1)
                    a.wait_ge(setup_pe, 3)
                    a.activation(ff0[:, :], SB[:, 0:P], ACT.Copy)

                @block.tensor
                def _(pe):
                    pe.wait_ge(dma_vec, 16)
                    pe.wait_ge(dma_w["early"], 16)
                    pe.wait_ge(dma_w["ff0"], 16)
                    for l, (w, b) in enumerate((("o0", "bv0"), ("o1", "bv1"), ("oa", "bva"))):
                        mm = pe.matmul(OY[:, l:l + 1], Wt(w), V(b), start=True, stop=True)
                    mm.then_inc(setup_pe, 1)
                    pe.matmul(SA[:, 0:P], Wt("a1T"), Wt("a2"), start=True, stop=True).then_inc(setup_pe, 1)
                    pe.wait_ge(setup_act, 1)
                    pe.matmul(SB[:, 0:P], Wt("wT"), a12, start=True, stop=True).then_inc(setup_pe, 1)

                @block.vector
                def _(dve):
                    dve.memset(vdiag[:, :, :], 0.0)
                    dve.memset(negones[:, :], -1.0)
                    dve.memset(outS[:, :], 0.0).then_inc(out_free, 16)
                    dve.memset(vblk[:, :, :, 2 * DK:], 0.0).then_inc(setup_dve, 1)
                    dve.wait_ge(setup_dve, 1)
                    for h2 in range(2):
                        dve.memset(vblk[h2 * SEQ:(h2 + 1) * SEQ, :, :, 2 * DK + h2:2 * DK + h2 + 1], 1.0)
                    dve.memset(neghalf[:, :], -0.5)
                    dve.wait_ge(dma_vec, 16)
                    dve.tensor_scalar(cent2[:, :], V("cent", 0, NE), 2.0, None, ALU.mult)
                    dve.scalar_tensor_tensor(out=centsq[:, :], in0=V("cent", 0, NE), scalar=-float(P),
                                             in1=V("cent", 0, NE),
                                             op0=ALU.mult, op1=ALU.mult)
                    dve.tensor_scalar(b2x2[:, :], V("b2", 0, P)[0:NE, :], 2.0, None, ALU.mult)
                    dve.wait_ge(setup_pe, 1)
                    for l, b in enumerate(("bo0", "bo1", "boa")):
                        last = dve.tensor_tensor(bo[:, l:l + 1], OY[:, l:l + 1], V(b), ALU.add)
                    last.then_inc(setup_dve, 1)
                    dve.wait_ge(setup_dve, 2)
                    dve.wait_ge(setup_tanh, 1)
                    dve.tensor_tensor(bog[:, 0:2], bo[:, 0:2], tg[:, 0:2], ALU.mult)

        def setup_late():
            with nc.Block() as block:
                @block.gpsimd
                def _(pool):
                    clear_resting(1)

                @block.tensor
                def _(pe):
                    pe.wait_ge(dma_w["late"], 16)
                    pe.matmul(OY[:, 3:4], Wt("o3"), V("bv3"), start=True, stop=True).then_inc(late_pe, 1)

                @block.vector
                def _(dve):
                    dve.wait_ge(late_pe, 1)
                    dve.tensor_tensor(bo[:, 3:4], OY[:, 3:4], V("bo3"), ALU.add).then_inc(late_dve, 1)
                    dve.wait_ge(late_dve, 1)
                    dve.tensor_tensor(bog[:, 3:4], bo[:, 3:4], tg[:, 3:4], ALU.mult)

        setup()
        phase(2, False, False, following=True)
        setup_late()
        handoff(0, True, False)
        phase(1, True, False, load_at=1)
        phase(2, True, False, following=True, need_weights=("moe1",))
        phase(3, True, False, need_weights=("mid",))
        with nc.Fori(1, NT) as i:
            handoff(0, True, True)
            phase(1, True, True, load_at=i + 1, need_weights=("moe2",))
            phase(2, True, True, following=True, need_weights=("late",))
            phase(3, True, True, store_at=i - 1, need_weights=("moe3",))
        handoff(0, False, True)
        phase(1, False, True)
        phase(2, False, True)
        phase(3, False, True, store_at=NT - 1, last=True)


def _constants():
    p = np.arange(P)
    ident = np.eye(P, dtype=np.float32)
    d = p % DK
    inv = 1.0 / 10000.0 ** (np.arange(0, DK, 2, dtype=np.float32) / DK)
    ang = np.einsum("i,j->ij", np.arange(SEQ, dtype=np.float32), inv)[:, d % 4].T.astype(np.float32)
    cos, sin = np.cos(ang), np.sin(ang) * np.where(d < 4, -1.0, 1.0)[:, None]
    q, k = p % SEQ, np.arange(SEQ)
    parts = {
        "ident": ident, "center": ident - 1.0 / P, "mean": np.full((P, P), 1.0 / P),
        "cos": cos, "sin": sin,
        "causal": np.where(k[None, :] > q[:, None], -3e38, 3e38),
        "headsel": np.where((p % 32 // DK)[:, None] == np.arange(4)[None, :], DK ** -0.5, 0.0),
        "halves": np.where((p // SEQ)[:, None] == (np.arange(2 * DK) // DK)[None, :], 1.0, 0.0),
        "iota8": np.tile(np.arange(NE), (P, 1)),
    }
    return np.concatenate([parts[n].astype(np.float32) for n, _ in CONST_PARTS], axis=1)


def _rows(a):
    return a if a.shape[0] == P else np.concatenate([a, np.zeros((P - a.shape[0], *a.shape[1:]), a.dtype)])


def kernel(**inputs):
    import concourse.bacc as bacc
    from concourse.bass_utils import run_bass_kernel_spmd

    x = {k: np.asarray(v) for k, v in inputs.items()}
    col = lambda n: x[n].reshape(P, 1)
    across = lambda a: np.broadcast_to(a[None, :], (P, a.shape[0]))
    swap = lambda w: w.reshape(P, 16, 2, 4)[:, :, ::-1, :].reshape(P, P)
    experts = lambda w: w.transpose(1, 0, 2).reshape(P, -1)
    down = lambda w: w.reshape(NE, -1, P, P).transpose(2, 0, 1, 3).reshape(P, -1)
    pairs = lambda g, u: np.stack([g.reshape(NE, P, -1, P), u.reshape(NE, P, -1, P)], axis=3)\
        .transpose(1, 0, 2, 3, 4).reshape(P, -1)

    vec = {
        "gx": across(x["g_xattn"]), "gf": across(x["g_ffn"]),
        "bq0": col("L0_xattn_bq"), "bk0": col("L0_xattn_bk"), "bv0": col("L0_xattn_bv"),
        "bo0": col("L0_xattn_bo"), "bf0": col("L0_ffn_bias"),
        "bq1": col("L1_xattn_bq"), "bk1": col("L1_xattn_bk"), "bv1": col("L1_xattn_bv"), "bo1": col("L1_xattn_bo"),
        "ln1w": col("L1_ffn_ln1_w"), "ln1b": col("L1_ffn_ln1_b"),
        "ln2w": col("L1_ffn_ln2_w"), "ln2b": col("L1_ffn_ln2_b"),
        "bqa": x["L1_ffn_b_qkv"][0:P].reshape(P, 1), "bka": x["L1_ffn_b_qkv"][P:2 * P].reshape(P, 1),
        "bva": x["L1_ffn_b_qkv"][2 * P:].reshape(P, 1), "boa": col("L1_ffn_b_o"),
        "b1": x["L1_ffn_b1"].reshape(NE * 4, P).T, "g1": col("L2_ffn_g1"), "g2": col("L2_ffn_g2"),
        "lng": col("L2_xattn_ln_g"), "lnb": col("L2_xattn_ln_b"),
        "clng": col("L2_xattn_cln_g"), "clnb": col("L2_xattn_cln_b"),
        "bq3": col("L3_xattn_bq"), "bk3": col("L3_xattn_bk"), "bv3": col("L3_xattn_bv"),
        "bo3": col("L3_xattn_bo"), "scale3": col("L3_ffn_scale"), "cent": x["L3_ffn_centroids"].T,
        "gate1": x["L1_ffn_w_gate"], "router2": x["L2_ffn_w_router"], "b2": _rows(x["L1_ffn_b2"]),
    }
    qkv, kv, up3 = x["L1_ffn_w_qkv"], x["L2_xattn_Wkv"], x["L3_ffn_up_w"]
    mats = {
        "q0": x["L0_xattn_Wq"], "k0": x["L0_xattn_Wk"], "v0": x["L0_xattn_Wv"], "o0": x["L0_xattn_Wo"],
        "wT": x["L0_ffn_weight"].T, "a1T": x["L0_ffn_aux_weight1"].T, "a2": x["L0_ffn_aux_weight2"],
        "q1": x["L1_xattn_Wq"], "k1": x["L1_xattn_Wk"], "v1": x["L1_xattn_Wv"], "o1": x["L1_xattn_Wo"],
        "qa": qkv[:, 0:P], "ka": qkv[:, P:2 * P], "va": qkv[:, 2 * P:], "oa": x["L1_ffn_w_o"],
        "up1": experts(x["L1_ffn_w1"]), "dn1": down(x["L1_ffn_w2"]),
        "qx": x["L2_xattn_Wq"], "kx": np.concatenate([kv[:, 0:64], kv[:, 0:64]], axis=1), "vx": kv[:, 64:],
        "ox": x["L2_xattn_Wout"].reshape(2, 2, 2, 2, 64, P).transpose(1, 4, 3, 0, 2, 5).reshape(P, 8 * P),
        "ffx": x["L2_xattn_W1"].reshape(P, 2, 4, P).transpose(0, 2, 1, 3).reshape(P, 8 * P),
        "ff2x": x["L2_xattn_W2"].reshape(4, P, P).transpose(1, 0, 2).reshape(P, 4 * P),
        "q2": x["L2_ffn_wq"], "qr2": swap(x["L2_ffn_wq"]), "k2": x["L2_ffn_wk"], "kr2": swap(x["L2_ffn_wk"]),
        "v2": x["L2_ffn_wv"], "o2": x["L2_ffn_wo"],
        "up2": pairs(x["L2_ffn_wg"], x["L2_ffn_wu"]), "dn2": down(x["L2_ffn_wd"]),
        "q3": x["L3_xattn_Wq"].T, "k3": x["L3_xattn_Wk"].T, "v3": x["L3_xattn_Wv"].T, "o3": x["L3_xattn_Wo"].T,
        "up3": pairs(up3[:, :, 2 * P:], up3[:, :, 0:2 * P]), "dn3": down(x["L3_ffn_down_w"]),
    }
    tiles = lambda a: a.reshape(P, NT, -1)
    twice = lambda m: np.concatenate([m, m]).reshape(P, NT, -1)
    floats = np.concatenate([tiles(x["x"].reshape(-1, P).T), tiles(x["ctx_1024"].reshape(-1, P).T),
                             twice(x["mask_BxSxS2_ff0"].transpose(1, 0, 2))], axis=2)
    pairs_of = lambda m: m.reshape(NT, 2, 2, SEQ, -1).transpose(2, 3, 0, 1, 4).reshape(P, NT, -1)
    keys = x["mask_BxS2_ik0"]
    ints = np.concatenate([pairs_of(x["mask_Bx1xSxS2_ik1"]), pairs_of(np.repeat(keys[:, None, :], SEQ, axis=1)),
                           pairs_of(keys)], axis=2)
    floats = np.concatenate([floats, floats[:, 0:1]], axis=1).reshape(P, -1)
    ints = np.concatenate([ints, ints[:, 0:1]], axis=1).reshape(P, -1)

    arrays = {"fin": floats, "iin": ints, "consts": _constants(),
              "vecs": np.concatenate([vec[n] for n, _ in VEC_PARTS], axis=1)}
    for g, parts in W_PARTS:
        arrays[f"w_{g}"] = np.concatenate([mats[n] for n, _ in parts], axis=1)
    arrays = {f"in_{k}": np.ascontiguousarray(v) for k, v in arrays.items()}
    nc = bacc.Bacc("TRN2", target_bir_lowering=False, num_devices=1)
    aps = {k[3:]: nc.dram_tensor(k, v.shape, mybir.dt.from_np(v.dtype), kind="ExternalInput").ap()
           for k, v in arrays.items()}
    out = nc.dram_tensor("out_0", (P, NSEQ * SEQ), F32, kind="ExternalOutput").ap()
    build(nc, aps["fin"], aps["iin"], aps["consts"], aps["vecs"], {g: aps[f"w_{g}"] for g, _ in W_PARTS}, out)
    r = run_bass_kernel_spmd(nc, [arrays], core_ids=[0])
    y = r.results[0]["out_0"]
    return np.ascontiguousarray(y.T).reshape(NSEQ, SEQ, P)
```
